# Optimizing a Trainium2 kernel written in Bass

```python
import numpy as np
import jax
import jax.numpy as jnp

def _softmax(x, axis=-1):
    return jax.nn.softmax(x, axis=axis)

def _gelu(x):
    return jax.nn.gelu(x, approximate=True)

def _silu(x):
    return jax.nn.silu(x)

def _sigmoid(x):
    return jax.nn.sigmoid(x)

def _layernorm(x, axis=-1, eps=1e-05):
    m = jnp.mean(x, axis=axis, keepdims=True)
    v = jnp.var(x, axis=axis, keepdims=True)
    return (x - m) / jnp.sqrt(v + eps)

def _scatter_add(tgt, idx, src, axis=0):
    return tgt.at[idx].add(src)

def _segment_sum(src, seg, n):
    return jax.ops.segment_sum(src, seg, n)
kernel_name = 'mk_macaron_d1_jaxref_r4_68d7b1'

def setup_inputs(seed: int=0):
    np.random.seed(seed)
    _w = jnp.asarray

    def _L0_attn_setup():
        import jax, jax.numpy as jnp
        import numpy as np
        import math
        D_MODEL, D_C, D_R, NH = (256, 128, 32, 16)
        HD = D_MODEL // NH
        B, T = (2, 512)

        def _rope_tables(T, d_R):
            inv_freq = 1.0 / 10000.0 ** (jnp.arange(0, d_R, 2, dtype=jnp.float32) / d_R)
            t = jnp.arange(T, dtype=jnp.float32)
            freqs = jnp.outer(t, inv_freq)
            return (jnp.cos(freqs), jnp.sin(freqs))

        def _rotary_apply(x, cos, sin):
            d = x.shape[-1]
            x1, x2 = (x[..., :d // 2], x[..., d // 2:])
            return jnp.concatenate([x1 * cos - x2 * sin, x2 * cos + x1 * sin], axis=-1)
        key = jax.random.key(seed)
        ks = jax.random.split(key, 8)
        s = lambda fan_in: 1.0 / math.sqrt(fan_in)
        return {'x': jax.random.normal(ks[0], (B, T, D_MODEL), jnp.float32), 'W_kv_down': jax.random.normal(ks[1], (D_MODEL, D_C), jnp.float32) * s(D_MODEL), 'W_k_up': jax.random.normal(ks[2], (D_C, D_MODEL), jnp.float32) * s(D_C), 'W_v_up': jax.random.normal(ks[3], (D_C, D_MODEL), jnp.float32) * s(D_C), 'W_q': jax.random.normal(ks[4], (D_MODEL, D_MODEL), jnp.float32) * s(D_MODEL), 'W_q_rope': jax.random.normal(ks[5], (D_MODEL, D_R), jnp.float32) * s(D_MODEL), 'W_k_rope': jax.random.normal(ks[6], (D_C, D_R), jnp.float32) * s(D_C), 'W_o': jax.random.normal(ks[7], (D_MODEL, D_MODEL), jnp.float32) * s(D_MODEL)}
    _L0_attn_in = _L0_attn_setup()

    def _L0_ffn_setup():
        import jax, jax.numpy as jnp
        import numpy as np
        B, S, D, E = (4, 1024, 256, 8)
        key = jax.random.key(seed)
        k1, k2, k3, k4, k5 = jax.random.split(key, 5)
        scale = 1.0 / np.sqrt(D)
        return {'x': jax.random.normal(k1, (B, S, D), dtype=jnp.float32), 'Wg': jax.random.normal(k2, (D, D), dtype=jnp.float32) * scale, 'bg': jnp.zeros((D,), dtype=jnp.float32), 'We': jax.random.normal(k3, (E, D, D), dtype=jnp.float32) * scale, 'be': jnp.zeros((E, D), dtype=jnp.float32)}
    _L0_ffn_in = _L0_ffn_setup()
    _d = {'L0_attn_x': _L0_attn_in['x'], 'L0_attn_W_kv_down': _L0_attn_in['W_kv_down'], 'L0_attn_W_k_up': _L0_attn_in['W_k_up'], 'L0_attn_W_v_up': _L0_attn_in['W_v_up'], 'L0_attn_W_q': _L0_attn_in['W_q'], 'L0_attn_W_q_rope': _L0_attn_in['W_q_rope'], 'L0_attn_W_k_rope': _L0_attn_in['W_k_rope'], 'L0_attn_W_o': _L0_attn_in['W_o'], 'L0_ffn_Wg': _L0_ffn_in['Wg'], 'L0_ffn_bg': _L0_ffn_in['bg'], 'L0_ffn_We': _L0_ffn_in['We'], 'L0_ffn_be': _L0_ffn_in['be']}
    _x0 = _d['L0_attn_x']
    _d['L0_attn_x'] = jax.random.normal(jax.random.fold_in(jax.random.key(seed), 1), (16, 512, 256), dtype=_x0.dtype)
    del _x0
    return _d

def reference(L0_attn_x, L0_attn_W_kv_down, L0_attn_W_k_up, L0_attn_W_v_up, L0_attn_W_q, L0_attn_W_q_rope, L0_attn_W_k_rope, L0_attn_W_o, L0_ffn_Wg, L0_ffn_bg, L0_ffn_We, L0_ffn_be):

    def _L0_attn_ref(x, W_kv_down, W_k_up, W_v_up, W_q, W_q_rope, W_k_rope, W_o):
        import jax, jax.numpy as jnp
        import numpy as np
        import math
        D_MODEL, D_C, D_R, NH = (256, 128, 32, 16)
        HD = D_MODEL // NH
        B, T = (2, 512)

        def _rope_tables(T, d_R):
            inv_freq = 1.0 / 10000.0 ** (jnp.arange(0, d_R, 2, dtype=jnp.float32) / d_R)
            t = jnp.arange(T, dtype=jnp.float32)
            freqs = jnp.outer(t, inv_freq)
            return (jnp.cos(freqs), jnp.sin(freqs))

        def _rotary_apply(x, cos, sin):
            d = x.shape[-1]
            x1, x2 = (x[..., :d // 2], x[..., d // 2:])
            return jnp.concatenate([x1 * cos - x2 * sin, x2 * cos + x1 * sin], axis=-1)
        Bb, Tt, _ = x.shape
        cos, sin = _rope_tables(Tt, D_R)
        cos = cos[None]
        sin = sin[None]
        c_kv = x @ W_kv_down
        k_rope = _rotary_apply(c_kv @ W_k_rope, cos, sin)
        k = (c_kv @ W_k_up).reshape(Bb, Tt, NH, HD)
        v = (c_kv @ W_v_up).reshape(Bb, Tt, NH, HD)
        q = (x @ W_q).reshape(Bb, Tt, NH, HD)
        q_rope = _rotary_apply(x @ W_q_rope, cos, sin)
        scale = math.sqrt(HD + D_R)
        scores = jnp.einsum('bqhd,bkhd->bhqk', q, k)
        scores = scores + jnp.einsum('bqr,bkr->bqk', q_rope, k_rope)[:, None]
        scores = scores / scale
        causal = jnp.triu(jnp.ones((Tt, Tt), dtype=bool), k=1)
        scores = jnp.where(causal[None, None], -jnp.inf, scores)
        w = jax.nn.softmax(scores, axis=-1)
        attn = jnp.einsum('bhqk,bkhd->bqhd', w, v).reshape(Bb, Tt, D_MODEL)
        return attn @ W_o

    def _L0_ffn_ref(x, Wg, bg, We, be):
        import jax, jax.numpy as jnp
        import numpy as np
        B, S, D, E = (4, 1024, 256, 8)
        probs = jax.nn.softmax(x @ Wg + bg, axis=-1)
        idx = jnp.argmax(probs, axis=-1)
        p = jnp.take_along_axis(probs, idx[..., None], axis=-1)[..., 0]
        e_idx = idx % We.shape[0]
        h = jax.nn.relu(jnp.einsum('bsd,edf->besf', x, We) + be[None, :, None, :])
        onehot = jax.nn.one_hot(e_idx, We.shape[0], dtype=x.dtype)
        out = jnp.einsum('besf,bse->bsf', h, onehot) * p[..., None]
        return out
    x = L0_attn_x
    x = x + 0.5 * _L0_ffn_ref(_layernorm(x, axis=-1), L0_ffn_Wg, L0_ffn_bg, L0_ffn_We, L0_ffn_be)
    x = x + _L0_attn_ref(_layernorm(x, axis=-1), L0_attn_W_kv_down, L0_attn_W_k_up, L0_attn_W_v_up, L0_attn_W_q, L0_attn_W_q_rope, L0_attn_W_k_rope, L0_attn_W_o)
    x = x + 0.5 * _L0_ffn_ref(_layernorm(x, axis=-1), L0_ffn_Wg, L0_ffn_bg, L0_ffn_We, L0_ffn_be)
    return x

_drawn_inputs = setup_inputs


def setup_inputs(seed=0):
    import zlib

    import numpy as np

    out = dict(_drawn_inputs(seed))
    spreads = {'L0_ffn_bg': (0.0, 0.8), 'L0_ffn_be': (0.0, 0.8)}
    factors = {}
    for name, (base, spread) in spreads.items():
        noise = np.random.default_rng([zlib.crc32(name.encode()), seed]).standard_normal(out[name].shape)
        drawn = base * np.exp(spread * noise) if base else spread * noise
        out[name] = jnp.asarray(drawn.astype(out[name].dtype))
    for name, factor in factors.items():
        out[name] = (out[name] * factor).astype(out[name].dtype)
    return out
```

```python
from contextlib import ExitStack

import concourse.bass as bass
from concourse import mybir
from concourse.alu_op_type import AluOpType as ALU

F32 = mybir.dt.float32
F16 = mybir.dt.float16
BF16 = mybir.dt.bfloat16
I32 = mybir.dt.int32
U32 = mybir.dt.uint32
ACT = mybir.ActivationFunctionType
AX_X = mybir.AxisListType.X

P = 128
D = 256
DC = D // P
C = 128
R = 32
NH = 16
HD = D // NH
T = 512
TT = T // P
E = 8
EPS = 1e-5
GT = 4
RING = 4
ROW = D + 4
MASKED = -1e30
GH = 4
NG = NH // GH
KC = 96
ROW_MAX = R + HD
SCALE = float(HD + R) ** -0.5


def ffn_phase(nc, name, psum, const, x_in, x_out, routed, Wg, bg, We, be):
    tokens = x_in.shape[0]
    groups = tokens // (GT * P)
    xv = x_in.rearrange("(g t p) d -> g p t d", p=P, t=GT)
    region = (routed.shape[0] - P) // E
    spare = E * region
    sorted_tiles = -(-(tokens // P + E - 1) // RING) * RING
    ctx = ExitStack()
    with ctx:
        def sb(n, shape, dt=F32):
            return ctx.enter_context(nc.sbuf_tensor(f"{name}_{n}", shape, dt))

        def sem(n, count=0):
            if count:
                return [ctx.enter_context(nc.semaphore(f"{name}_{n}{k}")) for k in range(count)]
            return ctx.enter_context(nc.semaphore(f"{name}_{n}"))

        wg = sb("wg", [P, DC, D])
        we = sb("we", [P, DC, E * D])
        beb = sb("beb", [P, E * D])
        bg_row = sb("bg_row", [1, D])
        bg_rest = sb("bg_rest", [1, 2, D])
        bg3 = sb("bg3", [1, 3, D], BF16)
        bg_rows = sb("bg_rows", [3, D], BF16)
        ones = sb("ones", [P, P], BF16)
        before = sb("before", [P, P], BF16)
        power = sb("power", [P, GT])
        ids = sb("ids", [P, E])
        zeros = sb("zeros", [P, ROW])

        rows = sb("rows", [P, 2, GT, ROW])
        stats = sb("stats", [P, GT, 6])
        mv = sb("mv", [P, GT, 2])
        veps = sb("veps", [P, GT])
        xn = sb("xn", [P, 2, GT, D])
        xT = sb("xT", [P, DC, GT * P])
        top = sb("top", [P, GT, 8])
        top_at = sb("top_at", [P, GT, 8], U32)
        ntop = sb("ntop", [P, GT])
        expert_i = sb("expert_i", [P, GT], U32)
        expert = sb("expert", [P, GT])
        onehot = sb("onehot", [P, GT, E], BF16)
        junk = sb("junk", [P, GT, D])
        esum = sb("esum", [P, GT])
        prob = sb("prob", [P, GT])
        token = sb("token", [P, GT])
        base = sb("base", [P, 2, E])
        rank = sb("rank", [P, GT, E])
        chosen = sb("chosen", [P, GT, E])
        row_f = sb("row_f", [P, GT])
        row_i = sb("row_i", [P, 2, GT], U32)

        N = sorted_tiles
        start_f = sb("start_f", [P, E])
        start_i = sb("start_i", [P, E], I32)
        count = sb("count", [P, E])
        tiles_i = sb("tiles_i", [P, E], I32)
        tiles_f = sb("tiles_f", [P, E])
        ends = sb("ends", [P, E])
        one8 = sb("one8", [P, E])
        tile_no = sb("tile_no", [P, N])
        past = sb("past", [P, N, E])
        past_tiles = sb("past_tiles", [P, N, E])
        owner = sb("owner", [P, N])
        first_tile = sb("first_tile", [P, N])
        local = sb("local", [P, N])
        is_owner = sb("is_owner", [P, N, E])
        owned = sb("owned", [P, N, E])
        owner_count = sb("owner_count", [P, N])
        at_f = sb("at_f", [P, N])
        at_i = sb("at_i", [P, N], I32)
        column_f = sb("column_f", [P, N])
        column_i = sb("column_i", [P, N], I32)
        lane = sb("lane", [P, 1])
        lane_no = sb("lane_no", [P, N])
        skip = sb("skip", [P, N])

        srow = sb("srow", [P, RING, ROW])
        sxn = sb("sxn", [P, 2, D])
        sxT = sb("sxT", [P, 2, DC, P])
        pre = sb("pre", [P, 2, D])
        act_out = sb("act_out", [P, 2, D])
        y = sb("y", [P, RING, D])
        to_f = sb("to_f", [P, RING])
        to_i = sb("to_i", [P, RING], U32)

        xT_ps = psum[0:2]
        gate_ps = psum[2:4]
        rank_ps = psum[4]

        w_loaded = sem("w_loaded")
        made = sem("made")
        masks_made = sem("masks_made")
        bg_step = sem("bg_step")
        bg_ready = sem("bg_ready")
        bg_placed = sem("bg_placed")
        x_loaded = sem("x_loaded", 2)
        ln_stats = sem("ln_stats")
        ln_aggr = sem("ln_aggr")
        ln_eps = sem("ln_eps")
        ln_rstd = sem("ln_rstd")
        xn_ready = sem("xn_ready")
        xT_ps_ready = sem("xT_ps_ready")
        xT_ready = sem("xT_ready")
        gate_ready = sem("gate_ready")
        top_step = sem("top_step")
        top_ready = sem("top_ready")
        gate_read = sem("gate_read")
        exp_done = sem("exp_done")
        route_step = sem("route_step")
        onehot_ready = sem("onehot_ready")
        rank_ready = sem("rank_ready")
        rows_ready = sem("rows_ready")
        scattered = sem("scattered", 2)
        padded = sem("padded")
        plan_step = sem("plan_step")
        plan_ready = sem("plan_ready")
        srow_loaded = sem("srow_loaded", RING)
        sxn_ready = sem("sxn_ready")
        sxT_ps_ready = sem("sxT_ps_ready")
        sxT_ready = sem("sxT_ready")
        product_ready = sem("product_ready")
        pre_ready = sem("pre_ready")
        act_ready = sem("act_ready")
        to_step = sem("to_step")
        y_ready = sem("y_ready")
        y_stored = sem("y_stored", RING)
        ROUTE_STEPS = 8

        with nc.Block() as block:
            @block.sync
            def _(sp):
                for k in range(2):
                    sp.dma_start(rows[:, k, :, 0:D], xv[k]).then_inc(x_loaded[k], 16)
                sp.dma_start(wg[:], Wg.rearrange("(c p) f -> p c f", p=P)).then_inc(w_loaded, 16)
                sp.dma_start(bg_row[:], bg.rearrange("(o f) -> o f", o=1)).then_inc(w_loaded, 16)
                for c in range(DC):
                    sp.dma_start(we[:, c, :].rearrange("p (e f) -> p e f", e=E),
                                 We[:, c * P:(c + 1) * P, :].rearrange("e p f -> p e f")).then_inc(w_loaded, 16)
                sp.dma_start(beb[:], be.rearrange("e f -> (e f)").partition_broadcast(P)).then_inc(w_loaded, 16)
                sp.wait_ge(bg_ready, 1)
                for part in range(3):
                    sp.dma_start(bg_rows[part:part + 1, :], bg3[:, part, :]).then_inc(bg_placed, 16)
                sp.wait_ge(made, 1)
                sp.dma_start(routed[spare:spare + P, :], zeros[:]).then_inc(padded, 16)
                with sp.Fori(1, groups // 2) as i:
                    for k in range(2):
                        sp.wait_ge(scattered[k], 16 * GT * i)
                        sp.nop(nofuse=True)
                        sp.dma_start(rows[:, k, :, 0:D], xv[2 * i + k]).then_inc(x_loaded[k], 16)
                sp.wait_ge(plan_ready, 1)
                for e in range(E):
                    at = sp.value_load(start_i[0:1, e:e + 1], min_val=0, max_val=spare - P)
                    sp.dma_start(routed[bass.ds(at, P), :], zeros[:]).then_inc(padded, 16)
                sp.wait_ge(padded, 16 * (E + 1))
                for k in range(2):
                    sp.wait_ge(scattered[k], 16 * GT * (groups // 2))

                def load(j, k):
                    at = sp.value_load(at_i[0:1, bass.ds(j, 1)],
                                       min_val=0, max_val=spare)
                    sp.dma_start(srow[:, k, :], routed[bass.ds(at, P), :]).then_inc(srow_loaded[k], 16)

                sp.wait_ge(plan_ready, 2)
                for k in range(RING):
                    load(k, k)
                with sp.Fori(1, N // RING) as i:
                    for k in range(RING):
                        sp.wait_ge(y_ready, RING * (i - 1) + k + 1)
                        sp.nop(nofuse=True)
                        load(RING * i + k, k)

            @block.gpsimd
            def _(pool):
                nc.gpsimd.memset(zeros[:], 0.0)
                nc.gpsimd.memset(power[:], -0.5)
                nc.gpsimd.memset(ones[:], 1.0)
                nc.gpsimd.memset(one8[:], 1.0)
                nc.gpsimd.memset(before[:], 1.0)
                nc.gpsimd.iota(ids[:], [[1, E]], base=0, channel_multiplier=0, allow_small_or_imprecise_dtypes=True)
                nc.gpsimd.iota(tile_no[:], [[1, N]], base=0, channel_multiplier=0, allow_small_or_imprecise_dtypes=True)
                nc.gpsimd.iota(lane[:], [[0, 1]], base=0, channel_multiplier=1, allow_small_or_imprecise_dtypes=True)
                nc.gpsimd.iota(token[:], [[P, GT]], base=0, channel_multiplier=1, allow_small_or_imprecise_dtypes=True)
                nc.gpsimd.iota(base[:, 0, :], [[region, E]], base=0, channel_multiplier=0,
                               allow_small_or_imprecise_dtypes=True)
                nc.gpsimd.iota(start_f[:], [[region, E]], base=0, channel_multiplier=0,
                               allow_small_or_imprecise_dtypes=True).then_inc(made, 1)
                pool.wait_ge(made, 1)
                nc.gpsimd.affine_select(out=before[:], in_=before[:], compare_op=ALU.is_gt, fill=0.0,
                                        base=0, pattern=[[1, P]], channel_multiplier=-1).then_inc(masks_made, 1)

                def gate(i, k, first):
                    n = 2 * i + k
                    pool.wait_ge(ln_aggr, n + 1)
                    pool.nop(nofuse=True)
                    nc.gpsimd.tensor_scalar(veps[:], mv[:, :, 1], EPS, None, ALU.add).then_inc(ln_eps, 1)
                    pool.wait_ge(ln_eps, n + 1)
                    nc.gpsimd.tensor_tensor(rows[:, k, :, D], veps[:], power[:], ALU.pow).then_inc(ln_rstd, 1)

                def scatter(i, k):
                    pool.wait_ge(rows_ready, 2 * i + k + 1)
                    pool.nop(nofuse=True)
                    for t in range(GT):
                        nc.gpsimd.indirect_dma_start(
                            out=routed, out_offset=bass.IndirectOffsetOnAxis(ap=row_i[:, k, t:t + 1], axis=0),
                            in_=rows[:, k, t, :], in_offset=None).then_inc(scattered[k], 16)

                gate(0, 0, True)
                gate(0, 1, True)
                scatter(0, 0)
                with pool.Fori(1, groups // 2) as i:
                    gate(i, 0, False)
                    scatter(i - 1, 1)
                    gate(i, 1, False)
                    scatter(i, 0)
                scatter(groups // 2 - 1, 1)

                def combine(i, k):
                    j = RING * i + k
                    pool.wait_ge(y_ready, j + 1)
                    pool.nop(nofuse=True)
                    nc.gpsimd.indirect_dma_start(
                        out=x_out, out_offset=bass.IndirectOffsetOnAxis(ap=to_i[:, k:k + 1], axis=0),
                        in_=y[:, k, :], in_offset=None, bounds_check=tokens - 1,
                        oob_is_err=False).then_inc(y_stored[k], 16)

                with pool.Fori(0, N // RING) as i:
                    for k in range(RING):
                        combine(i, k)
                for k in range(RING):
                    pool.wait_ge(y_stored[k], 16 * (N // RING))

            @block.scalar
            def _(act):
                act.preload_act_table(ACT.Exp)

                def gate(i, k, first):
                    n = 2 * i + k
                    for c in range(DC):
                        act.wait_ge(xT_ps_ready, DC * n + c + 1)
                        if c == 0 and not (first and k == 0):
                            act.wait_ge(gate_ready, 2 * n)
                        nc.scalar.activation(xT[:, c, :], xT_ps[c][:], ACT.Copy).then_inc(xT_ready, 1)
                    for h in range(2):
                        for t in range(2 * h, 2 * h + 2):
                            if t == 2 * h:
                                act.wait_ge(top_ready, 2 * n + h + 1)
                            if not (first and k == 0):
                                act.wait_ge(exp_done, GT * (n - 1) + t + 1)
                            nc.scalar.activation(junk[:, t, :], gate_ps[h][:, (t % 2) * D:(t % 2 + 1) * D], ACT.Exp,
                                                 bias=ntop[:, t:t + 1], accum_out=esum[:, t:t + 1]).then_inc(exp_done, 1)

                gate(0, 0, True)
                gate(0, 1, True)
                with act.Fori(1, groups // 2) as i:
                    gate(i, 0, False)
                    gate(i, 1, False)

                def expert_out(i, k, first):
                    j = RING * i + k
                    act.wait_ge(pre_ready, j + 1)
                    if not (first and k < 2):
                        act.wait_ge(y_ready, j - 1)
                    nc.scalar.activation(act_out[:, k % 2, :], pre[:, k % 2, :], ACT.Relu,
                                         scale=srow[:, k, D + 2:D + 3]).then_inc(act_ready, 1)

                def transposed(i, k, first):
                    j = RING * i + k
                    act.wait_ge(sxT_ps_ready, j + 1)
                    if not (first and k < 2):
                        act.wait_ge(product_ready, j - 1)
                    nc.scalar.activation(sxT[:, k % 2, :, :], psum[k % 2][:, 0:DC * P].rearrange("p (c t) -> p c t", c=DC),
                                         ACT.Copy).then_inc(sxT_ready, 1)

                transposed(0, 0, True)
                for k in range(1, RING):
                    transposed(0, k, True)
                    expert_out(0, k - 1, True)
                with act.Fori(1, N // RING) as i:
                    for k in range(RING):
                        transposed(i, k, False)
                        if k:
                            expert_out(i, k - 1, False)
                        else:
                            expert_out(i - 1, RING - 1, False)
                expert_out(N // RING - 1, RING - 1, False)

            @block.vector
            def _(dve):
                dve.wait_ge(w_loaded, 16 * (3 + DC))
                dve.wait_ge(masks_made, 1)
                nc.vector.tensor_copy(bg3[:, 0, :], bg_row[:]).then_inc(bg_step, 1)
                dve.wait_ge(bg_step, 1)
                nc.vector.tensor_tensor(bg_rest[:, 0, :], bg_row[:], bg3[:, 0, :], ALU.subtract).then_inc(bg_step, 1)
                dve.wait_ge(bg_step, 2)
                nc.vector.tensor_copy(bg3[:, 1, :], bg_rest[:, 0, :]).then_inc(bg_step, 1)
                dve.wait_ge(bg_step, 3)
                nc.vector.tensor_tensor(bg_rest[:, 1, :], bg_rest[:, 0, :], bg3[:, 1, :], ALU.subtract).then_inc(bg_step, 1)
                dve.wait_ge(bg_step, 4)
                nc.vector.tensor_copy(bg3[:, 2, :], bg_rest[:, 1, :]).then_inc(bg_ready, 1)

                def normalise(i, k, first):
                    n = 2 * i + k
                    dve.wait_ge(x_loaded[k], 16 * (i + 1))
                    if not (first and k == 0):
                        dve.wait_ge(xn_ready, n)
                    for t in range(GT):
                        last = nc.vector.bn_stats(stats[:, t, :], rows[:, k, t, 0:D])
                    last.then_inc(ln_stats, 1)
                    dve.wait_ge(ln_stats, n + 1)
                    dve.nop(nofuse=True)
                    for t in range(GT):
                        last = nc.vector.bn_aggr(mv[:, t, :], stats[:, t, :])
                    last.then_inc(ln_aggr, 1)
                    dve.wait_ge(ln_rstd, n + 1)
                    if not first:
                        dve.wait_ge(xT_ps_ready, DC * (n - 1))
                    for t in range(GT):
                        last = nc.vector.tensor_scalar(xn[:, k, t, :], rows[:, k, t, 0:D], mv[:, t, 0:1],
                                                       rows[:, k, t, D:D + 1], ALU.subtract, ALU.mult)
                    nc.vector.tensor_copy(rows[:, k, :, D + 1], mv[:, :, 0]).then_inc(xn_ready, 1)

                def tops(i, k, first):
                    n = 2 * i + k
                    for h in range(2):
                        dve.wait_ge(gate_ready, 2 * n + h + 1)
                        if h == 0 and not first:
                            dve.wait_ge(exp_done, GT * n)
                            dve.wait_ge(onehot_ready, n)
                        dve.nop(nofuse=True)
                        for t in range(2 * h, 2 * h + 2):
                            last = nc.vector.max(top[:, t, :], gate_ps[h][:, (t % 2) * D:(t % 2 + 1) * D])
                        last.then_inc(top_step, 1)
                        dve.wait_ge(top_step, 2 * n + h + 1)
                        dve.nop(nofuse=True)
                        nc.vector.tensor_scalar(ntop[:, 2 * h:2 * h + 2], top[:, 2 * h:2 * h + 2, 0], -1.0, None, ALU.mult)
                        for t in range(2 * h, 2 * h + 2):
                            last = nc.vector.max_index(top_at[:, t, :], top[:, t, :],
                                                       gate_ps[h][:, (t % 2) * D:(t % 2 + 1) * D])
                        last.then_inc(top_ready, 1)

                def route(i, k, first):
                    n = 2 * i + k
                    step = ROUTE_STEPS * n
                    dve.wait_ge(top_ready, 2 * n + 2)
                    nc.vector.tensor_scalar(expert_i[:], top_at[:, :, 0], E - 1, None, ALU.bitwise_and).then_inc(route_step, 1)
                    dve.wait_ge(route_step, step + 1)
                    nc.vector.tensor_copy(expert[:], expert_i[:]).then_inc(route_step, 1)
                    dve.wait_ge(route_step, step + 2)
                    if not (first and k == 0):
                        dve.wait_ge(rank_ready, n)
                    nc.vector.tensor_tensor(onehot[:], ids[:].unsqueeze(1).broadcast_to([P, GT, E]),
                                            expert[:].unsqueeze(2).broadcast_to([P, GT, E]), ALU.is_equal).then_inc(onehot_ready, 1)
                    dve.wait_ge(exp_done, GT * (n + 1))
                    nc.vector.reciprocal(prob[:], esum[:]).then_inc(route_step, 1)
                    dve.wait_ge(route_step, step + 3)
                    nc.vector.tensor_scalar(rows[:, k, :, D + 2], prob[:], 0.5, None, ALU.mult)
                    nc.vector.tensor_copy(rows[:, k, :, D + 3], token[:]).then_inc(route_step, 1)
                    dve.wait_ge(route_step, step + 4)
                    nc.vector.tensor_scalar(token[:], token[:], float(GT * P), None, ALU.add).then_inc(route_step, 1)
                    dve.wait_ge(rank_ready, n + 1)
                    nc.vector.tensor_tensor(rank[:], rank_ps[:, 0:GT * E].rearrange("p (t e) -> p t e", t=GT),
                                            base[:, k, :].unsqueeze(1).broadcast_to([P, GT, E]), ALU.add)
                    nc.vector.tensor_tensor(base[:, 1 - k, :], rank_ps[:, GT * E:GT * E + E], base[:, k, :],
                                            ALU.add).then_inc(route_step, 1)
                    dve.wait_ge(route_step, step + 6)
                    nc.vector.tensor_tensor(chosen[:], rank[:], onehot[:], ALU.mult).then_inc(route_step, 1)
                    dve.wait_ge(route_step, step + 7)
                    nc.vector.tensor_reduce(row_f[:], chosen[:], AX_X, ALU.add).then_inc(route_step, 1)
                    dve.wait_ge(route_step, step + 8)
                    if not first:
                        dve.wait_ge(scattered[k], 16 * GT * i)
                    nc.vector.tensor_copy(row_i[:, k, :], row_f[:]).then_inc(rows_ready, 1)

                normalise(0, 0, True)
                normalise(0, 1, True)
                tops(0, 0, True)
                route(0, 0, True)

                def pair(i, first):
                    normalise(i, 0, False)
                    tops(i - 1, 1, False)
                    route(i - 1, 1, first)
                    normalise(i, 1, False)
                    tops(i, 0, False)
                    route(i, 0, False)

                pair(1, True)
                with dve.Fori(2, groups // 2) as i:
                    pair(i, False)
                tops(groups // 2 - 1, 1, False)
                route(groups // 2 - 1, 1, False)

                nc.vector.tensor_tensor(count[:], base[:, 0, :], start_f[:], ALU.subtract).then_inc(plan_step, 1)
                nc.vector.tensor_copy(start_i[:], base[:, 0, :]).then_inc(plan_ready, 1)
                dve.wait_ge(plan_step, 1)
                nc.vector.tensor_scalar(tiles_f[:], count[:], float(P - 1), None, ALU.add).then_inc(plan_step, 1)
                dve.wait_ge(plan_step, 2)
                nc.vector.tensor_copy(tiles_i[:], tiles_f[:]).then_inc(plan_step, 1)
                dve.wait_ge(plan_step, 3)
                nc.vector.tensor_scalar(tiles_i[:], tiles_i[:], 7, None, ALU.arith_shift_right).then_inc(plan_step, 1)
                dve.wait_ge(plan_step, 4)
                nc.vector.tensor_copy(tiles_f[:], tiles_i[:]).then_inc(plan_step, 1)
                dve.wait_ge(plan_step, 5)
                nc.vector.tensor_tensor_scan(ends[:], one8[:], tiles_f[:], 0.0, ALU.mult, ALU.add).then_inc(plan_step, 1)
                dve.wait_ge(plan_step, 6)
                nc.vector.tensor_tensor(past[:], tile_no[:].unsqueeze(2).broadcast_to([P, N, E]),
                                        ends[:].unsqueeze(1).broadcast_to([P, N, E]), ALU.is_ge).then_inc(plan_step, 1)
                dve.wait_ge(plan_step, 7)
                nc.vector.tensor_reduce(owner[:], past[:], AX_X, ALU.add)
                nc.vector.tensor_tensor(past_tiles[:], past[:], tiles_f[:].unsqueeze(1).broadcast_to([P, N, E]),
                                        ALU.mult).then_inc(plan_step, 1)
                dve.wait_ge(plan_step, 8)
                nc.vector.tensor_reduce(first_tile[:], past_tiles[:], AX_X, ALU.add)
                nc.vector.tensor_tensor(is_owner[:], ids[:].unsqueeze(1).broadcast_to([P, N, E]),
                                        owner[:].unsqueeze(2).broadcast_to([P, N, E]), ALU.is_equal)
                nc.vector.tensor_scalar(column_f[:], owner[:], float(E - 1), float(D), ALU.min, ALU.mult)
                nc.vector.tensor_scalar(at_f[:], owner[:], float(region), None, ALU.mult).then_inc(plan_step, 1)
                dve.wait_ge(plan_step, 9)
                nc.vector.tensor_tensor(local[:], tile_no[:], first_tile[:], ALU.subtract)
                nc.vector.tensor_tensor(owned[:], is_owner[:], count[:].unsqueeze(1).broadcast_to([P, N, E]), ALU.mult)
                nc.vector.tensor_copy(column_i[:], column_f[:]).then_inc(plan_step, 1)
                dve.wait_ge(plan_step, 10)
                nc.vector.tensor_reduce(owner_count[:], owned[:], AX_X, ALU.add)
                nc.vector.tensor_scalar(lane_no[:], local[:], float(P), lane[:, 0:1], ALU.mult, ALU.add)
                nc.vector.scalar_tensor_tensor(at_f[:], local[:], float(P), at_f[:], ALU.mult, ALU.add).then_inc(plan_step, 1)
                dve.wait_ge(plan_step, 11)
                nc.vector.tensor_scalar(at_f[:], at_f[:], float(spare), None, ALU.min)
                nc.vector.tensor_tensor(skip[:], lane_no[:], owner_count[:], ALU.is_ge).then_inc(plan_step, 1)
                dve.wait_ge(plan_step, 12)
                nc.vector.tensor_scalar(skip[:], skip[:], float(2 * tokens), None, ALU.mult)
                nc.vector.tensor_copy(at_i[:], at_f[:]).then_inc(plan_ready, 1)
                dve.wait_ge(plan_ready, 2)

                def sorted_norm(i, k, first):
                    j = RING * i + k
                    dve.wait_ge(srow_loaded[k], 16 * (i + 1))
                    if not (first and k < 2):
                        dve.wait_ge(sxT_ps_ready, j - 1)
                    nc.vector.tensor_scalar(sxn[:, k % 2, :], srow[:, k, 0:D], srow[:, k, D + 1:D + 2],
                                            srow[:, k, D:D + 1], ALU.subtract, ALU.mult).then_inc(sxn_ready, 1)

                def sorted_out(i, k, first):
                    j = RING * i + k
                    column = dve.value_load(column_i[0:1, bass.ds(j, 1)],
                                            min_val=0, max_val=(E - 1) * D)
                    dve.wait_ge(product_ready, j + 1)
                    if not (first and k < 2):
                        dve.wait_ge(act_ready, j - 1)
                    nc.vector.tensor_tensor(pre[:, k % 2, :], psum[2 + k % 2][:, 0:D], beb[:, bass.ds(column, D)],
                                            ALU.add).then_inc(pre_ready, 1)
                    if not first:
                        dve.wait_ge(y_stored[k], 16 * i)
                    nc.vector.tensor_tensor(to_f[:, k:k + 1], srow[:, k, D + 3:D + 4],
                                            skip[:, bass.ds(j, 1)],
                                            ALU.add).then_inc(to_step, 1)
                    dve.wait_ge(to_step, j + 1)
                    nc.vector.tensor_copy(to_i[:, k:k + 1], to_f[:, k:k + 1])
                    dve.wait_ge(act_ready, j + 1)
                    nc.vector.tensor_tensor(y[:, k, :], act_out[:, k % 2, :], srow[:, k, 0:D], ALU.add).then_inc(y_ready, 1)

                sorted_norm(0, 0, True)
                for k in range(1, RING):
                    sorted_norm(0, k, True)
                    sorted_out(0, k - 1, True)

                def ring(i, first):
                    for k in range(RING):
                        sorted_norm(i, k, False)
                        sorted_out(i, k - 1, False) if k else sorted_out(i - 1, RING - 1, first)

                ring(1, True)
                with dve.Fori(2, N // RING) as i:
                    ring(i, False)
                sorted_out(N // RING - 1, RING - 1, False)

            @block.tensor
            def _(pe):
                ident = const["ident"]
                pe.wait_ge(w_loaded, 16 * (3 + DC))
                pe.wait_ge(masks_made, 1)
                pe.wait_ge(bg_placed, 16 * 3)

                def transposes(i, k, first):
                    n = 2 * i + k
                    pe.wait_ge(xn_ready, n + 1)
                    for c in range(DC):
                        if not first:
                            pe.wait_ge(xT_ready, DC * (n - 1) + c + 1)
                        for t in range(GT):
                            last = nc.tensor.transpose(xT_ps[c][:, t * P:(t + 1) * P], xn[:, k, t, c * P:(c + 1) * P], ident[:])
                        last.then_inc(xT_ps_ready, 1)

                def gate(i, k, first):
                    n = 2 * i + k
                    pe.wait_ge(xT_ready, DC * (n + 1))
                    for h in range(2):
                        if not first:
                            pe.wait_ge(exp_done, GT * (n - 1) + 2 * h + 2)
                        nc.tensor.matmul(gate_ps[h][:], ones[0:3, :], bg_rows[:].unsqueeze(1).broadcast_to([3, 2, D]),
                                         start=True, stop=False, skip_group_check=True)
                        for t in range(2 * h, 2 * h + 2):
                            out = gate_ps[h][:, (t % 2) * D:(t % 2 + 1) * D]
                            for c in range(DC):
                                last = nc.tensor.matmul(out, xT[:, c, t * P:(t + 1) * P], wg[:, c, :], start=False,
                                                        stop=c == DC - 1, skip_group_check=True)
                        last.then_inc(gate_ready, 1)

                def ranks(i, k, first):
                    n = 2 * i + k
                    pe.wait_ge(onehot_ready, n + 1)
                    if not first:
                        pe.wait_ge(route_step, ROUTE_STEPS * (n - 1) + 6)
                    for t in range(GT + 1):
                        out = rank_ps[:, t * E:(t + 1) * E]
                        for s in range(t):
                            last = nc.tensor.matmul(out, ones[:], onehot[:, s, :], start=s == 0, stop=t == GT and s == t - 1)
                        if t < GT:
                            nc.tensor.matmul(out, before[:], onehot[:, t, :], start=t == 0, stop=True)
                    last.then_inc(rank_ready, 1)

                transposes(0, 0, True)
                gate(0, 0, True)
                transposes(0, 1, False)
                ranks(0, 0, True)
                with pe.Fori(1, groups // 2) as i:
                    gate(i - 1, 1, False)
                    transposes(i, 0, False)
                    ranks(i - 1, 1, False)
                    gate(i, 0, False)
                    transposes(i, 1, False)
                    ranks(i, 0, False)
                gate(groups // 2 - 1, 1, False)
                ranks(groups // 2 - 1, 1, False)

                pe.wait_ge(plan_ready, 2)

                def sorted_transposes(i, k, first):
                    j = RING * i + k
                    pe.wait_ge(sxn_ready, j + 1)
                    if not (first and k < 2):
                        pe.wait_ge(sxT_ready, j - 1)
                    for c in range(DC):
                        last = nc.tensor.transpose(psum[k % 2][:, c * P:(c + 1) * P], sxn[:, k % 2, c * P:(c + 1) * P], ident[:])
                    last.then_inc(sxT_ps_ready, 1)

                def product(i, k, first):
                    j = RING * i + k
                    column = pe.value_load(column_i[0:1, bass.ds(j, 1)],
                                           min_val=0, max_val=(E - 1) * D)
                    pe.wait_ge(sxT_ready, j + 1)
                    if not (first and k < 2):
                        pe.wait_ge(pre_ready, j - 1)
                    for c in range(DC):
                        last = nc.tensor.matmul(psum[2 + k % 2][:, 0:D], sxT[:, k % 2, c, :], we[:, c, bass.ds(column, D)],
                                                start=c == 0, stop=c == DC - 1)
                    last.then_inc(product_ready, 1)

                sorted_transposes(0, 0, True)
                for k in range(1, RING):
                    sorted_transposes(0, k, True)
                    product(0, k - 1, True)
                with pe.Fori(1, N // RING) as i:
                    for k in range(RING):
                        sorted_transposes(i, k, False)
                        if k:
                            product(i, k - 1, False)
                        else:
                            product(i - 1, RING - 1, False)
                product(N // RING - 1, RING - 1, False)


def attention_phase(nc, psum, const, x_in, x_out, W, rope_table, scratch):
    NB = x_in.shape[0] // T
    xv = x_in.rearrange("(b t p) d -> b p t d", p=P, t=TT)
    ov = x_out.rearrange("(b t p) d -> b p t d", p=P, t=TT)
    ctx = ExitStack()
    with ctx:
        def sb(n, shape, dt=F32):
            return ctx.enter_context(nc.sbuf_tensor(f"at_{n}", shape, dt))

        def sem(n):
            return ctx.enter_context(nc.semaphore(f"at_{n}"))

        w_down = sb("w_down", [P, DC, C])
        w_q = sb("w_q", [P, DC, D])
        w_qr = sb("w_qr", [P, DC, 2 * R])
        w_ku = sb("w_ku", [P, D])
        w_kr = sb("w_kr", [P, 2 * R])
        w_vu = sb("w_vu", [P, D])
        w_o = sb("w_o", [P, NG, D])
        rope = sb("rope", [2 * R, T])
        maskq = sb("maskq", [P, P], BF16)
        maskk = sb("maskk", [P, P], BF16)
        x = sb("x", [P, TT, D])
        stats = sb("stats", [P, TT, 6])
        mv = sb("mv", [P, TT, 2])
        veps = sb("veps", [P, TT])
        power = sb("power", [P, TT])
        rstd = sb("rstd", [P, TT])
        xn = sb("xn", [P, TT, D])
        xT = sb("xT", [P, DC, T])
        ckvT = sb("ckvT", [P, T])
        qc = sb("qc", [P, DC, T])
        kc = sb("kc", [P, DC, T])
        qc16 = sb("qc16", [P, DC, T], F16)
        kc16 = sb("kc16", [P, DC, T], F16)
        turned = sb("turned", [R, 2, T])
        rot = sb("rot", [R, 2, T])
        rot16 = sb("rot16", [R, 2, T], F16)
        v = sb("v", [P, TT, NH, 2 * HD])
        qs = sb("qs", [KC, NH, T])
        ks = sb("ks", [KC, NH, T])
        qs16 = sb("qs16", [KC, NH, T], F16)
        ks16 = sb("ks16", [KC, NH, T], F16)
        nmax = sb("nmax", [P, GH, TT])
        nmaxT = sb("nmaxT", [GH * TT, P])
        K_OFF = [0, T, T + 3 * P + P, T + 3 * P]
        K_N = [T - P * j for j in range(TT)]
        probs = sb("probs", [P, 2, GH, sum(K_N)])
        sums = sb("sums", [P, T])
        o_n = sb("o_n", [P, NG, T])
        res = sb("res", [P, TT, D])

        SC = psum[0:3]
        MX = psum[3:5]
        O = psum[5]
        PJ = psum[6:8]

        w_loaded = sem("w_loaded")
        zeroed = sem("zeroed")
        masks_made = sem("masks_made")
        stacks_set = sem("stacks_set")
        x_loaded = sem("x_loaded")
        res_loaded = sem("res_loaded")
        ln_stats = sem("ln_stats")
        ln_aggr = sem("ln_aggr")
        var_eps = sem("var_eps")
        ln_rstd = sem("ln_rstd")
        xn_ready = sem("xn_ready")
        pj_ready = [sem("pj_ready0"), sem("pj_ready1")]
        pj_free = [sem("pj_free0"), sem("pj_free1")]
        rot_step = sem("rot_step")
        rot_ready = sem("rot_ready")
        half_ready = sem("half_ready")
        scratch_written = sem("scratch_written")
        stack_loaded = [sem(f"stack_loaded{g}") for g in range(NG)]
        mx_ready = sem("mx_ready")
        mx_free = sem("mx_free")
        nmax_written = sem("nmax_written")
        nmax_loaded = [sem(f"nmax_loaded{g}") for g in range(NG)]
        sc_ready = sem("sc_ready")
        probs_ready = sem("probs_ready")
        o_ready = sem("o_ready")
        o_free = sem("o_free")
        norm_step = sem("norm_step")
        y_stored = sem("y_stored")

        N_SC = 3 * NH
        N_MX = 12 * NG
        N_O = NG + 2
        N_PJ = (6, 5)

        def pj(b, u):
            return u % 2, N_PJ[u % 2] * b + u // 2

        def wait_out(eng, b, u):
            bank, before = pj(b, u)
            eng.wait_ge(pj_free[bank], before + 1)

        with nc.Block() as block:
            @block.sync
            def _(sp):
                w = 0
                for dst, src in ((w_down[:], W["kv_down"].rearrange("(c p) n -> p c n", p=P)),
                                 (w_q[:], W["q"].rearrange("(c p) n -> p c n", p=P)),
                                 (w_qr[:, :, 0:R], W["q_rope"].rearrange("(c p) n -> p c n", p=P)),
                                 (w_qr[:, :, R:R + R // 2], W["q_rope"].rearrange("(c p) n -> p c n", p=P)[:, :, R // 2:R]),
                                 (w_qr[:, :, R + R // 2:2 * R], W["q_rope"].rearrange("(c p) n -> p c n", p=P)[:, :, 0:R // 2]),
                                 (w_ku[:], W["k_up"]), (w_vu[:], W["v_up"]),
                                 (w_kr[:, 0:R], W["k_rope"]),
                                 (w_kr[:, R:R + R // 2], W["k_rope"][:, R // 2:R]),
                                 (w_kr[:, R + R // 2:2 * R], W["k_rope"][:, 0:R // 2]),
                                 (rope[:], rope_table)):
                    sp.dma_start(dst, src).then_inc(w_loaded, 16)
                    w += 16
                sp.wait_ge(zeroed, 1)
                sp.nop(nofuse=True)
                sp.wait_ge(stacks_set, 1)
                sp.nop(nofuse=True)
                for h in range(NH):
                    hq, g = h % GH, h // GH
                    sp.dma_start(w_o[32 * hq:32 * hq + HD, g, :], W["o"][h * HD:(h + 1) * HD, :]).then_inc(w_loaded, 16)

                def load_x(b):
                    sp.dma_start(x[:], xv[b]).then_inc(x_loaded, 16)

                def write_scratch(b):
                    for u in (3, 4, 6, 7):
                        wait_out(sp, b, u)
                        sp.nop(nofuse=True)
                    sp.dma_start(scratch["q"][b].rearrange("(c p) n -> p c n", p=P), qc[:]).then_inc(scratch_written, 16)
                    sp.dma_start(scratch["k"][b].rearrange("(c p) n -> p c n", p=P), kc[:]).then_inc(scratch_written, 16)
                    sp.wait_ge(half_ready, 4 * b + 4)
                    sp.nop(nofuse=True)
                    sp.dma_start(scratch["q16"][b].rearrange("(c p) n -> p c n", p=P), qc16[:]).then_inc(scratch_written, 16)
                    sp.dma_start(scratch["k16"][b].rearrange("(c p) n -> p c n", p=P), kc16[:]).then_inc(scratch_written, 16)

                def load_stack(b, g, first):
                    if g == 0:
                        sp.wait_ge(scratch_written, 64 * (b + 1))
                        sp.nop(nofuse=True)
                        sp.wait_ge(half_ready, 4 * b + 4)
                        sp.nop(nofuse=True)
                    if not first:
                        sp.wait_ge(sc_ready, N_SC * (b - 1) + 3 * GH * (g + 1))
                        sp.nop(nofuse=True)
                    slots = slice(g * GH, (g + 1) * GH)
                    for k, (dst, key, r) in enumerate(((qs, "q", rot[:, 0, :]), (ks, "k", rot[:, 1, :]),
                                                       (qs16, "q16", rot16[:, 0, :]), (ks16, "k16", rot16[:, 1, :]))):
                        sp.dma_start(dst[0:R, slots, :], r.unsqueeze(1).broadcast_to([R, GH, T])).then_inc(stack_loaded[g], 16)
                        src = scratch[key][b][g * GH * HD:(g + 1) * GH * HD, :].rearrange("(h r) n -> r h n", r=HD)
                        sp.dma_start(dst[R:R + HD, slots, :], src).then_inc(stack_loaded[g], 16)

                def load_max(b, g):
                    sp.wait_ge(mx_free, N_MX * b + 12 * (g + 1))
                    sp.nop(nofuse=True)
                    row = scratch["nmax"][b, g]
                    sp.dma_start(row.rearrange("(s q) -> s q", q=P), nmaxT[:]).then_inc(nmax_written, 16)
                    sp.wait_ge(nmax_written, 16 * (NG * b + g + 1))
                    sp.nop(nofuse=True)
                    sp.dma_start(qs[ROW_MAX:ROW_MAX + 1, g * GH:(g + 1) * GH, :],
                                 row.rearrange("(o h t) -> o h t", o=1, t=T)).then_inc(nmax_loaded[g], 16)

                def store(b):
                    sp.wait_ge(o_free, N_O * (b + 1))
                    sp.nop(nofuse=True)
                    sp.dma_start(ov[b], res[:]).then_inc(y_stored, 16)

                def body(b, first, last):
                    load_stack(b, 3, first)
                    if not last:
                        sp.wait_ge(xn_ready, b + 2)
                        sp.nop(nofuse=True)
                    if not first:
                        store(b - 1)
                        sp.wait_ge(y_stored, 16 * b)
                        sp.nop(nofuse=True)
                    sp.dma_start(res[:], xv[b]).then_inc(res_loaded, 16)
                    load_max(b, 2)
                    if not last:
                        write_scratch(b + 1)
                        sp.dma_start(x[:], xv[(b + 2) % NB]).then_inc(x_loaded, 16)
                        load_stack(b + 1, 0, False)
                    load_max(b, 3)
                    if not last:
                        load_stack(b + 1, 1, False)
                        load_max(b + 1, 0)
                        load_stack(b + 1, 2, False)
                        load_max(b + 1, 1)

                load_x(0)
                write_scratch(0)
                sp.wait_ge(xn_ready, 1)
                sp.nop(nofuse=True)
                load_x(1)
                for g in range(3):
                    load_stack(0, g, True)
                load_max(0, 0)
                load_max(0, 1)
                body(0, True, False)
                with sp.Fori(1, NB - 1) as b:
                    body(b, False, False)
                body(NB - 1, False, True)
                store(NB - 1)
                sp.wait_ge(y_stored, 16 * NB)
                sp.nop(nofuse=True)
                sp.wait_ge(x_loaded, 16 * (NB + 1))
                sp.nop(nofuse=True)

            @block.gpsimd
            def _(pool):
                nc.gpsimd.memset(power[:], -0.5).then_inc(var_eps, 1)
                nc.gpsimd.memset(w_o[:], 0.0)
                nc.gpsimd.memset(qs16[:], 0.0)
                nc.gpsimd.memset(ks16[:], 0.0)
                nc.gpsimd.memset(v[:], 1.0)
                nc.gpsimd.memset(maskq[:], 0.0)
                nc.gpsimd.memset(maskk[:], 0.0).then_inc(zeroed, 1)
                pool.wait_ge(zeroed, 1)
                nc.gpsimd.affine_select(out=maskq[:], in_=maskq[:], compare_op=ALU.is_ge, fill=MASKED,
                                        base=0, pattern=[[-1, P]], channel_multiplier=1)
                nc.gpsimd.affine_select(out=maskk[:], in_=maskk[:], compare_op=ALU.is_ge, fill=MASKED,
                                        base=0, pattern=[[1, P]], channel_multiplier=-1).then_inc(masks_made, 1)

                def ln(b):
                    pool.wait_ge(ln_aggr, b + 1)
                    pool.nop(nofuse=True)
                    nc.gpsimd.tensor_scalar(veps[:], mv[:, :, 1], EPS, None, ALU.add).then_inc(var_eps, 1)
                    pool.wait_ge(var_eps, b + 2)
                    nc.gpsimd.tensor_tensor(rstd[:], veps[:], power[:], ALU.pow).then_inc(ln_rstd, 1)

                def halves(b, first):
                    if not first:
                        pool.wait_ge(scratch_written, 64 * b)
                        pool.wait_ge(stack_loaded[NG - 1], 128 * b)
                    pool.wait_ge(rot_ready, 2 * b + 1)
                    pool.nop(nofuse=True)
                    nc.gpsimd.tensor_copy(rot16[:, 0, :], rot[:, 0, :]).then_inc(half_ready, 1)
                    for u in (3, 4, 6, 7):
                        wait_out(pool, b, u)
                        pool.nop(nofuse=True)
                    nc.gpsimd.tensor_copy(qc16[:], qc[:]).then_inc(half_ready, 1)
                    nc.gpsimd.tensor_copy(kc16[:], kc[:]).then_inc(half_ready, 1)
                    pool.wait_ge(rot_ready, 2 * b + 2)
                    pool.nop(nofuse=True)
                    nc.gpsimd.tensor_copy(rot16[:, 1, :], rot[:, 1, :]).then_inc(half_ready, 1)

                ln(0)
                halves(0, True)
                with pool.Fori(1, NB) as b:
                    ln(b)
                    halves(b, False)

            @block.vector
            def _(dve):
                nc.vector.memset(qs[:], 0.0)
                nc.vector.memset(ks[:], 1.0).then_inc(stacks_set, 1)
                dve.wait_ge(w_loaded, 16 * (11 + NH))

                def ln(b, first):
                    dve.wait_ge(x_loaded, 16 * (b + 1))
                    for t in range(TT):
                        last = nc.vector.bn_stats(stats[:, t, :], x[:, t, :])
                    last.then_inc(ln_stats, 1)
                    dve.wait_ge(ln_stats, b + 1)
                    dve.nop(nofuse=True)
                    for t in range(TT):
                        last = nc.vector.bn_aggr(mv[:, t, :], stats[:, t, :])
                    last.then_inc(ln_aggr, 1)
                    dve.wait_ge(ln_rstd, b + 1)
                    if not first:
                        dve.wait_ge(pj_ready[1], pj(b - 1, 1)[1] + 1)
                    for t in range(TT):
                        last = nc.vector.tensor_scalar(xn[:, t, :], x[:, t, :], mv[:, t, 0:1], rstd[:, t:t + 1],
                                                       ALU.subtract, ALU.mult)
                    last.then_inc(xn_ready, 1)

                def rotate(b, s, u, first):
                    bank, before = pj(b, u)
                    dve.wait_ge(pj_ready[bank], before + 1)
                    if not first:
                        dve.wait_ge(stack_loaded[NG - 1], 128 * b)
                    if not (first and s == 0):
                        dve.wait_ge(rot_ready, 2 * b + s)
                    nc.vector.tensor_tensor(turned[:, 0, :], PJ[bank][0:R, :], rope[0:R, :], ALU.mult)
                    nc.vector.tensor_tensor(turned[:, 1, :], PJ[bank][R:2 * R, :], rope[R:2 * R, :],
                                            ALU.mult).then_inc(pj_free[bank], 1)
                    dve.wait_ge(pj_free[bank], before + 1)
                    nc.vector.tensor_tensor(rot[:, s, :], turned[:, 0, :], turned[:, 1, :], ALU.add).then_inc(rot_ready, 1)

                def maxima(b, g, quarter, first):
                    for j in range(3 * quarter, 3 * quarter + 3):
                        use = N_MX * b + 12 * g + j
                        bank = MX[j % 2]
                        dve.wait_ge(mx_ready, use + 1)
                        if j == 0:
                            ins = nc.vector.tensor_reduce(nmax[:, :, 0], bank[:].rearrange("p (h k) -> p h k", h=GH),
                                                          AX_X, ALU.max, negate=True)
                        elif j < 3:
                            h = 2 * (j - 1)
                            ins = nc.vector.tensor_reduce(nmax[:, h:h + 2, 1], bank[:].rearrange("p (h k) -> p h k", h=2),
                                                          AX_X, ALU.max, negate=True)
                        elif j < 7:
                            ins = nc.vector.tensor_reduce(nmax[:, j - 3, 2:3], bank[:, 0:3 * P], AX_X, ALU.max, negate=True)
                        elif j < 11:
                            ins = nc.vector.tensor_reduce(nmax[:, j - 7, 3:4], bank[:], AX_X, ALU.max, negate=True)
                        else:
                            if not (first and g == 0):
                                dve.wait_ge(nmax_written, 16 * (NG * b + g))
                            ins = nc.vector.tensor_copy(nmaxT[:], bank[0:GH * TT, 0:P])
                        ins.then_inc(mx_free, 1)

                def normalise(b, g):
                    dve.wait_ge(o_ready, N_O * b + g + 1)
                    dve.nop(nofuse=True)
                    nc.vector.stream_shuffle(sums[:], O[:], [HD] * HD + list(range(HD, 32))).then_inc(norm_step, 1)
                    dve.wait_ge(norm_step, 2 * (NG * b + g) + 1)
                    nc.vector.reciprocal(sums[:], sums[:]).then_inc(norm_step, 1)
                    dve.wait_ge(norm_step, 2 * (NG * b + g) + 2)
                    nc.vector.tensor_tensor(o_n[:, g, :], O[:], sums[:], ALU.mult).then_inc(o_free, 1)

                def output(b):
                    dve.wait_ge(res_loaded, 16 * (b + 1))
                    for half in range(2):
                        dve.wait_ge(o_ready, N_O * b + NG + half + 1)
                        nc.vector.tensor_tensor(res[:, 2 * half:2 * half + 2, :],
                                                O[:].rearrange("p (t d) -> p t d", t=2),
                                                res[:, 2 * half:2 * half + 2, :], ALU.add).then_inc(o_free, 1)

                def body(b, first, last):
                    for s in range(NH):
                        g, hq = s // GH, s % GH
                        if hq == 0 and not (first and g == 0):
                            normalise(b, g - 1) if g else normalise(b - 1, NG - 1)
                        if s == 0 and not last:
                            ln(b + 1, False)
                        if s == 2 and not first:
                            output(b - 1)
                        if s == 4 and not last:
                            rotate(b + 1, 0, 5, False)
                        if s == 5 and not last:
                            rotate(b + 1, 1, 8, False)
                        if g < 2:
                            maxima(b, g + 2, hq, False)
                        elif not last:
                            maxima(b + 1, g - 2, hq, False)

                ln(0, True)
                rotate(0, 0, 5, True)
                rotate(0, 1, 8, True)
                for g in range(2):
                    for quarter in range(4):
                        maxima(0, g, quarter, True)
                body(0, True, False)
                with dve.Fori(1, NB - 1) as b:
                    body(b, False, False)
                body(NB - 1, False, True)
                normalise(NB - 1, NG - 1)
                output(NB - 1)

            @block.scalar
            def _(act):
                def copy_out(b, u, first):
                    bank, before = pj(b, u)
                    act.wait_ge(pj_ready[bank], before + 1)
                    src = PJ[bank]
                    if u < 2:
                        if u == 0 and not first:
                            act.wait_ge(pj_ready[1], pj(b - 1, 5)[1] + 1)
                        dst = xT[:, u, :]
                    elif u == 2:
                        if not first:
                            act.wait_ge(pj_ready[0], pj(b - 1, 10)[1] + 1)
                        dst = ckvT[:]
                    elif u in (3, 4):
                        if u == 3 and not first:
                            act.wait_ge(scratch_written, 64 * b)
                        dst = qc[:, u - 3, :]
                    elif u in (6, 7):
                        dst = kc[:, u - 6, :]
                    else:
                        if u == 9 and not first:
                            act.wait_ge(o_ready, N_O * (b - 1) + NG)
                        t = 2 * (u - 9)
                        dst = v[:, t:t + 2, :, 0:HD]
                        src = src.rearrange("p (t h d) -> p t h d", t=2, h=NH)
                    nc.scalar.activation(dst, src if u >= 9 else src[:], ACT.Copy).then_inc(pj_free[bank], 1)

                def exps(b, g, hq, first):
                    if hq == 0 and not (first and g < 2):
                        before = N_O * b + g - 2 if g >= 2 else N_O * (b - 1) + g + 2
                        act.wait_ge(o_ready, before + 1)
                    h = GH * g + hq
                    for j in range(3):
                        act.wait_ge(sc_ready, N_SC * b + 3 * h + j + 1)
                        n = K_N[2] if j == 2 else T
                        at = j * T
                        nc.scalar.activation(probs[:, g % 2, hq, at:at + n], SC[j][:, 0:n], ACT.Exp,
                                             scale=SCALE).then_inc(probs_ready, 1)

                def body(b, first, last):
                    for s in range(NH):
                        exps(b, s // GH, s % GH, first)
                        if s == 1:
                            copy_out(b, 9, first)
                            copy_out(b, 10, first)
                        if not last:
                            for u in {2: (0, 1), 3: (2, 3, 4), 5: (6, 7)}.get(s, ()):
                                copy_out(b + 1, u, False)

                for u in (0, 1, 2, 3, 4, 6, 7):
                    copy_out(0, u, True)
                body(0, True, False)
                with act.Fori(1, NB - 1) as b:
                    body(b, False, False)
                body(NB - 1, False, True)

            @block.tensor
            def _(pe):
                pe.wait_ge(w_loaded, 16 * (11 + NH))
                pe.wait_ge(masks_made, 1)
                ident, identb = const["ident"], const["identb"]

                def project(b, u, first):
                    bank, before = pj(b, u)
                    if not (first and u < 2):
                        pe.wait_ge(pj_free[bank], before)
                    out = PJ[bank]
                    if u < 2:
                        if u == 0:
                            pe.wait_ge(xn_ready, b + 1)
                        for t in range(TT):
                            last = nc.tensor.transpose(out[:, t * P:(t + 1) * P], xn[:, t, u * P:(u + 1) * P], ident[:])
                    elif u in (2, 3, 4, 5):
                        if u == 2:
                            wait_out(pe, b, 0)
                            wait_out(pe, b, 1)
                        for c in range(DC):
                            lhsT = {2: w_down[:, c, :], 3: w_q[:, c, 0:P], 4: w_q[:, c, P:2 * P], 5: w_qr[:, c, :]}[u]
                            last = nc.tensor.matmul(out[0:lhsT.shape[-1], :], lhsT, xT[:, c, :], start=c == 0, stop=c == DC - 1)
                    elif u in (6, 7, 8):
                        if u == 6:
                            wait_out(pe, b, 2)
                        lhsT = {6: w_ku[:, 0:P], 7: w_ku[:, P:2 * P], 8: w_kr[:]}[u]
                        last = nc.tensor.matmul(out[0:lhsT.shape[-1], :], lhsT, ckvT[:], start=True, stop=True)
                    else:
                        for k in range(2):
                            t = 2 * (u - 9) + k
                            last = nc.tensor.matmul(out[:, k * D:(k + 1) * D], ckvT[:, t * P:(t + 1) * P], w_vu[:],
                                                    start=True, stop=True)
                    last.then_inc(pj_ready[bank], 1)

                def maxima(b, g, quarter, first):
                    if quarter == 0:
                        pe.wait_ge(stack_loaded[g], 128 * (b + 1))
                    for j in range(3 * quarter, 3 * quarter + 3):
                        use = N_MX * b + 12 * g + j
                        out = MX[j % 2]
                        if not (first and g == 0 and j < 2):
                            pe.wait_ge(mx_free, use if j == 11 else use - 1)
                        if j == 11:
                            last = nc.tensor.transpose(out[0:GH * TT, 0:P], nmax[:].rearrange("p h i -> p (h i)"), ident[:])
                        else:
                            if j == 0:
                                i, heads = 0, range(GH)
                            elif j < 3:
                                i, heads = 1, range(2 * (j - 1), 2 * j)
                            elif j < 7:
                                i, heads = 2, (j - 3,)
                            else:
                                i, heads = 3, (j - 7,)
                            n = P * (i + 1)
                            for k, hq in enumerate(heads):
                                slot = GH * g + hq
                                nc.tensor.matmul(out[:, k * n:(k + 1) * n], qs16[:, slot, i * P:(i + 1) * P],
                                                 ks16[:, slot, 0:n], start=True, stop=False)
                                last = nc.tensor.matmul(out[:, (k + 1) * n - P:(k + 1) * n], identb[:], maskq[:],
                                                        start=False, stop=True)
                        last.then_inc(mx_ready, 1)

                def scores(b, g, hq, first):
                    slot = GH * g + hq
                    if hq == 0:
                        pe.wait_ge(stack_loaded[g], 128 * (b + 1))
                        pe.wait_ge(nmax_loaded[g], 16 * (b + 1))
                    for j in range(3):
                        if not (first and slot == 0):
                            pe.wait_ge(probs_ready, N_SC * b + 3 * slot + j - 2)
                        for kt in ((0,), (1, 3), (2,))[j]:
                            at = K_OFF[kt] - j * T
                            n = K_N[kt]
                            nc.tensor.matmul(SC[j][:, at:at + n], ks[:, slot, kt * P:(kt + 1) * P],
                                             qs[:, slot, kt * P:T], start=True, stop=False)
                            last = nc.tensor.matmul(SC[j][:, at:at + P], identb[:], maskk[:], start=False, stop=True)
                        last.then_inc(sc_ready, 1)

                def weigh(b, g, first):
                    if not (first and g == 0):
                        pe.wait_ge(o_free, N_O * b + g)
                    pe.wait_ge(probs_ready, N_SC * b + 3 * GH * (g + 1))
                    if g == 0:
                        wait_out(pe, b, 9)
                        wait_out(pe, b, 10)
                    for kt in range(TT):
                        for hq in range(GH):
                            last = nc.tensor.matmul(O[32 * hq:32 * hq + 32, kt * P:T], v[:, kt, GH * g + hq, :],
                                                    probs[:, g % 2, hq, K_OFF[kt]:K_OFF[kt] + K_N[kt]],
                                                    start=kt == 0, stop=kt == TT - 1)
                    last.then_inc(o_ready, 1)

                def output(b):
                    for half in range(2):
                        pe.wait_ge(o_free, N_O * b + NG + half)
                        for k in range(2):
                            t = 2 * half + k
                            for g in range(NG):
                                last = nc.tensor.matmul(O[:, k * D:(k + 1) * D], o_n[:, g, t * P:(t + 1) * P], w_o[:, g, :],
                                                        start=g == 0, stop=g == NG - 1)
                        last.then_inc(o_ready, 1)

                def body(b, first, last):
                    for s in range(NH):
                        g, hq = s // GH, s % GH
                        scores(b, g, hq, first)
                        if hq == 0 and not (first and g == 0):
                            weigh(b, g - 1, first) if g else weigh(b - 1, NG - 1, False)
                        if s == 1:
                            project(b, 9, False)
                            project(b, 10, False)
                        if s == 2 and not first:
                            output(b - 1)
                        if not last:
                            for u in {2: (0, 1), 3: (2, 3, 4), 4: (5, 6), 5: (7, 8)}.get(s, ()):
                                project(b + 1, u, False)
                        if g < 2:
                            maxima(b, g + 2, hq, False)
                        elif not last:
                            maxima(b + 1, g - 2, hq, False)

                for u in range(9):
                    project(0, u, True)
                for g in range(2):
                    for quarter in range(4):
                        maxima(0, g, quarter, True)
                body(0, True, False)
                with pe.Fori(1, NB - 1) as b:
                    body(b, False, False)
                body(NB - 1, False, True)
                weigh(NB - 1, NG - 1, False)
                output(NB - 1)


def build(nc, a, rope_table, out):
    N = a["x"].shape[0]
    x1 = nc.dram_tensor("x1", [N, D], F32, kind="Internal").ap()
    x2 = nc.dram_tensor("x2", [N, D], F32, kind="Internal").ap()
    routed = nc.dram_tensor("routed", [E * (N + P) + P, ROW], F32, kind="Internal").ap()
    scratch = {k: nc.dram_tensor(f"scratch_{k}", [N // T, D, T], F16 if "16" in k else F32, kind="Internal").ap()
               for k in ("q", "k", "q16", "k16")}
    scratch["nmax"] = nc.dram_tensor("scratch_nmax", [N // T, NG, GH * T], F32, kind="Internal").ap()
    with ExitStack() as ctx:
        psum = [ctx.enter_context(nc.psum_tensor(f"bank{i}", [P, 512], F32)) for i in range(8)]
        ident = ctx.enter_context(nc.sbuf_tensor("ident", [P, P], F32))
        identb = ctx.enter_context(nc.sbuf_tensor("identb", [P, P], BF16))
        made = ctx.enter_context(nc.semaphore("ident_made"))
        with nc.Block() as block:
            @block.gpsimd
            def _(pool):
                nc.gpsimd.memset(ident[:], 0.0)
                nc.gpsimd.memset(identb[:], 0.0).then_inc(made, 1)
                pool.wait_ge(made, 1)
                for m in (ident, identb):
                    nc.gpsimd.affine_select(out=m[:], in_=m[:], compare_op=ALU.not_equal, fill=1.0,
                                            base=0, pattern=[[-1, P]], channel_multiplier=1)
        const = {"ident": ident, "identb": identb}
        ffn = (a["Wg"], a["bg"], a["We"], a["be"])
        ffn_phase(nc, "f1", psum, const, a["x"], x1, routed, *ffn)
        attention_phase(nc, psum, const, x1, x2, a, rope_table, scratch)
        ffn_phase(nc, "f2", psum, const, x2, out, routed, *ffn)


def rope_constants(np):
    inv = (np.float32(1.0) / np.power(np.float32(10000.0), np.arange(0, R, 2, dtype=np.float32) / np.float32(R))).astype(np.float32)
    angle = np.outer(inv, np.arange(T, dtype=np.float32)).astype(np.float32)
    cos, sin = np.cos(angle), np.sin(angle)
    return np.concatenate([cos, cos, -sin, sin])


def kernel(**inputs):
    import numpy as np
    import concourse.bacc as bacc
    from concourse.bass_utils import run_bass_kernel_spmd

    nc = bacc.Bacc("TRN2", target_bir_lowering=False, num_devices=1)
    x = np.ascontiguousarray(inputs["L0_attn_x"])
    shape = x.shape
    arrays = {"x": x.reshape(-1, shape[-1])}
    for name in inputs:
        if name != "L0_attn_x":
            short = name.replace("L0_attn_W_", "").replace("L0_ffn_", "")
            arrays[short] = np.ascontiguousarray(inputs[name])
    arrays["rope_table"] = rope_constants(np)
    aps = {n: nc.dram_tensor(f"in_{n}", v.shape, mybir.dt.from_np(v.dtype), kind="ExternalInput").ap()
           for n, v in arrays.items()}
    out = nc.dram_tensor("out", arrays["x"].shape, F32, kind="ExternalOutput").ap()
    build(nc, aps, aps["rope_table"], out)
    r = run_bass_kernel_spmd(nc, [{f"in_{n}": v for n, v in arrays.items()}], core_ids=[0])
    return r.results[0]["out"].reshape(shape)
```

```python
from contextlib import ExitStack

import concourse.bass as bass
from concourse import mybir
from concourse.alu_op_type import AluOpType as ALU

F32 = mybir.dt.float32
F16 = mybir.dt.float16
BF16 = mybir.dt.bfloat16
I32 = mybir.dt.int32
U32 = mybir.dt.uint32
ACT = mybir.ActivationFunctionType
AX_X = mybir.AxisListType.X

P = 128
D = 256
DC = D // P
C = 128
R = 32
NH = 16
HD = D // NH
T = 512
TT = T // P
E = 8
EPS = 1e-5
GT = 4
GR = 4
RING = 8
ROW = D + 4
MASKED = -1e30
GH = 4
NG = NH // GH
HR = 2 * HD
KC = HR + 2 * R
ROW_MAX = KC
SCALE = float(HD + R) ** -0.5


def ffn_phase(nc, name, psum, const, x_in, x_out, routed, Wg, bg, We, be):
    tokens = x_in.shape[0]
    groups = tokens // (GT * P)
    xv = x_in.rearrange("(g t p) d -> g p t d", p=P, t=GT)
    region = (routed.shape[0] - P) // E
    spare = E * region
    HALF = RING // 2
    sorted_tiles = -(-(tokens // P + E - 1) // RING) * RING
    ctx = ExitStack()
    with ctx:
        def sb(n, shape, dt=F32):
            return ctx.enter_context(nc.sbuf_tensor(f"{name}_{n}", shape, dt))

        def sem(n, count=0):
            if count:
                return [ctx.enter_context(nc.semaphore(f"{name}_{n}{k}")) for k in range(count)]
            return ctx.enter_context(nc.semaphore(f"{name}_{n}"))

        wg = sb("wg", [P, DC, D])
        we = sb("we", [P, DC, E * D])
        beb = sb("beb", [P, E * D])
        bg_row = sb("bg_row", [1, D])
        bg_rest = sb("bg_rest", [1, 2, D])
        bg3 = sb("bg3", [1, 3, D], BF16)
        bg_rows = sb("bg_rows", [3, D], BF16)
        ones = sb("ones", [P, P], BF16)
        before = sb("before", [P, P], BF16)
        power = sb("power", [P, GT])
        ids = sb("ids", [P, E])
        zeros = sb("zeros", [P, ROW])

        x = sb("x", [P, GR, GT, D])
        rows = sb("rows", [P, GR, GT, ROW])
        stats = sb("stats", [P, 2, GT, 6])
        mv = sb("mv", [P, GR, GT, 2])
        veps = sb("veps", [P, GT])
        xn = sb("xn", [P, 2, GT, D])
        xT = sb("xT", [P, 2, DC, GT * P])
        top = sb("top", [P, 2, GT, 8])
        top_at = sb("top_at", [P, 2, GT, 8], U32)
        ntop = sb("ntop", [P, 2, GT])
        expert_i = sb("expert_i", [P, GT], U32)
        expert = sb("expert", [P, GT])
        onehot = sb("onehot", [P, 2, GT, E], BF16)
        junk = sb("junk", [P, GT, D])
        esum = sb("esum", [P, 2, GT])
        prob = sb("prob", [P, GT])
        token = sb("token", [P, GT])
        base = sb("base", [P, 2, E])
        rank = sb("rank", [P, GT, E])
        chosen = sb("chosen", [P, GT, E])
        row_f = sb("row_f", [P, GT])
        row_i = sb("row_i", [P, GR, GT], U32)

        N = sorted_tiles
        start_f = sb("start_f", [P, E])
        start_i = sb("start_i", [P, E], I32)
        count = sb("count", [P, E])
        tiles_i = sb("tiles_i", [P, E], I32)
        tiles_f = sb("tiles_f", [P, E])
        ends = sb("ends", [P, E])
        one8 = sb("one8", [P, E])
        tile_no = sb("tile_no", [P, N])
        past = sb("past", [P, N, E])
        past_tiles = sb("past_tiles", [P, N, E])
        owner = sb("owner", [P, N])
        first_tile = sb("first_tile", [P, N])
        local = sb("local", [P, N])
        is_owner = sb("is_owner", [P, N, E])
        owned = sb("owned", [P, N, E])
        owner_count = sb("owner_count", [P, N])
        at_f = sb("at_f", [P, N])
        at_i = sb("at_i", [P, N], I32)
        column_f = sb("column_f", [P, N])
        column_i = sb("column_i", [P, N], I32)
        lane = sb("lane", [P, 1])
        lane_no = sb("lane_no", [P, N])
        skip = sb("skip", [P, N])

        srow = sb("srow", [P, RING, ROW])
        sxn = sb("sxn", [P, HALF, D])
        sxT = sb("sxT", [P, HALF, DC, P])
        pre = sb("pre", [P, HALF, D])
        act_out = sb("act_out", [P, HALF, D])
        y = sb("y", [P, RING, D])
        to_i = sb("to_i", [P, RING], U32)

        xT_ps = psum[0:2]
        gate_ps = psum[2:6]
        rank_ps = psum[6:8]
        sxT_ps = psum[0:HALF]
        product_ps = psum[HALF:2 * HALF]

        w_loaded = sem("w_loaded")
        bg_loaded = sem("bg_loaded")
        we_loaded = sem("we_loaded")
        made = sem("made")
        bg_step = sem("bg_step")
        bg_placed = sem("bg_placed")
        x_loaded = sem("x_loaded", GR)
        ln_stats = sem("ln_stats")
        ln_aggr = sem("ln_aggr")
        ln_eps = sem("ln_eps")
        ln_rstd = sem("ln_rstd")
        xn_ready = sem("xn_ready")
        xT_ps_ready = sem("xT_ps_ready")
        xT_ready = sem("xT_ready")
        gate_ready = sem("gate_ready")
        top_step = sem("top_step")
        top_ready = sem("top_ready")
        exp_done = sem("exp_done")
        mark_step = sem("mark_step")
        route_step = sem("route_step")
        onehot_ready = sem("onehot_ready")
        rank_ready = sem("rank_ready")
        rows_ready = sem("rows_ready")
        scattered = sem("scattered", GR)
        x_copied = sem("x_copied")
        padded = sem("padded")
        plan_step = sem("plan_step")
        plan_ready = sem("plan_ready")
        srow_loaded = sem("srow_loaded", RING)
        sxn_ready = sem("sxn_ready")
        sxT_ps_ready = sem("sxT_ps_ready")
        sxT_ready = sem("sxT_ready")
        product_ready = sem("product_ready")
        pre_ready = sem("pre_ready")
        act_ready = sem("act_ready")
        y_ready = sem("y_ready")
        y_stored = sem("y_stored", RING)
        ROUTE_STEPS = 8
        MARK_STEPS = 2

        def at(i, k):
            return i + k // GR, k % GR

        def tile_at(i, k):
            return i + k // RING, k % RING

        def gate_steps(eng, step):
            turns = groups // GR
            for k in range(GR):
                step(0, k, True, False)
            with eng.Fori(1, turns - 1) as i:
                for k in range(GR):
                    step(i, k, False, False)
            for k in range(GR):
                step(turns - 1, k, False, True)

        def tile_steps(eng, step):
            turns = N // RING
            for k in range(RING):
                step(0, k, True, False)
            with eng.Fori(1, turns - 1) as i:
                for k in range(RING):
                    step(i, k, False, False)
            for k in range(RING):
                step(turns - 1, k, False, True)

        with nc.Block() as block:
            @block.sync
            def _(sp):
                sp.dma_start(bg_row[:], bg.rearrange("(o f) -> o f", o=1)).then_inc(bg_loaded, 16)
                for k in range(2):
                    sp.dma_start(x[:, k], xv[k]).then_inc(x_loaded[k], 16)
                sp.dma_start(wg[:], Wg.rearrange("(c p) f -> p c f", p=P)).then_inc(w_loaded, 16)
                sp.wait_ge(bg_step, 5)
                for part in range(3):
                    sp.dma_start(bg_rows[part:part + 1, :], bg3[:, part, :]).then_inc(bg_placed, 16)
                for k in range(2, GR):
                    sp.dma_start(x[:, k], xv[k]).then_inc(x_loaded[k], 16)
                for c in range(DC):
                    sp.dma_start(we[:, c, :].rearrange("p (e f) -> p e f", e=E),
                                 We[:, c * P:(c + 1) * P, :].rearrange("e p f -> p e f")).then_inc(we_loaded, 16)
                sp.dma_start(beb[:], be.rearrange("e f -> (e f)").partition_broadcast(P)).then_inc(we_loaded, 16)
                sp.wait_ge(made, 3)
                sp.dma_start(routed[spare:spare + P, :], zeros[:]).then_inc(padded, 16)
                with sp.Fori(1, groups // GR) as i:
                    for k in range(GR):
                        sp.wait_ge(xn_ready, GR * (i - 1) + k + 1)
                        sp.nop(nofuse=True)
                        sp.wait_ge(x_copied, GR * (i - 1) + k + 1)
                        sp.nop(nofuse=True)
                        sp.dma_start(x[:, k], xv[GR * i + k]).then_inc(x_loaded[k], 16)
                sp.wait_ge(plan_ready, 1)
                for e in range(E):
                    row = sp.value_load(start_i[0:1, e:e + 1], min_val=0, max_val=spare - P)
                    sp.dma_start(routed[bass.ds(row, P), :], zeros[:]).then_inc(padded, 16)
                sp.wait_ge(padded, 16 * (E + 1))
                for k in range(GR):
                    sp.wait_ge(scattered[k], 16 * GT * (groups // GR))

                def load(j, k):
                    row = sp.value_load(at_i[0:1, bass.ds(j, 1)], min_val=0, max_val=spare)
                    sp.dma_start(srow[:, k, :], routed[bass.ds(row, P), :]).then_inc(srow_loaded[k], 16)

                sp.wait_ge(plan_ready, 2)
                for k in range(RING):
                    load(k, k)
                with sp.Fori(1, N // RING) as i:
                    for k in range(RING):
                        sp.wait_ge(y_ready, RING * (i - 1) + k + 1)
                        sp.nop(nofuse=True)
                        load(RING * i + k, k)

            @block.gpsimd
            def _(pool):
                nc.gpsimd.memset(power[:], -0.5)
                nc.gpsimd.memset(ones[:], 1.0)
                nc.gpsimd.memset(before[:], 1.0).then_inc(made, 1)
                pool.wait_ge(made, 1)
                nc.gpsimd.affine_select(out=before[:], in_=before[:], compare_op=ALU.is_gt, fill=0.0,
                                        base=0, pattern=[[1, P]], channel_multiplier=-1).then_inc(made, 1)

                def deviation(i, k, first=False):
                    n = GR * i + k
                    if not first:
                        pool.wait_ge(ln_rstd, n)
                    pool.wait_ge(ln_aggr, n + 1)
                    pool.nop(nofuse=True)
                    nc.gpsimd.tensor_scalar(veps[:], mv[:, k, :, 1], EPS, None, ALU.add).then_inc(ln_eps, 1)
                    pool.wait_ge(ln_eps, n + 1)
                    nc.gpsimd.tensor_tensor(mv[:, k, :, 1], veps[:], power[:], ALU.pow).then_inc(ln_rstd, 1)

                def scatter(i, k):
                    n = GR * i + k
                    pool.wait_ge(x_copied, n + 1)
                    pool.nop(nofuse=True)
                    pool.wait_ge(rows_ready, n + 1)
                    pool.nop(nofuse=True)
                    for t in range(GT):
                        nc.gpsimd.indirect_dma_start(
                            out=routed, out_offset=bass.IndirectOffsetOnAxis(ap=row_i[:, k, t:t + 1], axis=0),
                            in_=rows[:, k, t, :], in_offset=None).then_inc(scattered[k], 16)

                def step(i, k, first, last):
                    if not (last and k >= GR - 2):
                        deviation(*at(i, k + 2))
                    if not (first and k == 0):
                        scatter(*at(i - 1, k + GR - 1))

                for k in range(2):
                    deviation(0, k, k == 0)
                nc.gpsimd.memset(zeros[:], 0.0)
                nc.gpsimd.memset(one8[:], 1.0)
                nc.gpsimd.iota(ids[:], [[1, E]], base=0, channel_multiplier=0, allow_small_or_imprecise_dtypes=True)
                nc.gpsimd.iota(tile_no[:], [[1, N]], base=0, channel_multiplier=0, allow_small_or_imprecise_dtypes=True)
                nc.gpsimd.iota(lane[:], [[0, 1]], base=0, channel_multiplier=1, allow_small_or_imprecise_dtypes=True)
                nc.gpsimd.iota(token[:], [[P, GT]], base=0, channel_multiplier=1, allow_small_or_imprecise_dtypes=True)
                nc.gpsimd.iota(base[:, 0, :], [[region, E]], base=0, channel_multiplier=0,
                               allow_small_or_imprecise_dtypes=True)
                nc.gpsimd.iota(start_f[:], [[region, E]], base=0, channel_multiplier=0,
                               allow_small_or_imprecise_dtypes=True).then_inc(made, 1)
                gate_steps(pool, step)
                scatter(groups // GR - 1, GR - 1)

                def combine(i, k, first, last):
                    j = RING * i + k
                    pool.wait_ge(y_ready, j + 1)
                    pool.nop(nofuse=True)
                    nc.gpsimd.indirect_dma_start(
                        out=x_out, out_offset=bass.IndirectOffsetOnAxis(ap=to_i[:, k:k + 1], axis=0),
                        in_=y[:, k, :], in_offset=None, bounds_check=tokens - 1,
                        oob_is_err=False).then_inc(y_stored[k], 16)

                tile_steps(pool, combine)
                for k in range(RING):
                    pool.wait_ge(y_stored[k], 16 * (N // RING))

            @block.scalar
            def _(act):
                act.preload_act_table(ACT.Exp)

                def transposed(i, k, first):
                    n = GR * i + k
                    for c in range(DC):
                        act.wait_ge(xT_ps_ready, DC * n + c + 1)
                        if c == 0 and not (first and k < 2):
                            act.wait_ge(gate_ready, 2 * (n - 1))
                        nc.scalar.activation(xT[:, k % 2, c, :], xT_ps[c][:], ACT.Copy).then_inc(xT_ready, 1)

                def copy_x(i, k, first):
                    n = GR * i + k
                    act.wait_ge(x_loaded[k], 16 * (i + 1))
                    if not first:
                        act.wait_ge(scattered[k], 16 * GT * i)
                    nc.scalar.activation(rows[:, k, :, 0:D], x[:, k], ACT.Copy).then_inc(x_copied, 1)

                def exps(i, k, first):
                    n = GR * i + k
                    for h in range(2):
                        act.wait_ge(top_ready, 2 * n + h + 1)
                        for t in range(2 * h, 2 * h + 2):
                            if not (first and k == 0):
                                act.wait_ge(exp_done, GT * (n - 1) + t + 1)
                            if not (first and k < 2) and t == 0:
                                act.wait_ge(route_step, ROUTE_STEPS * (n - 2) + 1)
                            nc.scalar.activation(junk[:, t, :], gate_ps[2 * (k % 2) + h][:, (t % 2) * D:(t % 2 + 1) * D], ACT.Exp,
                                                 bias=ntop[:, k % 2, t:t + 1],
                                                 accum_out=esum[:, k % 2, t:t + 1]).then_inc(exp_done, 1)

                def step(i, k, first, last):
                    if not (last and k == GR - 1):
                        to = at(i, k + 1)
                        transposed(*to, first and k < GR - 1)
                    copy_x(i, k, first)
                    exps(i, k, first)

                transposed(0, 0, True)
                gate_steps(act, step)

                def expert_out(i, k, first):
                    j = RING * i + k
                    act.wait_ge(pre_ready, j + 1)
                    if not (first and k < HALF):
                        act.wait_ge(y_ready, j - HALF + 1)
                    nc.scalar.activation(act_out[:, k % HALF, :], pre[:, k % HALF, :], ACT.Relu,
                                         scale=srow[:, k, D + 2:D + 3]).then_inc(act_ready, 1)

                def tile_transposed(i, k, first):
                    j = RING * i + k
                    act.wait_ge(sxT_ps_ready, j + 1)
                    if not (first and k < HALF):
                        act.wait_ge(product_ready, j - HALF + 1)
                    nc.scalar.activation(sxT[:, k % HALF], sxT_ps[k % HALF][:, 0:DC * P].rearrange("p (c t) -> p c t", c=DC),
                                         ACT.Copy).then_inc(sxT_ready, 1)

                def tile_step(i, k, first, last):
                    if not (last and k >= RING - 2):
                        tile_transposed(*tile_at(i, k + 2), first and k < RING - 2)
                    if not (first and k == 0):
                        expert_out(*tile_at(i - 1, k + RING - 1), first)

                for k in range(2):
                    tile_transposed(0, k, True)
                tile_steps(act, tile_step)
                expert_out(N // RING - 1, RING - 1, False)

            @block.vector
            def _(dve):
                dve.wait_ge(bg_loaded, 16)
                nc.vector.tensor_copy(bg3[:, 0, :], bg_row[:]).then_inc(bg_step, 1)
                dve.wait_ge(bg_step, 1)
                nc.vector.tensor_tensor(bg_rest[:, 0, :], bg_row[:], bg3[:, 0, :], ALU.subtract).then_inc(bg_step, 1)
                dve.wait_ge(bg_step, 2)
                nc.vector.tensor_copy(bg3[:, 1, :], bg_rest[:, 0, :]).then_inc(bg_step, 1)
                dve.wait_ge(bg_step, 3)
                nc.vector.tensor_tensor(bg_rest[:, 1, :], bg_rest[:, 0, :], bg3[:, 1, :], ALU.subtract).then_inc(bg_step, 1)
                dve.wait_ge(bg_step, 4)
                nc.vector.tensor_copy(bg3[:, 2, :], bg_rest[:, 1, :]).then_inc(bg_step, 1)

                def statistics(i, k, first):
                    n = GR * i + k
                    dve.wait_ge(x_loaded[k], 16 * (i + 1))
                    if not (first and k < 2):
                        dve.wait_ge(ln_aggr, n - 1)
                    for t in range(GT):
                        last = nc.vector.bn_stats(stats[:, k % 2, t, :], x[:, k, t, :])
                    last.then_inc(ln_stats, 1)
                    dve.wait_ge(ln_stats, n + 1)
                    if not first:
                        dve.wait_ge(rows_ready, n - GR + 1)
                    dve.nop(nofuse=True)
                    for t in range(GT):
                        last = nc.vector.bn_aggr(mv[:, k, t, :], stats[:, k % 2, t, :])
                    last.then_inc(ln_aggr, 1)

                def normalise(i, k, first):
                    n = GR * i + k
                    dve.wait_ge(ln_rstd, n + 1)
                    if not (first and k < 2):
                        dve.wait_ge(xT_ps_ready, DC * (n - 1))
                    for t in range(GT):
                        last = nc.vector.tensor_scalar(xn[:, k % 2, t, :], x[:, k, t, :], mv[:, k, t, 0:1],
                                                       mv[:, k, t, 1:2], ALU.subtract, ALU.mult)
                    last.then_inc(xn_ready, 1)

                def tops(i, k, first):
                    n = GR * i + k
                    for h in range(2):
                        logits = gate_ps[2 * (k % 2) + h]
                        pair = slice(2 * h, 2 * h + 2)
                        dve.wait_ge(gate_ready, 2 * n + h + 1)
                        if h == 0 and not (first and k < 2):
                            dve.wait_ge(exp_done, GT * (n - 1))
                            dve.wait_ge(onehot_ready, n - 1)
                        dve.nop(nofuse=True)
                        for t in range(2 * h, 2 * h + 2):
                            last = nc.vector.max(top[:, k % 2, t, :], logits[:, (t % 2) * D:(t % 2 + 1) * D])
                        last.then_inc(top_step, 1)
                        dve.wait_ge(top_step, 2 * n + h + 1)
                        dve.nop(nofuse=True)
                        nc.vector.tensor_scalar(ntop[:, k % 2, pair], top[:, k % 2, pair, 0], -1.0, None, ALU.mult)
                        for t in range(2 * h, 2 * h + 2):
                            last = nc.vector.max_index(top_at[:, k % 2, t, :], top[:, k % 2, t, :],
                                                       logits[:, (t % 2) * D:(t % 2 + 1) * D])
                        last.then_inc(top_ready, 1)

                def mark(i, k, first):
                    n = GR * i + k
                    step = MARK_STEPS * n
                    if not (first and k == 0):
                        dve.wait_ge(onehot_ready, n)
                    dve.wait_ge(top_ready, 2 * n + 2)
                    nc.vector.tensor_scalar(expert_i[:], top_at[:, k % 2, :, 0], E - 1, None, ALU.bitwise_and).then_inc(mark_step, 1)
                    dve.wait_ge(mark_step, step + 1)
                    nc.vector.tensor_copy(expert[:], expert_i[:]).then_inc(mark_step, 1)
                    dve.wait_ge(mark_step, step + 2)
                    if not (first and k < 2):
                        dve.wait_ge(rows_ready, n - 1)
                    nc.vector.tensor_tensor(onehot[:, k % 2], ids[:].unsqueeze(1).broadcast_to([P, GT, E]),
                                            expert[:].unsqueeze(2).broadcast_to([P, GT, E]), ALU.is_equal).then_inc(onehot_ready, 1)

                def route(i, k, first):
                    n = GR * i + k
                    step = ROUTE_STEPS * n
                    if not (first and k == 0):
                        dve.wait_ge(rows_ready, n)
                    dve.wait_ge(exp_done, GT * (n + 1))
                    nc.vector.reciprocal(prob[:], esum[:, k % 2, :]).then_inc(route_step, 1)
                    dve.wait_ge(rank_ready, n + 1)
                    counted = rank_ps[k % 2]
                    nc.vector.tensor_tensor(rank[:], counted[:, 0:GT * E].rearrange("p (t e) -> p t e", t=GT),
                                            base[:, k % 2, :].unsqueeze(1).broadcast_to([P, GT, E]),
                                            ALU.add).then_inc(route_step, 1)
                    nc.vector.tensor_tensor(base[:, 1 - k % 2, :], counted[:, GT * E:GT * E + E], base[:, k % 2, :],
                                            ALU.add).then_inc(route_step, 1)
                    dve.wait_ge(route_step, step + 2)
                    nc.vector.tensor_tensor(chosen[:], rank[:], onehot[:, k % 2], ALU.mult).then_inc(route_step, 1)
                    nc.vector.tensor_scalar(rows[:, k, :, D + 2], prob[:], 0.5, None, ALU.mult).then_inc(route_step, 1)
                    nc.vector.tensor_copy(rows[:, k, :, D + 3], token[:]).then_inc(route_step, 1)
                    dve.wait_ge(route_step, step + 4)
                    nc.vector.tensor_reduce(row_f[:], chosen[:], AX_X, ALU.add).then_inc(route_step, 1)
                    nc.vector.tensor_copy(rows[:, k, :, D:D + 2], mv[:, k])
                    dve.wait_ge(route_step, step + 6)
                    nc.vector.tensor_scalar(token[:], token[:], float(GT * P), None, ALU.add).then_inc(route_step, 1)
                    dve.wait_ge(route_step, step + 7)
                    nc.vector.tensor_copy(row_i[:, k, :], row_f[:]).then_inc(rows_ready, 1)

                def step(i, k, first, last):
                    if not (last and k >= GR - 2):
                        statistics(*at(i, k + 2), first and k < GR - 2)
                    if not (last and k == GR - 1):
                        normalise(*at(i, k + 1), first and k < GR - 1)
                    tops(i, k, first)
                    if not first:
                        dve.wait_ge(scattered[k], 16 * GT * i)
                    mark(i, k, first)
                    if not (first and k == 0):
                        route(*at(i - 1, k + GR - 1), first)

                for k in range(2):
                    statistics(0, k, True)
                normalise(0, 0, True)
                dve.wait_ge(made, 3)
                gate_steps(dve, step)
                route(groups // GR - 1, GR - 1, False)

                dve.wait_ge(rows_ready, groups)
                nc.vector.tensor_tensor(count[:], base[:, 0, :], start_f[:], ALU.subtract).then_inc(plan_step, 1)
                nc.vector.tensor_copy(start_i[:], base[:, 0, :]).then_inc(plan_ready, 1)
                dve.wait_ge(plan_step, 1)
                nc.vector.tensor_scalar(tiles_f[:], count[:], float(P - 1), None, ALU.add).then_inc(plan_step, 1)
                dve.wait_ge(plan_step, 2)
                nc.vector.tensor_copy(tiles_i[:], tiles_f[:]).then_inc(plan_step, 1)
                dve.wait_ge(plan_step, 3)
                nc.vector.tensor_scalar(tiles_i[:], tiles_i[:], 7, None, ALU.arith_shift_right).then_inc(plan_step, 1)
                dve.wait_ge(plan_step, 4)
                nc.vector.tensor_copy(tiles_f[:], tiles_i[:]).then_inc(plan_step, 1)
                dve.wait_ge(plan_step, 5)
                nc.vector.tensor_tensor_scan(ends[:], one8[:], tiles_f[:], 0.0, ALU.mult, ALU.add).then_inc(plan_step, 1)
                dve.wait_ge(plan_step, 6)
                nc.vector.tensor_tensor(past[:], tile_no[:].unsqueeze(2).broadcast_to([P, N, E]),
                                        ends[:].unsqueeze(1).broadcast_to([P, N, E]), ALU.is_ge).then_inc(plan_step, 1)
                dve.wait_ge(plan_step, 7)
                nc.vector.tensor_reduce(owner[:], past[:], AX_X, ALU.add)
                nc.vector.tensor_tensor(past_tiles[:], past[:], tiles_f[:].unsqueeze(1).broadcast_to([P, N, E]),
                                        ALU.mult).then_inc(plan_step, 1)
                dve.wait_ge(plan_step, 8)
                nc.vector.tensor_reduce(first_tile[:], past_tiles[:], AX_X, ALU.add)
                nc.vector.tensor_tensor(is_owner[:], ids[:].unsqueeze(1).broadcast_to([P, N, E]),
                                        owner[:].unsqueeze(2).broadcast_to([P, N, E]), ALU.is_equal)
                nc.vector.tensor_scalar(column_f[:], owner[:], float(E - 1), float(D), ALU.min, ALU.mult)
                nc.vector.tensor_scalar(at_f[:], owner[:], float(region), None, ALU.mult).then_inc(plan_step, 1)
                dve.wait_ge(plan_step, 9)
                nc.vector.tensor_tensor(local[:], tile_no[:], first_tile[:], ALU.subtract)
                nc.vector.tensor_tensor(owned[:], is_owner[:], count[:].unsqueeze(1).broadcast_to([P, N, E]), ALU.mult)
                nc.vector.tensor_copy(column_i[:], column_f[:]).then_inc(plan_step, 1)
                dve.wait_ge(plan_step, 10)
                nc.vector.tensor_reduce(owner_count[:], owned[:], AX_X, ALU.add)
                nc.vector.tensor_scalar(lane_no[:], local[:], float(P), lane[:, 0:1], ALU.mult, ALU.add)
                nc.vector.scalar_tensor_tensor(at_f[:], local[:], float(P), at_f[:], ALU.mult, ALU.add).then_inc(plan_step, 1)
                dve.wait_ge(plan_step, 11)
                nc.vector.tensor_scalar(at_f[:], at_f[:], float(spare), None, ALU.min)
                nc.vector.tensor_tensor(skip[:], lane_no[:], owner_count[:], ALU.is_ge).then_inc(plan_step, 1)
                dve.wait_ge(plan_step, 12)
                nc.vector.tensor_scalar(skip[:], skip[:], float(2 * tokens), None, ALU.mult)
                nc.vector.tensor_copy(at_i[:], at_f[:]).then_inc(plan_ready, 1)
                dve.wait_ge(plan_ready, 2)

                def tile_norm(i, k, first):
                    j = RING * i + k
                    dve.wait_ge(srow_loaded[k], 16 * (i + 1))
                    if not (first and k < HALF):
                        dve.wait_ge(sxT_ps_ready, j - HALF + 1)
                    nc.vector.tensor_scalar(sxn[:, k % HALF, :], srow[:, k, 0:D], srow[:, k, D:D + 1],
                                            srow[:, k, D + 1:D + 2], ALU.subtract, ALU.mult).then_inc(sxn_ready, 1)

                def add_bias(i, k, first):
                    j = RING * i + k
                    column = dve.value_load(column_i[0:1, bass.ds(j, 1)], min_val=0, max_val=(E - 1) * D)
                    dve.wait_ge(product_ready, j + 1)
                    if not (first and k < HALF):
                        dve.wait_ge(act_ready, j - HALF + 1)
                    nc.vector.tensor_tensor(pre[:, k % HALF, :], product_ps[k % HALF][:, 0:D], beb[:, bass.ds(column, D)],
                                            ALU.add).then_inc(pre_ready, 1)

                def add_x(i, k):
                    j = RING * i + k
                    nc.vector.tensor_tensor(to_i[:, k:k + 1], srow[:, k, D + 3:D + 4], skip[:, bass.ds(j, 1)], ALU.add)
                    dve.wait_ge(act_ready, j + 1)
                    nc.vector.tensor_tensor(y[:, k, :], act_out[:, k % HALF, :], srow[:, k, 0:D], ALU.add).then_inc(y_ready, 1)

                def tile_step(i, k, first, last):
                    if not (last and k >= RING - 3):
                        tile_norm(*tile_at(i, k + 3), first and k < RING - 3)
                    if not first:
                        dve.wait_ge(y_stored[k], 16 * i)
                    add_bias(i, k, first)
                    if not (first and k < 2):
                        add_x(*tile_at(i - 1, k + RING - 2))

                dve.wait_ge(we_loaded, 16 * (DC + 1))
                for k in range(3):
                    tile_norm(0, k, True)
                tile_steps(dve, tile_step)
                for k in range(RING - 2, RING):
                    add_x(N // RING - 1, k)

            @block.tensor
            def _(pe):
                ident = const["ident"]

                def transposes(i, k, first):
                    n = GR * i + k
                    pe.wait_ge(xn_ready, n + 1)
                    for c in range(DC):
                        if not (first and k == 0):
                            pe.wait_ge(xT_ready, DC * (n - 1) + c + 1)
                        for t in range(GT):
                            last = nc.tensor.transpose(xT_ps[c][:, t * P:(t + 1) * P], xn[:, k % 2, t, c * P:(c + 1) * P], ident[:])
                        last.then_inc(xT_ps_ready, 1)

                def gate(i, k, first):
                    n = GR * i + k
                    pe.wait_ge(xT_ready, DC * (n + 1))
                    for h in range(2):
                        logits = gate_ps[2 * (k % 2) + h]
                        if not (first and k < 2):
                            pe.wait_ge(exp_done, GT * (n - 2) + 2 * h + 2)
                        nc.tensor.matmul(logits[:], ones[0:3, :], bg_rows[:].unsqueeze(1).broadcast_to([3, 2, D]),
                                         start=True, stop=False, skip_group_check=True)
                        for t in range(2 * h, 2 * h + 2):
                            out = logits[:, (t % 2) * D:(t % 2 + 1) * D]
                            for c in range(DC):
                                last = nc.tensor.matmul(out, xT[:, k % 2, c, t * P:(t + 1) * P], wg[:, c, :], start=False,
                                                        stop=c == DC - 1, skip_group_check=True)
                        last.then_inc(gate_ready, 1)

                def ranks(i, k, first):
                    n = GR * i + k
                    pe.wait_ge(onehot_ready, n + 1)
                    if not (first and k < 2):
                        pe.wait_ge(rows_ready, n - 1)
                    for t in range(GT + 1):
                        out = rank_ps[k % 2][:, t * E:(t + 1) * E]
                        for s in range(t):
                            last = nc.tensor.matmul(out, ones[:], onehot[:, k % 2, s, :], start=s == 0, stop=t == GT and s == t - 1)
                        if t < GT:
                            nc.tensor.matmul(out, before[:], onehot[:, k % 2, t, :], start=t == 0, stop=True)
                    last.then_inc(rank_ready, 1)

                def step(i, k, first, last):
                    gate(i, k, first)
                    if not (last and k == GR - 1):
                        transposes(*at(i, k + 1), False)
                    if not (first and k == 0):
                        ranks(*at(i - 1, k + GR - 1), first)

                transposes(0, 0, True)
                pe.wait_ge(w_loaded, 16)
                pe.wait_ge(made, 2)
                pe.wait_ge(bg_placed, 16 * 3)
                gate_steps(pe, step)
                ranks(groups // GR - 1, GR - 1, False)

                pe.wait_ge(plan_ready, 2)
                pe.wait_ge(we_loaded, 16 * (DC + 1))

                def tile_transposes(i, k, first):
                    j = RING * i + k
                    pe.wait_ge(sxn_ready, j + 1)
                    if not (first and k < HALF):
                        pe.wait_ge(sxT_ready, j - HALF + 1)
                    for c in range(DC):
                        last = nc.tensor.transpose(sxT_ps[k % HALF][:, c * P:(c + 1) * P], sxn[:, k % HALF, c * P:(c + 1) * P], ident[:])
                    last.then_inc(sxT_ps_ready, 1)

                def product(i, k, first):
                    j = RING * i + k
                    column = pe.value_load(column_i[0:1, bass.ds(j, 1)], min_val=0, max_val=(E - 1) * D)
                    pe.wait_ge(sxT_ready, j + 1)
                    if not (first and k < HALF):
                        pe.wait_ge(pre_ready, j - HALF + 1)
                    for c in range(DC):
                        last = nc.tensor.matmul(product_ps[k % HALF][:, 0:D], sxT[:, k % HALF, c, :], we[:, c, bass.ds(column, D)],
                                                start=c == 0, stop=c == DC - 1)
                    last.then_inc(product_ready, 1)

                def tile_step(i, k, first, last):
                    if not (last and k >= RING - 2):
                        tile_transposes(*tile_at(i, k + 2), first and k < RING - 2)
                    product(i, k, first)

                for k in range(2):
                    tile_transposes(0, k, True)
                tile_steps(pe, tile_step)


def attention_phase(nc, psum, const, x_in, x_out, W, rope_table, scratch):
    NB = x_in.shape[0] // T
    xv = x_in.rearrange("(b t p) d -> b p t d", p=P, t=TT)
    ov = x_out.rearrange("(b t p) d -> b p t d", p=P, t=TT)
    ctx = ExitStack()
    with ctx:
        def sb(n, shape, dt=F32):
            return ctx.enter_context(nc.sbuf_tensor(f"at_{n}", shape, dt))

        def sem(n):
            return ctx.enter_context(nc.semaphore(f"at_{n}"))

        w_down = sb("w_down", [P, DC, C])
        w_q = sb("w_q", [P, DC, D])
        w_qr = sb("w_qr", [P, DC, 2 * R])
        w_ku = sb("w_ku", [P, D])
        w_kr = sb("w_kr", [P, 2 * R])
        w_vu = sb("w_vu", [P, D])
        w_o = sb("w_o", [P, NG // 2, D])
        rope = sb("rope", [2 * R, T])
        maskq = sb("maskq", [P, P], BF16)
        maskk = sb("maskk", [P, P], BF16)
        x = sb("x", [P, TT, D])
        stats = sb("stats", [P, TT, 6])
        mv = sb("mv", [P, TT, 2])
        veps = sb("veps", [P, TT])
        power = sb("power", [P, TT])
        rstd = sb("rstd", [P, TT])
        xn = sb("xn", [P, TT, D])
        xT = sb("xT", [P, DC, T])
        ckvT = sb("ckvT", [P, T])
        q2 = sb("q2", [P, DC, 2, T], F16)
        k_hi = sb("k_hi", [P, DC, T], F16)
        k_lo = sb("k_lo", [P, DC, T], F16)
        turned = sb("turned", [R, 2, T])
        rot = sb("rot", [R, 2, T])
        rot_q = sb("rot_q", [2 * R, T], F16)
        rot_k_hi = sb("rot_k_hi", [2 * R, T], F16)
        rot_k_lo = sb("rot_k_lo", [2 * R, T], F16)
        v = sb("v", [P, TT, NH, 2 * HD])
        qs = sb("qs", [KC + 1, NH, T], F16)
        ks_hi = sb("ks_hi", [KC + 1, NH, T], F16)
        ks_lo = sb("ks_lo", [KC, NH, T], F16)
        nmax = sb("nmax", [P, 2, GH, TT])
        nmaxT = sb("nmaxT", [GH * TT, P], F16)
        K_OFF = [0, T, T + 3 * P + P, T + 3 * P]
        K_N = [T - P * j for j in range(TT)]
        probs = sb("probs", [P, 2, GH, sum(K_N)])
        o_T = sb("o_T", [P, T // 32, 32])
        inv_sum = sb("inv_sum", [P, T // 32])
        on_T = sb("on_T", [P, T // 32, 32])
        o_n = sb("o_n", [P, NG // 2, T])
        res = sb("res", [P, TT, D])

        SC = psum[0:3]
        MX = psum[3:5]
        O = psum[5]
        PJ = psum[6:8]

        w_loaded = sem("w_loaded")
        zeroed = sem("zeroed")
        ones_set = sem("ones_set")
        x_loaded = sem("x_loaded")
        res_loaded = sem("res_loaded")
        ln_stats = sem("ln_stats")
        ln_aggr = sem("ln_aggr")
        var_eps = sem("var_eps")
        ln_rstd = sem("ln_rstd")
        xn_ready = sem("xn_ready")
        pj_ready = [sem("pj_ready0"), sem("pj_ready1")]
        pj_free = [sem("pj_free0"), sem("pj_free1")]
        hi_ready = sem("hi_ready")
        rot_ready = sem("rot_ready")
        rot_parted = sem("rot_parted")
        rot_hi_ready = sem("rot_hi_ready")
        hi_written = sem("hi_written")
        lo_written = sem("lo_written")
        stack_loaded = [sem(f"stack_loaded{g}") for g in range(NG)]
        rope_loaded = [sem(f"rope_loaded{g}") for g in range(NG)]
        mx_ready = sem("mx_ready")
        mx_free = sem("mx_free")
        nmax_written = sem("nmax_written")
        score_loaded = [sem(f"score_loaded{g}") for g in range(NG)]
        sc_ready = sem("sc_ready")
        probs_ready = sem("probs_ready")
        o_ready = sem("o_ready")
        o_free = sem("o_free")
        norm_step = sem("norm_step")
        on_ready = sem("on_ready")
        y_stored = sem("y_stored")

        U_XT, U_CKV, U_QR, U_KR, U_Q, U_K, U_V = (0, 1), 2, 3, 5, (4, 6), (7, 8), (9, 10)
        N_SC = 3 * NH
        N_MX = 12 * NG
        N_O = NG + 2
        N_PJ = (6, 5)
        N_ROT = 3
        N_HI = 3
        N_LO = 2
        N_STACK = 2
        N_SCORE = 2
        N_ROPE = 3
        STEP_UNITS = {0: (0, 1), 1: (2,), 2: (3, 4), 3: (5, 6), 4: (7, 8)}
        OUTPUT_STEPS = (2, 3)

        def pj(b, u):
            return u % 2, N_PJ[u % 2] * b + u // 2

        def wait_out(eng, b, u):
            bank, before = pj(b, u)
            eng.wait_ge(pj_free[bank], before + 1)

        with nc.Block() as block:
            @block.sync
            def _(sp):
                sp.dma_start(x[:], xv[0]).then_inc(x_loaded, 16)
                for dst, src in ((w_down[:], W["kv_down"].rearrange("(c p) n -> p c n", p=P)),
                                 (w_q[:], W["q"].rearrange("(c p) n -> p c n", p=P)),
                                 (w_qr[:, :, 0:R], W["q_rope"].rearrange("(c p) n -> p c n", p=P)),
                                 (w_qr[:, :, R:R + R // 2], W["q_rope"].rearrange("(c p) n -> p c n", p=P)[:, :, R // 2:R]),
                                 (w_qr[:, :, R + R // 2:2 * R], W["q_rope"].rearrange("(c p) n -> p c n", p=P)[:, :, 0:R // 2]),
                                 (w_ku[:], W["k_up"]), (w_vu[:], W["v_up"]),
                                 (w_kr[:, 0:R], W["k_rope"]),
                                 (w_kr[:, R:R + R // 2], W["k_rope"][:, R // 2:R]),
                                 (w_kr[:, R + R // 2:2 * R], W["k_rope"][:, 0:R // 2]),
                                 (rope[:], rope_table)):
                    sp.dma_start(dst, src).then_inc(w_loaded, 16)
                wo = W["o"].rearrange("(c s h d) n -> s h d c n", c=NG // 2, s=2, h=GH)
                for s in range(2):
                    for hq in range(GH):
                        at = 32 * hq + HD * s
                        sp.dma_start(w_o[at:at + HD, :, :], wo[s, hq]).then_inc(w_loaded, 16)

                def load_x(b):
                    sp.wait_ge(xn_ready, b)
                    sp.nop(nofuse=True)
                    sp.dma_start(x[:], xv[b]).then_inc(x_loaded, 16)

                def write_scratch(b):
                    for u in U_Q:
                        wait_out(sp, b, u)
                        sp.nop(nofuse=True)
                    sp.dma_start(scratch["q"][b].rearrange("(c p) s n -> p c (s n)", p=P),
                                 q2[:].rearrange("p c s n -> p c (s n)")).then_inc(hi_written, 16)
                    for u in U_K:
                        wait_out(sp, b, u)
                        sp.nop(nofuse=True)
                    for key, part, written in (("k_hi", k_hi, hi_written), ("k_lo", k_lo, lo_written)):
                        for s in range(2):
                            sp.dma_start(scratch[key][b].rearrange("(c p) s n -> p c s n", p=P)[:, :, s, :],
                                         part[:]).then_inc(written, 16)

                def load_stack(b, g, first):
                    if g == 0:
                        sp.wait_ge(hi_written, 16 * N_HI * (b + 1))
                        sp.nop(nofuse=True)
                    if not first:
                        sp.wait_ge(sc_ready, N_SC * (b - 1) + 3 * GH * (g + 1))
                        sp.nop(nofuse=True)
                    slots = slice(g * GH, (g + 1) * GH)
                    for dst, key, loaded in ((qs, "q", stack_loaded), (ks_hi, "k_hi", stack_loaded), (ks_lo, "k_lo", score_loaded)):
                        if key == "k_lo" and g == 0:
                            sp.wait_ge(lo_written, 16 * N_LO * (b + 1))
                            sp.nop(nofuse=True)
                        src = scratch[key][b].rearrange("(h r) s n -> (r s) h n", r=HD)
                        sp.dma_start(dst[0:HR, slots, :], src[:, slots, :]).then_inc(loaded[g], 16)

                def load_max(b, g):
                    sp.wait_ge(mx_free, N_MX * b + 12 * (g + 1))
                    sp.nop(nofuse=True)
                    row = scratch["nmax"][b, g]
                    sp.dma_start(row.rearrange("(s q) -> s q", q=P), nmaxT[:]).then_inc(nmax_written, 16)
                    sp.wait_ge(nmax_written, 16 * (NG * b + g + 1))
                    sp.nop(nofuse=True)
                    sp.dma_start(qs[ROW_MAX:ROW_MAX + 1, g * GH:(g + 1) * GH, :],
                                 row.rearrange("(o h t) -> o h t", o=1, t=T)).then_inc(score_loaded[g], 16)

                def store(b):
                    sp.wait_ge(o_free, N_O * (b + 1))
                    sp.nop(nofuse=True)
                    sp.dma_start(ov[b], res[:]).then_inc(y_stored, 16)

                def body(b, first, rest):
                    load_stack(b, 3, first)
                    load_max(b, 1)
                    if rest >= 2:
                        load_x(b + 2)
                    if not first:
                        store(b - 1)
                    load_max(b, 2)
                    if rest:
                        write_scratch(b + 1)
                    if not first:
                        sp.wait_ge(y_stored, 16 * b)
                        sp.nop(nofuse=True)
                    sp.dma_start(res[:], xv[b]).then_inc(res_loaded, 16)
                    if rest:
                        load_stack(b + 1, 0, False)
                    load_max(b, 3)
                    if rest:
                        load_stack(b + 1, 1, False)
                        load_max(b + 1, 0)
                        load_stack(b + 1, 2, False)

                load_x(1)
                write_scratch(0)
                for g in range(3):
                    load_stack(0, g, True)
                load_max(0, 0)
                body(0, True, 2)
                with sp.Fori(1, NB - 2) as b:
                    body(b, False, 2)
                body(NB - 2, False, 1)
                body(NB - 1, False, 0)
                store(NB - 1)
                sp.wait_ge(y_stored, 16 * NB)
                sp.nop(nofuse=True)

            @block.gpsimd
            def _(pool):
                nc.gpsimd.memset(power[:], -0.5).then_inc(var_eps, 1)
                nc.gpsimd.memset(maskq[:], 0.0)
                nc.gpsimd.memset(maskk[:], 0.0).then_inc(zeroed, 1)
                pool.wait_ge(zeroed, 1)
                nc.gpsimd.affine_select(out=maskq[:], in_=maskq[:], compare_op=ALU.is_ge, fill=MASKED,
                                        base=0, pattern=[[-1, P]], channel_multiplier=1)
                nc.gpsimd.affine_select(out=maskk[:], in_=maskk[:], compare_op=ALU.is_ge, fill=MASKED,
                                        base=0, pattern=[[1, P]], channel_multiplier=-1).then_inc(zeroed, 1)

                def ln(b):
                    pool.wait_ge(ln_aggr, b + 1)
                    pool.nop(nofuse=True)
                    nc.gpsimd.tensor_scalar(veps[:], mv[:, :, 1], EPS, None, ALU.add).then_inc(var_eps, 1)
                    pool.wait_ge(var_eps, b + 2)
                    nc.gpsimd.tensor_tensor(rstd[:], veps[:], power[:], ALU.pow).then_inc(ln_rstd, 1)

                def part_rotary(b):
                    pool.wait_ge(rot_hi_ready, 3 * b + 1)
                    pool.nop(nofuse=True)
                    nc.gpsimd.tensor_tensor(rot_q[R:2 * R, :], rot[:, 0, :], rot_q[0:R, :], ALU.subtract).then_inc(rot_parted, 1)
                    pool.wait_ge(rot_hi_ready, 3 * b + 3)
                    pool.nop(nofuse=True)
                    for half in range(2):
                        nc.gpsimd.tensor_tensor(rot_k_lo[half * R:(half + 1) * R, :], rot[:, 1, :], rot_k_hi[0:R, :],
                                                ALU.subtract).then_inc(rot_parted, 1)
                    pool.wait_ge(rot_parted, N_ROT * (b + 1))
                    pool.nop(nofuse=True)

                def load_rope(b, g, first):
                    if not first:
                        pool.wait_ge(sc_ready, N_SC * (b - 1) + 3 * GH * (g + 1))
                        pool.nop(nofuse=True)
                    for dst, r in ((qs, rot_q), (ks_hi, rot_k_hi), (ks_lo, rot_k_lo)):
                        pool.dma_start(dst[HR:KC, g * GH:(g + 1) * GH, :],
                                       r[:].unsqueeze(1).broadcast_to([2 * R, GH, T])).then_inc(rope_loaded[g], 16)

                ln(0)
                part_rotary(0)
                for g in range(3):
                    load_rope(0, g, True)
                ln(1)
                load_rope(0, 3, True)
                with pool.Fori(0, NB - 2) as b:
                    part_rotary(b + 1)
                    for g in range(3):
                        load_rope(b + 1, g, False)
                        if g == 1:
                            ln(b + 2)
                    load_rope(b + 1, 3, False)
                part_rotary(NB - 1)
                for g in range(NG):
                    load_rope(NB - 1, g, False)

            @block.vector
            def _(dve):
                def ln_statistics(b):
                    dve.wait_ge(x_loaded, 16 * (b + 1))
                    for t in range(TT):
                        last = nc.vector.bn_stats(stats[:, t, :], x[:, t, :])
                    last.then_inc(ln_stats, 1)
                    dve.wait_ge(ln_stats, b + 1)
                    dve.nop(nofuse=True)
                    for t in range(TT):
                        last = nc.vector.bn_aggr(mv[:, t, :], stats[:, t, :])
                    last.then_inc(ln_aggr, 1)

                def ln_apply(b, first):
                    dve.wait_ge(ln_rstd, b + 1)
                    if not first:
                        dve.wait_ge(pj_ready[1], pj(b - 1, U_XT[1])[1] + 1)
                    for t in range(TT):
                        last = nc.vector.tensor_scalar(xn[:, t, :], x[:, t, :], mv[:, t, 0:1], rstd[:, t:t + 1],
                                                       ALU.subtract, ALU.mult)
                    last.then_inc(xn_ready, 1)

                def rotate(b, s, first):
                    bank, before = pj(b, (U_QR, U_KR)[s])
                    dve.wait_ge(pj_ready[bank], before + 1)
                    if not first:
                        dve.wait_ge(rot_parted, N_ROT * b)
                    if not (first and s == 0):
                        dve.wait_ge(rot_ready, 2 * b + s)
                    nc.vector.tensor_tensor(turned[:, 0, :], PJ[bank][0:R, :], rope[0:R, :], ALU.mult)
                    nc.vector.tensor_tensor(turned[:, 1, :], PJ[bank][R:2 * R, :], rope[R:2 * R, :],
                                            ALU.mult).then_inc(pj_free[bank], 1)
                    dve.wait_ge(pj_free[bank], before + 1)
                    nc.vector.tensor_tensor(rot[:, s, :], turned[:, 0, :], turned[:, 1, :], ALU.add).then_inc(rot_ready, 1)

                def second_part(b, u, first):
                    bank, before = pj(b, u)
                    n = (U_Q + U_K).index(u)
                    dve.wait_ge(hi_ready, 4 * b + n + 1)
                    if not first and n in (0, 2):
                        dve.wait_ge(*((hi_written, 16 * N_HI * b), (lo_written, 16 * N_LO * b))[n // 2])
                    if n < 2:
                        hi, lo = q2[:, n, 0, :], q2[:, n, 1, :]
                    else:
                        hi, lo = k_hi[:, n - 2, :], k_lo[:, n - 2, :]
                    nc.vector.tensor_tensor(lo, PJ[bank][:], hi, ALU.subtract).then_inc(pj_free[bank], 1)

                def maximum(b, g, j, first):
                    use = N_MX * b + 12 * g + j
                    bank = MX[j % 2]
                    dve.wait_ge(mx_ready, use + 1)
                    to = nmax[:, g % 2]
                    if j == -1:
                        if not (first and g <= 1):
                            dve.wait_ge(nmax_written, 16 * (NG * b + g - 1))
                        ins = nc.vector.tensor_copy(nmaxT[:], bank[0:GH * TT, 0:P])
                    elif j == 0:
                        ins = nc.vector.tensor_reduce(to[:, :, 0], bank[:].rearrange("p (h k) -> p h k", h=GH),
                                                      AX_X, ALU.max, negate=True)
                    elif j < 3:
                        h = 2 * (j - 1)
                        ins = nc.vector.tensor_reduce(to[:, h:h + 2, 1], bank[:].rearrange("p (h k) -> p h k", h=2),
                                                      AX_X, ALU.max, negate=True)
                    elif j < 7:
                        ins = nc.vector.tensor_reduce(to[:, j - 3, 2:3], bank[:, 0:3 * P], AX_X, ALU.max, negate=True)
                    else:
                        ins = nc.vector.tensor_reduce(to[:, j - 7, 3:4], bank[:], AX_X, ALU.max, negate=True)
                    ins.then_inc(mx_free, 1)

                def untangle(b, g, first=False):
                    count = N_O * b + g
                    if not (first and g == 0):
                        dve.wait_ge(norm_step, 2 * (NG * b + g))
                    dve.wait_ge(o_ready, count + 1)
                    dve.nop(nofuse=True)
                    nc.vector.transpose(o_T[:].rearrange("p j r -> p (j r)"), O[:]).then_inc(o_free, 1)

                def normalise(b, g, first=False):
                    step = 2 * (NG * b + g)
                    half = g % 2
                    dve.wait_ge(o_free, N_O * b + g + 1)
                    nc.vector.reciprocal(inv_sum[:], o_T[:, :, HD]).then_inc(norm_step, 1)
                    dve.wait_ge(norm_step, step + 1)
                    if not half and not (first and g == 0):
                        dve.wait_ge(on_ready, 2 * b + g // 2)
                    nc.vector.tensor_tensor(on_T[:, :, half * HD:(half + 1) * HD], o_T[:, :, 0:HD],
                                            inv_sum[:].unsqueeze(2).broadcast_to([P, T // 32, HD]),
                                            ALU.mult).then_inc(norm_step, 1)

                def turn_back(b, g):
                    dve.wait_ge(norm_step, 2 * (NG * b + g) + 2)
                    dve.nop(nofuse=True)
                    nc.vector.transpose(o_n[:, g // 2, :], on_T[:].rearrange("p j r -> p (j r)")).then_inc(on_ready, 1)

                def output(b, half):
                    dve.wait_ge(res_loaded, 16 * (b + 1))
                    dve.wait_ge(o_ready, N_O * b + NG + half + 1)
                    nc.vector.tensor_tensor(res[:, 2 * half:2 * half + 2, :],
                                            O[:].rearrange("p (t d) -> p t d", t=2),
                                            res[:, 2 * half:2 * half + 2, :], ALU.add).then_inc(o_free, 1)

                def body(b, first, rest):
                    def others(s):
                        g, hq = s // GH, s % GH
                        todo = []
                        if s - 1 in OUTPUT_STEPS and not first:
                            todo = [lambda: output(b - 1, OUTPUT_STEPS.index(s - 1))]
                        if hq == 1 and not (first and g == 0):
                            at, start = ((b, g - 1), first) if g else ((b - 1, NG - 1), False)
                            todo = [lambda: untangle(*at, start), lambda: normalise(*at, start)]
                            if at[1] % 2:
                                todo.append(lambda: turn_back(*at))
                        if rest:
                            for u in STEP_UNITS.get(s - 1, ()):
                                if u in (U_QR, U_KR):
                                    todo.append(lambda u=u: rotate(b + 1, (U_QR, U_KR).index(u), False))
                        if rest >= 2 and s == 10:
                            todo.append(lambda: ln_statistics(b + 2))
                        if rest >= 2 and s == 12:
                            todo.append(lambda: ln_apply(b + 2, False))
                        return todo

                    for s in range(NH):
                        g, hq = s // GH, s % GH
                        todo = others(s)
                        mb, mg = (b, g + 2) if g < 2 else (b + 1, g - 2)
                        for unit in range(3 * hq - 1, 3 * hq + 2):
                            if g < 2 or rest or s == 2 * GH and unit == -1:
                                maximum(mb, mg, unit, False)
                            if todo:
                                todo.pop(0)()
                        for work in todo:
                            work()
                        if rest:
                            for u in STEP_UNITS.get(s, ()):
                                if u in U_Q + U_K:
                                    second_part(b + 1, u, False)

                nc.vector.memset(v[:], 1.0)
                nc.vector.memset(ks_hi[ROW_MAX:ROW_MAX + 1, :, :], 1.0).then_inc(ones_set, 1)
                ln_statistics(0)
                ln_apply(0, True)
                dve.wait_ge(w_loaded, 16 * (11 + 2 * GH))
                for u in range(3, 9):
                    if u in (U_QR, U_KR):
                        rotate(0, (U_QR, U_KR).index(u), True)
                    else:
                        second_part(0, u, True)
                ln_statistics(1)
                ln_apply(1, False)
                for g in range(2):
                    for j in range(-1, 11):
                        if g or j >= 0:
                            maximum(0, g, j, True)
                body(0, True, 2)
                with dve.Fori(1, NB - 2) as b:
                    body(b, False, 2)
                body(NB - 2, False, 1)
                body(NB - 1, False, 0)
                untangle(NB - 1, NG - 1)
                normalise(NB - 1, NG - 1)
                turn_back(NB - 1, NG - 1)
                for half in range(2):
                    output(NB - 1, half)

            @block.scalar
            def _(act):
                act.preload_act_table(ACT.Exp)

                def copy_out(b, u, first):
                    bank, before = pj(b, u)
                    act.wait_ge(pj_ready[bank], before + 1)
                    src, done = PJ[bank], (pj_free[bank], 1)
                    if u in U_XT:
                        if u == U_XT[0] and not first:
                            act.wait_ge(pj_ready[0], pj(b - 1, U_Q[1])[1] + 1)
                            act.wait_ge(pj_ready[1], pj(b - 1, U_QR)[1] + 1)
                        dst = xT[:, u, :]
                    elif u == U_CKV:
                        if not first:
                            act.wait_ge(pj_ready[1], pj(b - 1, U_V[0])[1] + 1)
                        dst = ckvT[:]
                    elif u in U_Q + U_K:
                        if u == U_Q[0] and not first:
                            act.wait_ge(hi_written, 16 * N_HI * b)
                        dst = q2[:, U_Q.index(u), 0, :] if u in U_Q else k_hi[:, U_K.index(u), :]
                        done = (hi_ready, 1)
                    else:
                        if u == U_V[0]:
                            if first:
                                act.wait_ge(ones_set, 1)
                            else:
                                act.wait_ge(o_ready, N_O * (b - 1) + NG)
                        t = 2 * (u - U_V[0])
                        dst = v[:, t:t + 2, :, 0:HD]
                        src = src.rearrange("p (t h d) -> p t h d", t=2, h=NH)
                    nc.scalar.activation(dst, src if u in U_V else src[:], ACT.Copy).then_inc(*done)

                def first_rotary_parts(b, s, first):
                    if s == 0 and not first:
                        for g in range(NG):
                            act.wait_ge(rope_loaded[g], 16 * N_ROPE * b)
                    act.wait_ge(rot_ready, 2 * b + s + 1)
                    for dst in ((rot_q[0:R, :],), (rot_k_hi[0:R, :], rot_k_hi[R:2 * R, :]))[s]:
                        nc.scalar.activation(dst, rot[:, s, :], ACT.Copy).then_inc(rot_hi_ready, 1)

                def exps(b, g, hq, first):
                    if hq == 0 and not (first and g < 2):
                        before = N_O * b + g - 2 if g >= 2 else N_O * (b - 1) + g + 2
                        act.wait_ge(o_ready, before + 1)
                    h = GH * g + hq
                    for j in range(3):
                        act.wait_ge(sc_ready, N_SC * b + 3 * h + j + 1)
                        n = K_N[2] if j == 2 else T
                        at = j * T
                        nc.scalar.activation(probs[:, g % 2, hq, at:at + n], SC[j][:, 0:n], ACT.Exp,
                                             scale=SCALE).then_inc(probs_ready, 1)

                def body(b, first, rest):
                    for s in range(NH):
                        exps(b, s // GH, s % GH, first)
                        if s == 0:
                            for u in U_V:
                                copy_out(b, u, first)
                        if rest:
                            for u in STEP_UNITS.get(s, ()):
                                if u not in (U_QR, U_KR):
                                    copy_out(b + 1, u, False)
                            for u in STEP_UNITS.get(s - 1, ()):
                                if u in (U_QR, U_KR):
                                    first_rotary_parts(b + 1, (U_QR, U_KR).index(u), False)

                for u in range(9):
                    if u in (U_QR, U_KR):
                        first_rotary_parts(0, (U_QR, U_KR).index(u), True)
                    else:
                        copy_out(0, u, True)
                body(0, True, 2)
                with act.Fori(1, NB - 2) as b:
                    body(b, False, 2)
                body(NB - 2, False, 1)
                body(NB - 1, False, 0)

            @block.tensor
            def _(pe):
                pe.wait_ge(w_loaded, 16 * (11 + 2 * GH))
                pe.wait_ge(zeroed, 2)
                ident, identb = const["ident"], const["identb"]

                def project(b, u, first):
                    bank, before = pj(b, u)
                    if not (first and u < 2):
                        pe.wait_ge(pj_free[bank], before)
                    out = PJ[bank]
                    if u in U_XT:
                        if u == U_XT[0]:
                            pe.wait_ge(xn_ready, b + 1)
                        for t in range(TT):
                            last = nc.tensor.transpose(out[:, t * P:(t + 1) * P], xn[:, t, u * P:(u + 1) * P], ident[:])
                    elif u in (U_CKV, U_QR, *U_Q):
                        if u == U_CKV:
                            for before_u in U_XT:
                                wait_out(pe, b, before_u)
                        for c in range(DC):
                            lhsT = {U_CKV: w_down[:, c, :], U_Q[0]: w_q[:, c, 0:P], U_Q[1]: w_q[:, c, P:2 * P],
                                    U_QR: w_qr[:, c, :]}[u]
                            last = nc.tensor.matmul(out[0:lhsT.shape[-1], :], lhsT, xT[:, c, :], start=c == 0, stop=c == DC - 1)
                    elif u in (U_KR, *U_K):
                        if u == U_KR:
                            wait_out(pe, b, U_CKV)
                        lhsT = {U_K[0]: w_ku[:, 0:P], U_K[1]: w_ku[:, P:2 * P], U_KR: w_kr[:]}[u]
                        last = nc.tensor.matmul(out[0:lhsT.shape[-1], :], lhsT, ckvT[:], start=True, stop=True)
                    else:
                        for k in range(2):
                            t = 2 * (u - U_V[0]) + k
                            last = nc.tensor.matmul(out[:, k * D:(k + 1) * D], ckvT[:, t * P:(t + 1) * P], w_vu[:],
                                                    start=True, stop=True)
                    last.then_inc(pj_ready[bank], 1)

                def stacked(b, g):
                    pe.wait_ge(stack_loaded[g], 16 * N_STACK * (b + 1))
                    pe.wait_ge(rope_loaded[g], 16 * N_ROPE * (b + 1))

                def maximum(b, g, j, first):
                    use = N_MX * b + 12 * g + j
                    out = MX[j % 2]
                    if not (first and g == 0 and j < 2):
                        pe.wait_ge(mx_free, use if j == -1 else use - 1)
                    if j == -1:
                        last = nc.tensor.transpose(out[0:GH * TT, 0:P],
                                                   nmax[:, (g - 1) % 2].rearrange("p h i -> p (h i)"), ident[:])
                    else:
                        if j == 0:
                            i, heads = 0, range(GH)
                        elif j < 3:
                            i, heads = 1, range(2 * (j - 1), 2 * j)
                        elif j < 7:
                            i, heads = 2, (j - 3,)
                        else:
                            i, heads = 3, (j - 7,)
                        n = P * (i + 1)
                        for k, hq in enumerate(heads):
                            slot = GH * g + hq
                            nc.tensor.matmul(out[:, k * n:(k + 1) * n], qs[0:KC, slot, i * P:(i + 1) * P],
                                             ks_hi[0:KC, slot, 0:n], start=True, stop=False)
                            last = nc.tensor.matmul(out[:, (k + 1) * n - P:(k + 1) * n], identb[:], maskq[:],
                                                    start=False, stop=True)
                    last.then_inc(mx_ready, 1)

                def score(b, slot, j, first):
                    if not (first and slot == 0):
                        pe.wait_ge(probs_ready, N_SC * b + 3 * slot + j - 2)
                    for kt in ((0,), (1, 3), (2,))[j]:
                        at = K_OFF[kt] - j * T
                        n = K_N[kt]
                        keys = slice(kt * P, (kt + 1) * P)
                        nc.tensor.matmul(SC[j][:, at:at + n], ks_hi[:, slot, keys], qs[:, slot, kt * P:T],
                                         start=True, stop=False)
                        nc.tensor.matmul(SC[j][:, at:at + n], ks_lo[:, slot, keys], qs[0:KC, slot, kt * P:T],
                                         start=False, stop=False)
                        last = nc.tensor.matmul(SC[j][:, at:at + P], identb[:], maskk[:], start=False, stop=True)
                    last.then_inc(sc_ready, 1)

                def weigh(b, g, first):
                    if not (first and g == 0):
                        pe.wait_ge(o_free, N_O * b + g)
                    pe.wait_ge(probs_ready, N_SC * b + 3 * GH * (g + 1))
                    if g == 0:
                        for u in U_V:
                            wait_out(pe, b, u)
                    for kt in range(TT):
                        for hq in range(GH):
                            last = nc.tensor.matmul(O[32 * hq:32 * hq + 32, kt * P:T], v[:, kt, GH * g + hq, :],
                                                    probs[:, g % 2, hq, K_OFF[kt]:K_OFF[kt] + K_N[kt]],
                                                    start=kt == 0, stop=kt == TT - 1)
                    last.then_inc(o_ready, 1)

                def output(b, half):
                    pe.wait_ge(on_ready, 2 * (b + 1))
                    pe.wait_ge(o_free, N_O * b + NG + half)
                    for k in range(2):
                        t = 2 * half + k
                        for c in range(NG // 2):
                            last = nc.tensor.matmul(O[:, k * D:(k + 1) * D], o_n[:, c, t * P:(t + 1) * P], w_o[:, c, :],
                                                    start=c == 0, stop=c == NG // 2 - 1)
                    last.then_inc(o_ready, 1)

                def body(b, first, rest):
                    for s in range(NH):
                        g, hq = s // GH, s % GH
                        if hq == 0:
                            stacked(b, g)
                            pe.wait_ge(score_loaded[g], 16 * N_SCORE * (b + 1))
                        for j in range(3):
                            score(b, s, j, first)
                            unit = 3 * hq + j - 1
                            mb, mg = (b, g + 2) if g < 2 else (b + 1, g - 2)
                            if g < 2 or rest or s == 2 * GH and unit == -1:
                                if unit == 0:
                                    stacked(mb, mg)
                                maximum(mb, mg, unit, False)
                        if hq == 0 and not (first and g == 0):
                            weigh(b, g - 1, first) if g else weigh(b - 1, NG - 1, False)
                        if s == 0:
                            for u in U_V:
                                project(b, u, False)
                        if s in OUTPUT_STEPS and not first:
                            output(b - 1, OUTPUT_STEPS.index(s))
                        if rest:
                            for u in STEP_UNITS.get(s, ()):
                                project(b + 1, u, False)

                for u in range(9):
                    project(0, u, True)
                for g in range(2):
                    stacked(0, g)
                    for j in range(-1, 11):
                        if g or j >= 0:
                            maximum(0, g, j, True)
                pe.wait_ge(ones_set, 1)
                body(0, True, 2)
                with pe.Fori(1, NB - 2) as b:
                    body(b, False, 2)
                body(NB - 2, False, 1)
                body(NB - 1, False, 0)
                weigh(NB - 1, NG - 1, False)
                for half in range(2):
                    output(NB - 1, half)


def build(nc, a, rope_table, out):
    N = a["x"].shape[0]
    x1 = nc.dram_tensor("x1", [N, D], F32, kind="Internal").ap()
    x2 = nc.dram_tensor("x2", [N, D], F32, kind="Internal").ap()
    routed = nc.dram_tensor("routed", [E * (N + P) + P, ROW], F32, kind="Internal").ap()
    scratch = {k: nc.dram_tensor(f"scratch_{k}", [N // T, D, 2, T], F16, kind="Internal").ap()
               for k in ("q", "k_hi", "k_lo")}
    scratch["nmax"] = nc.dram_tensor("scratch_nmax", [N // T, NG, GH * T], F16, kind="Internal").ap()
    with ExitStack() as ctx:
        psum = [ctx.enter_context(nc.psum_tensor(f"bank{i}", [P, 512], F32)) for i in range(8)]
        ident = ctx.enter_context(nc.sbuf_tensor("ident", [P, P], F32))
        identb = ctx.enter_context(nc.sbuf_tensor("identb", [P, P], BF16))
        made = ctx.enter_context(nc.semaphore("ident_made"))
        with nc.Block() as block:
            @block.gpsimd
            def _(pool):
                nc.gpsimd.memset(ident[:], 0.0)
                nc.gpsimd.memset(identb[:], 0.0).then_inc(made, 1)
                pool.wait_ge(made, 1)
                for m in (ident, identb):
                    nc.gpsimd.affine_select(out=m[:], in_=m[:], compare_op=ALU.not_equal, fill=1.0,
                                            base=0, pattern=[[-1, P]], channel_multiplier=1)
        const = {"ident": ident, "identb": identb}
        ffn = (a["Wg"], a["bg"], a["We"], a["be"])
        ffn_phase(nc, "f1", psum, const, a["x"], x1, routed, *ffn)
        attention_phase(nc, psum, const, x1, x2, a, rope_table, scratch)
        ffn_phase(nc, "f2", psum, const, x2, out, routed, *ffn)


def rope_constants(np):
    inv = (np.float32(1.0) / np.power(np.float32(10000.0), np.arange(0, R, 2, dtype=np.float32) / np.float32(R))).astype(np.float32)
    angle = np.outer(inv, np.arange(T, dtype=np.float32)).astype(np.float32)
    cos, sin = np.cos(angle), np.sin(angle)
    return np.concatenate([cos, cos, -sin, sin])


def kernel(**inputs):
    import numpy as np
    import concourse.bacc as bacc
    from concourse.bass_utils import run_bass_kernel_spmd

    nc = bacc.Bacc("TRN2", target_bir_lowering=False, num_devices=1)
    x = np.ascontiguousarray(inputs["L0_attn_x"])
    shape = x.shape
    arrays = {"x": x.reshape(-1, shape[-1])}
    for name in inputs:
        if name != "L0_attn_x":
            short = name.replace("L0_attn_W_", "").replace("L0_ffn_", "")
            arrays[short] = np.ascontiguousarray(inputs[name])
    arrays["rope_table"] = rope_constants(np)
    aps = {n: nc.dram_tensor(f"in_{n}", v.shape, mybir.dt.from_np(v.dtype), kind="ExternalInput").ap()
           for n, v in arrays.items()}
    out = nc.dram_tensor("out", arrays["x"].shape, F32, kind="ExternalOutput").ap()
    build(nc, aps, aps["rope_table"], out)
    r = run_bass_kernel_spmd(nc, [{f"in_{n}": v for n, v in arrays.items()}], core_ids=[0])
    return r.results[0]["out"].reshape(shape)
```

```python
from contextlib import ExitStack

import concourse.bass as bass
from concourse import mybir
from concourse.alu_op_type import AluOpType as ALU

F32 = mybir.dt.float32
F16 = mybir.dt.float16
BF16 = mybir.dt.bfloat16
I32 = mybir.dt.int32
U32 = mybir.dt.uint32
ACT = mybir.ActivationFunctionType
AX_X = mybir.AxisListType.X

P = 128
D = 256
DC = D // P
C = 128
R = 32
NH = 16
HD = D // NH
T = 512
TT = T // P
E = 8
EPS = 1e-5
GT = 4
GR = 4
RING = 12
ROW = D + 4
MASKED = -1e30
GH = 4
NG = NH // GH
HR = 2 * HD
KC = HR + 2 * R
ROW_MAX = KC
SCALE = float(HD + R) ** -0.5


def ffn_weights(nc, ctx):
    def sb(n, shape, dt=F32):
        return ctx.enter_context(nc.sbuf_tensor(f"ffn_{n}", shape, dt))

    w = {"wg": sb("wg", [P, DC, D]), "we": sb("we", [P, DC, E * D]), "beb": sb("beb", [P, E * D]),
         "bg_rows": sb("bg_rows", [3, D], BF16)}
    for n in ("wg_loaded", "we_loaded", "bg_placed"):
        w[n] = ctx.enter_context(nc.semaphore(f"ffn_{n}"))
    return w


def ffn_phase(nc, name, psum, const, x_in, x_out, routed, w, weights=None, load_next=None):
    tokens = x_in.shape[0]
    groups = tokens // (GT * P)
    xv = x_in.rearrange("(g t p) d -> g p t d", p=P, t=GT)
    region = (routed.shape[0] - P) // E
    spare = E * region
    SHORT = 4
    sorted_tiles = -(-(tokens // P + E - 1) // RING) * RING
    ctx = ExitStack()
    with ctx:
        def sb(n, shape, dt=F32):
            return ctx.enter_context(nc.sbuf_tensor(f"{name}_{n}", shape, dt))

        def sem(n, count=0):
            if count:
                return [ctx.enter_context(nc.semaphore(f"{name}_{n}{k}")) for k in range(count)]
            return ctx.enter_context(nc.semaphore(f"{name}_{n}"))

        wg, we, beb, bg_rows = w["wg"], w["we"], w["beb"], w["bg_rows"]
        w_loaded, we_loaded, bg_placed = w["wg_loaded"], w["we_loaded"], w["bg_placed"]
        if weights:
            bg_row = sb("bg_row", [1, D])
            bg_rest = sb("bg_rest", [1, 2, D])
            bg3 = sb("bg3", [1, 3, D], BF16)
            bg_loaded = sem("bg_loaded")
            bg_step = sem("bg_step")
        ones = sb("ones", [P, P], BF16)
        before = sb("before", [P, P], BF16)
        power = sb("power", [P, GT])
        ids = sb("ids", [P, E])
        padding = sb("padding", [P, ROW])

        x = sb("x", [P, GR, GT, D])
        rows = sb("rows", [P, GR, GT, ROW])
        stats = sb("stats", [P, 2, GT, 6])
        mv = sb("mv", [P, GR, GT, 2])
        veps = sb("veps", [P, GT])
        shift = sb("shift", [P, GR, GT])
        xn = sb("xn", [P, 2, GT, D])
        xT = sb("xT", [P, 2, DC, GT * P])
        top = sb("top", [P, 2, GT, 8])
        top_at = sb("top_at", [P, 2, GT, 8], U32)
        ntop = sb("ntop", [P, 2, GT])
        expert_i = sb("expert_i", [P, GT], U32)
        expert = sb("expert", [P, GT])
        onehot = sb("onehot", [P, 2, GT, E], BF16)
        junk = sb("junk", [P, GT, D])
        esum = sb("esum", [P, 2, GT])
        prob = sb("prob", [P, GT])
        token = sb("token", [P, GT])
        base = sb("base", [P, 2, E])
        rank = sb("rank", [P, GT, E])
        chosen = sb("chosen", [P, GT, E])
        row_f = sb("row_f", [P, GT])
        row_i = sb("row_i", [P, GR, GT], U32)

        N = sorted_tiles
        start_f = sb("start_f", [P, E])
        start_i = sb("start_i", [P, E], I32)
        count = sb("count", [P, E])
        tiles_i = sb("tiles_i", [P, E], I32)
        tiles_f = sb("tiles_f", [P, E])
        ends = sb("ends", [P, E])
        one8 = sb("one8", [P, E])
        tile_no = sb("tile_no", [P, N])
        past = sb("past", [P, N, E])
        past_tiles = sb("past_tiles", [P, N, E])
        owner = sb("owner", [P, N])
        first_tile = sb("first_tile", [P, N])
        local = sb("local", [P, N])
        at_f = sb("at_f", [P, N])
        at_i = sb("at_i", [P, N], I32)
        column_f = sb("column_f", [P, N])
        column_i = sb("column_i", [P, N], I32)

        srow = sb("srow", [P, RING, ROW])
        sxn = sb("sxn", [P, SHORT, D])
        sxT = sb("sxT", [P, SHORT, DC, P])
        pre = sb("pre", [P, SHORT, D])
        act_out = sb("act_out", [P, SHORT, D])
        y = sb("y", [P, SHORT, D])
        to_i = sb("to_i", [P, SHORT], U32)

        xT_ps = psum[0:2]
        gate_ps = psum[2:6]
        rank_ps = psum[6:8]
        sxT_ps = psum[0:SHORT]
        product_ps = psum[SHORT:2 * SHORT]

        made = sem("made")
        x_loaded = sem("x_loaded", GR)
        ln_stats = sem("ln_stats")
        ln_aggr = sem("ln_aggr")
        ln_eps = sem("ln_eps")
        ln_rstd = sem("ln_rstd")
        ln_shift = sem("ln_shift")
        xn_ready = sem("xn_ready")
        xT_ps_ready = sem("xT_ps_ready")
        xT_ready = sem("xT_ready")
        gate_ready = sem("gate_ready")
        top_step = sem("top_step")
        top_ready = sem("top_ready")
        exp_done = sem("exp_done")
        mark_step = sem("mark_step")
        route_step = sem("route_step")
        onehot_ready = sem("onehot_ready")
        rank_ready = sem("rank_ready")
        rows_ready = sem("rows_ready")
        scattered = sem("scattered", GR)
        x_copied = sem("x_copied")
        padded = sem("padded")
        plan_step = sem("plan_step")
        plan_ready = sem("plan_ready")
        srow_loaded = sem("srow_loaded", RING)
        sxn_ready = sem("sxn_ready")
        sxT_ps_ready = sem("sxT_ps_ready")
        sxT_ready = sem("sxT_ready")
        product_ready = sem("product_ready")
        pre_ready = sem("pre_ready")
        act_ready = sem("act_ready")
        y_ready = sem("y_ready")
        y_stored = sem("y_stored", SHORT)
        ROUTE_STEPS = 8
        MARK_STEPS = 2

        def at(i, k):
            return i + k // GR, k % GR

        def tile_at(i, k):
            return i + k // RING, k % RING

        def gate_steps(eng, step):
            turns = groups // GR
            for k in range(GR):
                step(0, k, True, False)
            with eng.Fori(1, turns - 1) as i:
                for k in range(GR):
                    step(i, k, False, False)
            for k in range(GR):
                step(turns - 1, k, False, True)

        def tile_steps(eng, step):
            turns = N // RING
            for k in range(RING):
                step(0, k, True, False)
            with eng.Fori(1, turns - 1) as i:
                for k in range(RING):
                    step(i, k, False, False)
            for k in range(RING):
                step(turns - 1, k, False, True)

        def pad(eng, start):
            eng.wait_ge(plan_ready, 1)
            for e in range(start, E, 2):
                row = eng.value_load(start_i[0:1, e:e + 1], min_val=0, max_val=spare - P)
                eng.dma_start(routed[bass.ds(row, P), :], padding[:]).then_inc(padded, 16)

        with nc.Block() as block:
            @block.sync
            def _(sp):
                if weights:
                    sp.dma_start(bg_row[:], weights["bg"].rearrange("(o f) -> o f", o=1)).then_inc(bg_loaded, 16)
                for k in range(2):
                    sp.dma_start(x[:, k], xv[k]).then_inc(x_loaded[k], 16)
                if weights:
                    sp.dma_start(wg[:], weights["Wg"].rearrange("(c p) f -> p c f", p=P)).then_inc(w_loaded, 16)
                    sp.wait_ge(bg_step, 5)
                    for part in range(3):
                        sp.dma_start(bg_rows[part:part + 1, :], bg3[:, part, :]).then_inc(bg_placed, 16)
                for k in range(2, GR):
                    sp.dma_start(x[:, k], xv[k]).then_inc(x_loaded[k], 16)
                if weights:
                    for c in range(DC):
                        sp.dma_start(we[:, c, :].rearrange("p (e f) -> p e f", e=E),
                                     weights["We"][:, c * P:(c + 1) * P, :].rearrange("e p f -> p e f")).then_inc(we_loaded, 16)
                    sp.dma_start(beb[:], weights["be"].rearrange("e f -> (e f)").partition_broadcast(P)).then_inc(we_loaded, 16)
                sp.wait_ge(made, 3)
                sp.dma_start(routed[spare:spare + P, :], padding[:]).then_inc(padded, 16)
                with sp.Fori(1, groups // GR) as i:
                    for k in range(GR):
                        sp.wait_ge(xn_ready, GR * (i - 1) + k + 1)
                        sp.nop(nofuse=True)
                        sp.wait_ge(x_copied, GR * (i - 1) + k + 1)
                        sp.nop(nofuse=True)
                        sp.dma_start(x[:, k], xv[GR * i + k]).then_inc(x_loaded[k], 16)
                if load_next:
                    load_next(sp)
                pad(sp, 0)
                sp.wait_ge(padded, 16 * (E + 1))
                for k in range(GR):
                    sp.wait_ge(scattered[k], 16 * GT * (groups // GR))

                def load(j, k):
                    row = sp.value_load(at_i[0:1, bass.ds(j, 1)], min_val=0, max_val=spare)
                    sp.dma_start(srow[:, k, :], routed[bass.ds(row, P), :]).then_inc(srow_loaded[k], 16)

                sp.wait_ge(plan_ready, 2)
                for k in range(RING):
                    load(k, k)
                with sp.Fori(1, N // RING) as i:
                    for k in range(RING):
                        sp.wait_ge(y_ready, RING * (i - 1) + k + 1)
                        sp.nop(nofuse=True)
                        load(RING * i + k, k)

            @block.gpsimd
            def _(pool):
                nc.gpsimd.memset(power[:], -0.5)
                nc.gpsimd.memset(ones[:], 1.0)
                nc.gpsimd.memset(before[:], 1.0).then_inc(made, 1)
                pool.wait_ge(made, 1)
                nc.gpsimd.affine_select(out=before[:], in_=before[:], compare_op=ALU.is_gt, fill=0.0,
                                        base=0, pattern=[[1, P]], channel_multiplier=-1).then_inc(made, 1)

                def deviation(i, k, first=False):
                    n = GR * i + k
                    if not first:
                        pool.wait_ge(ln_rstd, n)
                    pool.wait_ge(ln_aggr, n + 1)
                    pool.nop(nofuse=True)
                    nc.gpsimd.tensor_scalar(veps[:], mv[:, k, :, 1], EPS, None, ALU.add).then_inc(ln_eps, 1)
                    pool.wait_ge(ln_eps, n + 1)
                    nc.gpsimd.tensor_tensor(mv[:, k, :, 1], veps[:], power[:], ALU.pow).then_inc(ln_rstd, 1)

                def scatter(i, k):
                    n = GR * i + k
                    pool.wait_ge(x_copied, n + 1)
                    pool.nop(nofuse=True)
                    pool.wait_ge(rows_ready, n + 1)
                    pool.nop(nofuse=True)
                    for t in range(GT):
                        nc.gpsimd.indirect_dma_start(
                            out=routed, out_offset=bass.IndirectOffsetOnAxis(ap=row_i[:, k, t:t + 1], axis=0),
                            in_=rows[:, k, t, :], in_offset=None).then_inc(scattered[k], 16)

                def step(i, k, first, last):
                    if not (last and k >= GR - 2):
                        deviation(*at(i, k + 2))
                    if not (first and k == 0):
                        scatter(*at(i - 1, k + GR - 1))

                for k in range(2):
                    deviation(0, k, k == 0)
                nc.gpsimd.memset(padding[:, 0:ROW - 1], 0.0)
                nc.gpsimd.memset(padding[:, ROW - 1:ROW], float(tokens))
                nc.gpsimd.memset(one8[:], 1.0)
                nc.gpsimd.iota(ids[:], [[1, E]], base=0, channel_multiplier=0, allow_small_or_imprecise_dtypes=True)
                nc.gpsimd.iota(tile_no[:], [[1, N]], base=0, channel_multiplier=0, allow_small_or_imprecise_dtypes=True)
                nc.gpsimd.iota(token[:], [[P, GT]], base=0, channel_multiplier=1, allow_small_or_imprecise_dtypes=True)
                nc.gpsimd.iota(base[:, 0, :], [[region, E]], base=0, channel_multiplier=0,
                               allow_small_or_imprecise_dtypes=True)
                nc.gpsimd.iota(start_f[:], [[region, E]], base=0, channel_multiplier=0,
                               allow_small_or_imprecise_dtypes=True).then_inc(made, 1)
                gate_steps(pool, step)
                scatter(groups // GR - 1, GR - 1)

                def combine(i, k, first, last):
                    j = RING * i + k
                    pool.wait_ge(y_ready, j + 1)
                    pool.nop(nofuse=True)
                    nc.gpsimd.indirect_dma_start(
                        out=x_out, out_offset=bass.IndirectOffsetOnAxis(ap=to_i[:, k % SHORT:k % SHORT + 1], axis=0),
                        in_=y[:, k % SHORT, :], in_offset=None, bounds_check=tokens - 1,
                        oob_is_err=False).then_inc(y_stored[k % SHORT], 16)

                tile_steps(pool, combine)
                for k in range(SHORT):
                    pool.wait_ge(y_stored[k], 16 * (N // SHORT))

            @block.scalar
            def _(act):
                act.preload_act_table(ACT.Exp)

                def normalise(i, k, first):
                    n = GR * i + k
                    act.wait_ge(x_loaded[k], 16 * (i + 1))
                    act.wait_ge(ln_shift, n + 1)
                    if not (first and k < 2):
                        act.wait_ge(xT_ps_ready, DC * (n - 1))
                    for t in range(GT):
                        last = nc.scalar.activation(xn[:, k % 2, t, :], x[:, k, t, :], ACT.Identity,
                                                    bias=shift[:, k, t:t + 1], scale=mv[:, k, t, 1:2])
                    last.then_inc(xn_ready, 1)

                def transposed(i, k, first):
                    n = GR * i + k
                    for c in range(DC):
                        act.wait_ge(xT_ps_ready, DC * n + c + 1)
                        if c == 0 and not (first and k < 2):
                            act.wait_ge(gate_ready, 2 * (n - 1))
                        nc.scalar.activation(xT[:, k % 2, c, :], xT_ps[c][:], ACT.Copy).then_inc(xT_ready, 1)

                def copy_x(i, k, first):
                    n = GR * i + k
                    act.wait_ge(x_loaded[k], 16 * (i + 1))
                    if not first:
                        act.wait_ge(scattered[k], 16 * GT * i)
                    nc.scalar.activation(rows[:, k, :, 0:D], x[:, k], ACT.Copy).then_inc(x_copied, 1)

                def exps(i, k, first):
                    n = GR * i + k
                    for h in range(2):
                        act.wait_ge(top_ready, 2 * n + h + 1)
                        for t in range(2 * h, 2 * h + 2):
                            if not (first and k == 0):
                                act.wait_ge(exp_done, GT * (n - 1) + t + 1)
                            if not (first and k < 2) and t == 0:
                                act.wait_ge(route_step, ROUTE_STEPS * (n - 2) + 1)
                            nc.scalar.activation(junk[:, t, :], gate_ps[2 * (k % 2) + h][:, (t % 2) * D:(t % 2 + 1) * D], ACT.Exp,
                                                 bias=ntop[:, k % 2, t:t + 1],
                                                 accum_out=esum[:, k % 2, t:t + 1]).then_inc(exp_done, 1)

                def step(i, k, first, last):
                    if not (last and k == GR - 1):
                        to = at(i, k + 1)
                        transposed(*to, first and k < GR - 1)
                    copy_x(i, k, first)
                    exps(i, k, first)
                    if not (last and k >= GR - 2):
                        normalise(*at(i, k + 2), first and k < GR - 2)

                for k in range(2):
                    normalise(0, k, True)
                transposed(0, 0, True)
                gate_steps(act, step)
                pad(act, 1)

                def expert_out(i, k, first):
                    j = RING * i + k
                    act.wait_ge(pre_ready, j + 1)
                    nc.scalar.activation(act_out[:, k % SHORT, :], pre[:, k % SHORT, :], ACT.Relu,
                                         scale=srow[:, k, D + 2:D + 3]).then_inc(act_ready, 1)

                def tile_transposed(i, k, first):
                    j = RING * i + k
                    act.wait_ge(sxT_ps_ready, j + 1)
                    nc.scalar.activation(sxT[:, k % SHORT], sxT_ps[k % SHORT][:, 0:DC * P].rearrange("p (c t) -> p c t", c=DC),
                                         ACT.Copy).then_inc(sxT_ready, 1)

                def tile_step(i, k, first, last):
                    if not (last and k >= RING - 2):
                        tile_transposed(*tile_at(i, k + 2), first and k < RING - 2)
                    if not (first and k == 0):
                        expert_out(*tile_at(i - 1, k + RING - 1), first)

                for k in range(2):
                    tile_transposed(0, k, True)
                tile_steps(act, tile_step)
                expert_out(N // RING - 1, RING - 1, False)

            @block.vector
            def _(dve):
                if weights:
                    dve.wait_ge(bg_loaded, 16)
                    nc.vector.tensor_copy(bg3[:, 0, :], bg_row[:]).then_inc(bg_step, 1)
                    dve.wait_ge(bg_step, 1)
                    nc.vector.tensor_tensor(bg_rest[:, 0, :], bg_row[:], bg3[:, 0, :], ALU.subtract).then_inc(bg_step, 1)
                    dve.wait_ge(bg_step, 2)
                    nc.vector.tensor_copy(bg3[:, 1, :], bg_rest[:, 0, :]).then_inc(bg_step, 1)
                    dve.wait_ge(bg_step, 3)
                    nc.vector.tensor_tensor(bg_rest[:, 1, :], bg_rest[:, 0, :], bg3[:, 1, :], ALU.subtract).then_inc(bg_step, 1)
                    dve.wait_ge(bg_step, 4)
                    nc.vector.tensor_copy(bg3[:, 2, :], bg_rest[:, 1, :]).then_inc(bg_step, 1)

                def statistics(i, k, first):
                    n = GR * i + k
                    dve.wait_ge(x_loaded[k], 16 * (i + 1))
                    if not (first and k < 2):
                        dve.wait_ge(ln_aggr, n - 1)
                    for t in range(GT):
                        last = nc.vector.bn_stats(stats[:, k % 2, t, :], x[:, k, t, :])
                    last.then_inc(ln_stats, 1)
                    dve.wait_ge(ln_stats, n + 1)
                    if not first:
                        dve.wait_ge(rows_ready, n - GR + 1)
                    dve.nop(nofuse=True)
                    for t in range(GT):
                        last = nc.vector.bn_aggr(mv[:, k, t, :], stats[:, k % 2, t, :])
                    last.then_inc(ln_aggr, 1)

                def offset(i, k, first):
                    n = GR * i + k
                    dve.wait_ge(ln_rstd, n + 1)
                    if not first:
                        dve.wait_ge(xn_ready, n - GR + 1)
                    nc.vector.scalar_tensor_tensor(shift[:, k, :], mv[:, k, :, 0], -1.0, mv[:, k, :, 1],
                                                   ALU.mult, ALU.mult).then_inc(ln_shift, 1)

                def tops(i, k, first):
                    n = GR * i + k
                    for h in range(2):
                        logits = gate_ps[2 * (k % 2) + h]
                        pair = slice(2 * h, 2 * h + 2)
                        dve.wait_ge(gate_ready, 2 * n + h + 1)
                        if h == 0 and not (first and k < 2):
                            dve.wait_ge(exp_done, GT * (n - 1))
                            dve.wait_ge(onehot_ready, n - 1)
                        dve.nop(nofuse=True)
                        for t in range(2 * h, 2 * h + 2):
                            last = nc.vector.max(top[:, k % 2, t, :], logits[:, (t % 2) * D:(t % 2 + 1) * D])
                        last.then_inc(top_step, 1)
                        dve.wait_ge(top_step, 2 * n + h + 1)
                        dve.nop(nofuse=True)
                        nc.vector.tensor_scalar(ntop[:, k % 2, pair], top[:, k % 2, pair, 0], -1.0, None, ALU.mult)
                        for t in range(2 * h, 2 * h + 2):
                            last = nc.vector.max_index(top_at[:, k % 2, t, :], top[:, k % 2, t, :],
                                                       logits[:, (t % 2) * D:(t % 2 + 1) * D])
                        last.then_inc(top_ready, 1)

                def mark(i, k, first):
                    n = GR * i + k
                    step = MARK_STEPS * n
                    if not (first and k == 0):
                        dve.wait_ge(onehot_ready, n)
                    dve.wait_ge(top_ready, 2 * n + 2)
                    nc.vector.tensor_scalar(expert_i[:], top_at[:, k % 2, :, 0], E - 1, None, ALU.bitwise_and).then_inc(mark_step, 1)
                    dve.wait_ge(mark_step, step + 1)
                    nc.vector.tensor_copy(expert[:], expert_i[:]).then_inc(mark_step, 1)
                    dve.wait_ge(mark_step, step + 2)
                    if not (first and k < 2):
                        dve.wait_ge(rows_ready, n - 1)
                    nc.vector.tensor_tensor(onehot[:, k % 2], ids[:].unsqueeze(1).broadcast_to([P, GT, E]),
                                            expert[:].unsqueeze(2).broadcast_to([P, GT, E]), ALU.is_equal).then_inc(onehot_ready, 1)

                def route(i, k, first):
                    n = GR * i + k
                    step = ROUTE_STEPS * n
                    if not (first and k == 0):
                        dve.wait_ge(rows_ready, n)
                    dve.wait_ge(exp_done, GT * (n + 1))
                    nc.vector.reciprocal(prob[:], esum[:, k % 2, :]).then_inc(route_step, 1)
                    dve.wait_ge(rank_ready, n + 1)
                    counted = rank_ps[k % 2]
                    nc.vector.tensor_tensor(rank[:], counted[:, 0:GT * E].rearrange("p (t e) -> p t e", t=GT),
                                            base[:, k % 2, :].unsqueeze(1).broadcast_to([P, GT, E]),
                                            ALU.add).then_inc(route_step, 1)
                    nc.vector.tensor_tensor(base[:, 1 - k % 2, :], counted[:, GT * E:GT * E + E], base[:, k % 2, :],
                                            ALU.add).then_inc(route_step, 1)
                    dve.wait_ge(route_step, step + 2)
                    nc.vector.tensor_tensor(chosen[:], rank[:], onehot[:, k % 2], ALU.mult).then_inc(route_step, 1)
                    nc.vector.tensor_scalar(rows[:, k, :, D + 2], prob[:], 0.5, None, ALU.mult).then_inc(route_step, 1)
                    nc.vector.tensor_copy(rows[:, k, :, D + 3], token[:]).then_inc(route_step, 1)
                    dve.wait_ge(route_step, step + 4)
                    nc.vector.tensor_reduce(row_f[:], chosen[:], AX_X, ALU.add).then_inc(route_step, 1)
                    nc.vector.tensor_copy(rows[:, k, :, D:D + 2], mv[:, k])
                    dve.wait_ge(route_step, step + 6)
                    nc.vector.tensor_scalar(token[:], token[:], float(GT * P), None, ALU.add).then_inc(route_step, 1)
                    dve.wait_ge(route_step, step + 7)
                    nc.vector.tensor_copy(row_i[:, k, :], row_f[:]).then_inc(rows_ready, 1)

                def step(i, k, first, last):
                    if not (last and k >= GR - 2):
                        statistics(*at(i, k + 2), first and k < GR - 2)
                    tops(i, k, first)
                    if not first:
                        dve.wait_ge(scattered[k], 16 * GT * i)
                    mark(i, k, first)
                    if not (first and k == 0):
                        route(*at(i - 1, k + GR - 1), first)
                    if not (last and k >= GR - 2):
                        offset(*at(i, k + 2), first and k < GR - 2)

                for k in range(2):
                    statistics(0, k, True)
                for k in range(2):
                    offset(0, k, True)
                dve.wait_ge(made, 3)
                gate_steps(dve, step)
                route(groups // GR - 1, GR - 1, False)

                dve.wait_ge(rows_ready, groups)
                nc.vector.tensor_tensor(count[:], base[:, 0, :], start_f[:], ALU.subtract).then_inc(plan_step, 1)
                nc.vector.tensor_copy(start_i[:], base[:, 0, :]).then_inc(plan_ready, 1)
                dve.wait_ge(plan_step, 1)
                nc.vector.tensor_scalar(tiles_f[:], count[:], float(P - 1), None, ALU.add).then_inc(plan_step, 1)
                dve.wait_ge(plan_step, 2)
                nc.vector.tensor_copy(tiles_i[:], tiles_f[:]).then_inc(plan_step, 1)
                dve.wait_ge(plan_step, 3)
                nc.vector.tensor_scalar(tiles_i[:], tiles_i[:], 7, None, ALU.arith_shift_right).then_inc(plan_step, 1)
                dve.wait_ge(plan_step, 4)
                nc.vector.tensor_copy(tiles_f[:], tiles_i[:]).then_inc(plan_step, 1)
                dve.wait_ge(plan_step, 5)
                nc.vector.tensor_tensor_scan(ends[:], one8[:], tiles_f[:], 0.0, ALU.mult, ALU.add).then_inc(plan_step, 1)
                dve.wait_ge(plan_step, 6)
                nc.vector.tensor_tensor(past[:], tile_no[:].unsqueeze(2).broadcast_to([P, N, E]),
                                        ends[:].unsqueeze(1).broadcast_to([P, N, E]), ALU.is_ge).then_inc(plan_step, 1)
                dve.wait_ge(plan_step, 7)
                nc.vector.tensor_reduce(owner[:], past[:], AX_X, ALU.add)
                nc.vector.tensor_tensor(past_tiles[:], past[:], tiles_f[:].unsqueeze(1).broadcast_to([P, N, E]),
                                        ALU.mult).then_inc(plan_step, 1)
                dve.wait_ge(plan_step, 8)
                nc.vector.tensor_reduce(first_tile[:], past_tiles[:], AX_X, ALU.add)
                nc.vector.tensor_scalar(column_f[:], owner[:], float(E - 1), float(D), ALU.min, ALU.mult)
                nc.vector.tensor_scalar(at_f[:], owner[:], float(region), None, ALU.mult).then_inc(plan_step, 1)
                dve.wait_ge(plan_step, 9)
                nc.vector.tensor_tensor(local[:], tile_no[:], first_tile[:], ALU.subtract)
                nc.vector.tensor_copy(column_i[:], column_f[:]).then_inc(plan_step, 1)
                dve.wait_ge(plan_step, 10)
                nc.vector.scalar_tensor_tensor(at_f[:], local[:], float(P), at_f[:], ALU.mult, ALU.add).then_inc(plan_step, 1)
                dve.wait_ge(plan_step, 11)
                nc.vector.tensor_scalar(at_f[:], at_f[:], float(spare), None, ALU.min).then_inc(plan_step, 1)
                dve.wait_ge(plan_step, 12)
                nc.vector.tensor_copy(at_i[:], at_f[:]).then_inc(plan_ready, 1)
                dve.wait_ge(plan_ready, 2)

                def tile_norm(i, k, first):
                    j = RING * i + k
                    if first and k == SHORT:
                        dve.wait_ge(sxT_ps_ready, 1)
                    dve.wait_ge(srow_loaded[k], 16 * (i + 1))
                    nc.vector.tensor_scalar(sxn[:, k % SHORT, :], srow[:, k, 0:D], srow[:, k, D:D + 1],
                                            srow[:, k, D + 1:D + 2], ALU.subtract, ALU.mult).then_inc(sxn_ready, 1)

                def add_bias(i, k, first):
                    j = RING * i + k
                    column = dve.value_load(column_i[0:1, bass.ds(j, 1)], min_val=0, max_val=(E - 1) * D)
                    dve.wait_ge(product_ready, j + 1)
                    nc.vector.tensor_tensor(pre[:, k % SHORT, :], product_ps[k % SHORT][:, 0:D], beb[:, bass.ds(column, D)],
                                            ALU.add).then_inc(pre_ready, 1)

                def add_x(i, k, first=False):
                    j = RING * i + k
                    slot = k % SHORT
                    if not (first and k < SHORT):
                        dve.wait_ge(y_stored[slot], 16 * (RING // SHORT * i + k // SHORT))
                    nc.vector.tensor_copy(to_i[:, slot:slot + 1], srow[:, k, D + 3:D + 4])
                    dve.wait_ge(act_ready, j + 1)
                    nc.vector.tensor_tensor(y[:, slot, :], act_out[:, slot, :], srow[:, k, 0:D], ALU.add).then_inc(y_ready, 1)

                def tile_step(i, k, first, last):
                    if not (last and k >= RING - 4):
                        tile_norm(*tile_at(i, k + 4), first and k < RING - 4)
                    add_bias(i, k, first)
                    if not (first and k < 2):
                        add_x(*tile_at(i - 1, k + RING - 2), first)

                dve.wait_ge(we_loaded, 16 * (DC + 1))
                for k in range(4):
                    tile_norm(0, k, True)
                tile_steps(dve, tile_step)
                for k in range(RING - 2, RING):
                    add_x(N // RING - 1, k)

            @block.tensor
            def _(pe):
                ident = const["ident"]

                def transposes(i, k, first):
                    n = GR * i + k
                    pe.wait_ge(xn_ready, n + 1)
                    for c in range(DC):
                        if not (first and k == 0):
                            pe.wait_ge(xT_ready, DC * (n - 1) + c + 1)
                        for t in range(GT):
                            last = nc.tensor.transpose(xT_ps[c][:, t * P:(t + 1) * P], xn[:, k % 2, t, c * P:(c + 1) * P], ident[:])
                        last.then_inc(xT_ps_ready, 1)

                def gate(i, k, first):
                    n = GR * i + k
                    pe.wait_ge(xT_ready, DC * (n + 1))
                    for h in range(2):
                        logits = gate_ps[2 * (k % 2) + h]
                        if not (first and k < 2):
                            pe.wait_ge(exp_done, GT * (n - 2) + 2 * h + 2)
                        nc.tensor.matmul(logits[:], ones[0:3, :], bg_rows[:].unsqueeze(1).broadcast_to([3, 2, D]),
                                         start=True, stop=False, skip_group_check=True)
                        for t in range(2 * h, 2 * h + 2):
                            out = logits[:, (t % 2) * D:(t % 2 + 1) * D]
                            for c in range(DC):
                                last = nc.tensor.matmul(out, xT[:, k % 2, c, t * P:(t + 1) * P], wg[:, c, :], start=False,
                                                        stop=c == DC - 1, skip_group_check=True)
                        last.then_inc(gate_ready, 1)

                def ranks(i, k, first):
                    n = GR * i + k
                    pe.wait_ge(onehot_ready, n + 1)
                    if not (first and k < 2):
                        pe.wait_ge(rows_ready, n - 1)
                    for t in range(GT + 1):
                        out = rank_ps[k % 2][:, t * E:(t + 1) * E]
                        for s in range(t):
                            last = nc.tensor.matmul(out, ones[:], onehot[:, k % 2, s, :], start=s == 0, stop=t == GT and s == t - 1)
                        if t < GT:
                            nc.tensor.matmul(out, before[:], onehot[:, k % 2, t, :], start=t == 0, stop=True)
                    last.then_inc(rank_ready, 1)

                def step(i, k, first, last):
                    gate(i, k, first)
                    if not (last and k == GR - 1):
                        transposes(*at(i, k + 1), False)
                    if not (first and k == 0):
                        ranks(*at(i - 1, k + GR - 1), first)

                transposes(0, 0, True)
                pe.wait_ge(w_loaded, 16)
                pe.wait_ge(made, 2)
                pe.wait_ge(bg_placed, 16 * 3)
                gate_steps(pe, step)
                ranks(groups // GR - 1, GR - 1, False)

                pe.wait_ge(plan_ready, 2)
                pe.wait_ge(we_loaded, 16 * (DC + 1))

                def tile_transposes(i, k, first):
                    j = RING * i + k
                    pe.wait_ge(sxn_ready, j + 1)
                    for c in range(DC):
                        last = nc.tensor.transpose(sxT_ps[k % SHORT][:, c * P:(c + 1) * P], sxn[:, k % SHORT, c * P:(c + 1) * P], ident[:])
                    last.then_inc(sxT_ps_ready, 1)

                def product(i, k, first):
                    j = RING * i + k
                    column = pe.value_load(column_i[0:1, bass.ds(j, 1)], min_val=0, max_val=(E - 1) * D)
                    pe.wait_ge(sxT_ready, j + 1)
                    for c in range(DC):
                        last = nc.tensor.matmul(product_ps[k % SHORT][:, 0:D], sxT[:, k % SHORT, c, :], we[:, c, bass.ds(column, D)],
                                                start=c == 0, stop=c == DC - 1)
                    last.then_inc(product_ready, 1)

                def tile_step(i, k, first, last):
                    if not (last and k >= RING - 2):
                        tile_transposes(*tile_at(i, k + 2), first and k < RING - 2)
                    product(i, k, first)

                for k in range(2):
                    tile_transposes(0, k, True)
                tile_steps(pe, tile_step)


def attention_weights(nc, ctx):
    def sb(n, shape):
        return ctx.enter_context(nc.sbuf_tensor(f"at_{n}", shape, F32))

    return {"down": sb("w_down", [P, DC, C]), "q": sb("w_q", [P, DC, D]),
            "qr": sb("w_qr", [P, DC, 2 * R]),
            "ku": sb("w_ku", [P, D]), "kr": sb("w_kr", [P, 2 * R]), "vu": sb("w_vu", [P, D]),
            "o": sb("w_o", [P, NG // 2, D]),
            "rope": sb("rope", [2 * R, T]),
            "loaded": ctx.enter_context(nc.semaphore("at_w_loaded"))}


N_W_LOADS = 11 + 2 * GH


def load_attention_weights(sp, w, W, rope_table):
    for dst, src in ((w["down"][:], W["kv_down"].rearrange("(c p) n -> p c n", p=P)),
                     (w["q"][:], W["q"].rearrange("(c p) n -> p c n", p=P)),
                     (w["qr"][:, :, 0:R], W["q_rope"].rearrange("(c p) n -> p c n", p=P)),
                     (w["qr"][:, :, R:R + R // 2], W["q_rope"].rearrange("(c p) n -> p c n", p=P)[:, :, R // 2:R]),
                     (w["qr"][:, :, R + R // 2:2 * R], W["q_rope"].rearrange("(c p) n -> p c n", p=P)[:, :, 0:R // 2]),
                     (w["ku"][:], W["k_up"]), (w["vu"][:], W["v_up"]),
                     (w["kr"][:, 0:R], W["k_rope"]),
                     (w["kr"][:, R:R + R // 2], W["k_rope"][:, R // 2:R]),
                     (w["kr"][:, R + R // 2:2 * R], W["k_rope"][:, 0:R // 2]),
                     (w["rope"][:], rope_table)):
        sp.dma_start(dst, src).then_inc(w["loaded"], 16)
    wo = W["o"].rearrange("(c s h d) n -> s h d c n", c=NG // 2, s=2, h=GH)
    for s in range(2):
        for hq in range(GH):
            at = 32 * hq + HD * s
            sp.dma_start(w["o"][at:at + HD, :, :], wo[s, hq]).then_inc(w["loaded"], 16)


def attention_phase(nc, psum, const, x_in, x_out, w, scratch):
    NB = x_in.shape[0] // T
    xv = x_in.rearrange("(b t p) d -> b p t d", p=P, t=TT)
    ov = x_out.rearrange("(b t p) d -> b p t d", p=P, t=TT)
    ctx = ExitStack()
    with ctx:
        def sb(n, shape, dt=F32):
            return ctx.enter_context(nc.sbuf_tensor(f"at_{n}", shape, dt))

        def sem(n):
            return ctx.enter_context(nc.semaphore(f"at_{n}"))

        w_down, w_q, w_qr, w_ku, w_kr, w_vu, w_o, rope = (w[n] for n in ("down", "q", "qr", "ku", "kr", "vu", "o", "rope"))
        w_loaded = w["loaded"]
        maskq = sb("maskq", [P, P], BF16)
        x = sb("x", [P, TT, D])
        stats = sb("stats", [P, TT, 6])
        mv = sb("mv", [P, TT, 2])
        veps = sb("veps", [P, TT])
        power = sb("power", [P, TT])
        rstd = sb("rstd", [P, TT])
        xn = sb("xn", [P, TT, D])
        xT = sb("xT", [P, DC, T])
        ckvT = sb("ckvT", [P, T])
        q2 = sb("q2", [P, DC, 2, T], F16)
        k_hi = sb("k_hi", [P, DC, T], F16)
        k_lo = sb("k_lo", [P, DC, T], F16)
        turned = sb("turned", [R, 2, T])
        rot = sb("rot", [R, 2, T])
        rot_q = sb("rot_q", [2 * R, T], F16)
        rot_k_hi = sb("rot_k_hi", [2 * R, T], F16)
        rot_k_lo = sb("rot_k_lo", [2 * R, T], F16)
        v = sb("v", [P, TT, NH, 2 * HD])
        qs = sb("qs", [KC + 1, NH, T], F16)
        ks_hi = sb("ks_hi", [KC + 1, NH, T], F16)
        ks_lo = sb("ks_lo", [KC, NH, T], F16)
        nmax = sb("nmax", [P, 2, GH, TT])
        ones_row = sb("ones_row", [1, T], F16)
        nmaxT = sb("nmaxT", [GH * TT, P], F16)
        K_OFF = [0, T, T + 3 * P + P, T + 3 * P]
        K_N = [T - P * j for j in range(TT)]
        probs = sb("probs", [P, 2, GH, sum(K_N)])
        o_T = sb("o_T", [P, T // 32, 32])
        inv_sum = sb("inv_sum", [P, T // 32])
        on_T = sb("on_T", [P, T // 32, 32])
        o_n = sb("o_n", [P, NG // 2, T])
        res = sb("res", [P, TT, D])

        SC = psum[0:3]
        MX = psum[3:5]
        O = psum[5]
        PJ = psum[6:8]

        row_of_ones = sem("row_of_ones")
        zeroed = sem("zeroed")
        ones_set = sem("ones_set")
        x_loaded = sem("x_loaded")
        res_loaded = sem("res_loaded")
        ln_stats = sem("ln_stats")
        ln_aggr = sem("ln_aggr")
        var_eps = sem("var_eps")
        ln_rstd = sem("ln_rstd")
        xn_ready = sem("xn_ready")
        pj_ready = [sem("pj_ready0"), sem("pj_ready1")]
        pj_free = [sem("pj_free0"), sem("pj_free1")]
        hi_ready = sem("hi_ready")
        rot_ready = sem("rot_ready")
        rot_parted = sem("rot_parted")
        rot_hi_ready = sem("rot_hi_ready")
        hi_written = sem("hi_written")
        lo_written = sem("lo_written")
        stack_loaded = [sem(f"stack_loaded{g}") for g in range(NG)]
        rope_loaded = [sem(f"rope_loaded{g}") for g in range(NG)]
        mx_ready = sem("mx_ready")
        mx_free = sem("mx_free")
        nmax_written = sem("nmax_written")
        score_loaded = [sem(f"score_loaded{g}") for g in range(NG)]
        sc_ready = sem("sc_ready")
        probs_ready = sem("probs_ready")
        probs_masked = sem("probs_masked")
        o_ready = sem("o_ready")
        o_free = sem("o_free")
        norm_step = sem("norm_step")
        on_ready = sem("on_ready")
        y_stored = sem("y_stored")

        U_XT, U_CKV, U_QR, U_KR, U_Q, U_K, U_V = (0, 1), 2, 3, 5, (4, 6), (7, 8), (9, 10)
        N_SC = 3 * NH
        N_MX = 12 * NG
        N_O = NG + 2
        N_PJ = (6, 5)
        N_ROT = 3
        N_HI = 3
        N_LO = 2
        N_STACK = 2
        N_SCORE = 2
        N_ROPE = 3
        STEP_UNITS = {0: (0, 1), 1: (2,), 2: (3, 4), 3: (5, 6), 4: (7, 8)}
        LN_STEPS = (2, 4)
        OUTPUT_STEPS = (6, 7)

        def pj(b, u):
            return u % 2, N_PJ[u % 2] * b + u // 2

        def o_weighed(b, g):
            if g == 0 and not (isinstance(b, int) and b == 0):
                return N_O * b - 2
            return N_O * b + g

        def o_output(b, half, last):
            return N_O * (b + 1) + half - (2 if last else 1)

        def wait_out(eng, b, u):
            bank, before = pj(b, u)
            eng.wait_ge(pj_free[bank], before + 1)

        with nc.Block() as block:
            @block.sync
            def _(sp):
                sp.dma_start(x[:], xv[0]).then_inc(x_loaded, 16)
                sp.wait_ge(ones_set, 1)
                sp.dma_start(ks_hi[ROW_MAX:ROW_MAX + 1, :, :],
                             ones_row[:].unsqueeze(1).broadcast_to([1, NH, T])).then_inc(row_of_ones, 16)

                def load_x(b):
                    sp.wait_ge(xn_ready, 2 * b)
                    sp.nop(nofuse=True)
                    sp.dma_start(x[:], xv[b]).then_inc(x_loaded, 16)

                def write_scratch(b):
                    for u in U_Q:
                        wait_out(sp, b, u)
                        sp.nop(nofuse=True)
                    sp.dma_start(scratch["q"][b].rearrange("(c p) s n -> p c (s n)", p=P),
                                 q2[:].rearrange("p c s n -> p c (s n)")).then_inc(hi_written, 16)
                    for u in U_K:
                        wait_out(sp, b, u)
                        sp.nop(nofuse=True)
                    for key, part, written in (("k_hi", k_hi, hi_written), ("k_lo", k_lo, lo_written)):
                        for s in range(2):
                            sp.dma_start(scratch[key][b].rearrange("(c p) s n -> p c s n", p=P)[:, :, s, :],
                                         part[:]).then_inc(written, 16)

                def load_stack(b, g, first):
                    if g == 0:
                        sp.wait_ge(hi_written, 16 * N_HI * (b + 1))
                        sp.nop(nofuse=True)
                    if not first:
                        sp.wait_ge(sc_ready, N_SC * (b - 1) + 3 * GH * (g + 1))
                        sp.nop(nofuse=True)
                    slots = slice(g * GH, (g + 1) * GH)
                    for dst, key, loaded in ((qs, "q", stack_loaded), (ks_hi, "k_hi", stack_loaded), (ks_lo, "k_lo", score_loaded)):
                        if key == "k_lo" and g == 0:
                            sp.wait_ge(lo_written, 16 * N_LO * (b + 1))
                            sp.nop(nofuse=True)
                        src = scratch[key][b].rearrange("(h r) s n -> (r s) h n", r=HD)
                        sp.dma_start(dst[0:HR, slots, :], src[:, slots, :]).then_inc(loaded[g], 16)

                def load_max(b, g):
                    sp.wait_ge(mx_free, N_MX * b + 12 * (g + 1))
                    sp.nop(nofuse=True)
                    row = scratch["nmax"][b, g]
                    sp.dma_start(row.rearrange("(s q) -> s q", q=P), nmaxT[:]).then_inc(nmax_written, 16)
                    sp.wait_ge(nmax_written, 16 * (NG * b + g + 1))
                    sp.nop(nofuse=True)
                    sp.dma_start(qs[ROW_MAX:ROW_MAX + 1, g * GH:(g + 1) * GH, :],
                                 row.rearrange("(o h t) -> o h t", o=1, t=T)).then_inc(score_loaded[g], 16)

                def store(b, last=False):
                    sp.wait_ge(o_free, o_output(b, 1, last) + 1)
                    sp.nop(nofuse=True)
                    sp.dma_start(ov[b], res[:]).then_inc(y_stored, 16)

                def body(b, first, rest):
                    load_stack(b, 3, first)
                    load_max(b, 1)
                    if rest >= 2:
                        load_x(b + 2)
                    load_max(b, 2)
                    if rest:
                        write_scratch(b + 1)
                        load_stack(b + 1, 0, False)
                    load_max(b, 3)
                    if not first:
                        store(b - 1)
                    if rest:
                        load_stack(b + 1, 1, False)
                    if not first:
                        sp.wait_ge(y_stored, 16 * b)
                        sp.nop(nofuse=True)
                    sp.dma_start(res[:], xv[b]).then_inc(res_loaded, 16)
                    if rest:
                        load_max(b + 1, 0)
                        load_stack(b + 1, 2, False)

                load_x(1)
                write_scratch(0)
                for g in range(3):
                    load_stack(0, g, True)
                load_max(0, 0)
                body(0, True, 2)
                with sp.Fori(1, NB - 2) as b:
                    body(b, False, 2)
                body(NB - 2, False, 1)
                body(NB - 1, False, 0)
                store(NB - 1, True)
                sp.wait_ge(y_stored, 16 * NB)
                sp.nop(nofuse=True)

            @block.gpsimd
            def _(pool):
                nc.gpsimd.memset(power[:], -0.5).then_inc(var_eps, 1)
                nc.gpsimd.memset(maskq[:], 0.0).then_inc(zeroed, 1)
                pool.wait_ge(zeroed, 1)
                nc.gpsimd.affine_select(out=maskq[:], in_=maskq[:], compare_op=ALU.is_ge, fill=MASKED,
                                        base=0, pattern=[[-1, P]], channel_multiplier=1).then_inc(zeroed, 1)

                def ln(b):
                    pool.wait_ge(ln_aggr, b + 1)
                    pool.nop(nofuse=True)
                    nc.gpsimd.tensor_scalar(veps[:], mv[:, :, 1], EPS, None, ALU.add).then_inc(var_eps, 1)
                    pool.wait_ge(var_eps, b + 2)
                    nc.gpsimd.tensor_tensor(rstd[:], veps[:], power[:], ALU.pow).then_inc(ln_rstd, 1)

                def part_rotary(b, s):
                    if s == 0:
                        pool.wait_ge(rot_hi_ready, 3 * b + 1)
                        pool.nop(nofuse=True)
                        nc.gpsimd.tensor_tensor(rot_q[R:2 * R, :], rot[:, 0, :], rot_q[0:R, :], ALU.subtract).then_inc(rot_parted, 1)
                        pool.wait_ge(rot_parted, N_ROT * b + 1)
                        return
                    pool.wait_ge(rot_hi_ready, 3 * b + 3)
                    pool.nop(nofuse=True)
                    for half in range(2):
                        nc.gpsimd.tensor_tensor(rot_k_lo[half * R:(half + 1) * R, :], rot[:, 1, :], rot_k_hi[0:R, :],
                                                ALU.subtract).then_inc(rot_parted, 1)
                    pool.wait_ge(rot_parted, N_ROT * (b + 1))
                    pool.nop(nofuse=True)

                def mask(b, h):
                    pool.wait_ge(probs_ready, N_SC * b + 3 * (h + 1))
                    pool.nop(nofuse=True)
                    head = probs[:, (h // GH) % 2, h % GH, :]
                    for tiles in (head[:, 0:2 * T].rearrange("p (k n) -> p k n", k=2)[:, :, 0:P],
                                  head[:, K_OFF[3]:K_OFF[2] + P].rearrange("p (k n) -> p k n", k=2)):
                        nc.gpsimd.affine_select(out=tiles, in_=tiles, compare_op=ALU.is_ge, fill=0.0, base=0,
                                                pattern=[[0, 2], [1, P]], channel_multiplier=-1).then_inc(probs_masked, 1)

                def load_rope(b, g, first):
                    if not first:
                        pool.wait_ge(sc_ready, N_SC * (b - 1) + 3 * GH * (g + 1))
                        pool.nop(nofuse=True)
                    for dst, r in ((qs, rot_q), (ks_hi, rot_k_hi), (ks_lo, rot_k_lo)):
                        pool.dma_start(dst[HR:KC, g * GH:(g + 1) * GH, :],
                                       r[:].unsqueeze(1).broadcast_to([2 * R, GH, T])).then_inc(rope_loaded[g], 16)

                def body(b, first, rest):
                    for s in range(NH):
                        if rest >= 2 and s == LN_STEPS[0] + 1:
                            ln(b + 2)
                        mask(b, s)
                        if s == 0:
                            load_rope(b, 3, first)
                        if rest and s in (3, 4):
                            pool.wait_ge(probs_masked, 2 * (NH * b + s + 1))
                            part_rotary(b + 1, s - 3)
                        if rest and s in (4, 8, 12):
                            load_rope(b + 1, s // GH - 1, False)

                ln(0)
                for s in range(2):
                    part_rotary(0, s)
                load_rope(0, 0, True)
                ln(1)
                for g in range(1, 3):
                    load_rope(0, g, True)
                body(0, True, 2)
                with pool.Fori(1, NB - 2) as b:
                    body(b, False, 2)
                body(NB - 2, False, 1)
                body(NB - 1, False, 0)

            @block.vector
            def _(dve):
                def ln_statistics(b, half):
                    dve.wait_ge(x_loaded, 16 * (b + 1))
                    for t in range(2 * half, 2 * half + 2):
                        last = nc.vector.bn_stats(stats[:, t, :], x[:, t, :])
                    last.then_inc(ln_stats, 1)

                def ln_combine(b):
                    dve.wait_ge(ln_stats, 2 * (b + 1))
                    dve.nop(nofuse=True)
                    for t in range(TT):
                        last = nc.vector.bn_aggr(mv[:, t, :], stats[:, t, :])
                    last.then_inc(ln_aggr, 1)

                def ln_apply(b, half, first):
                    dve.wait_ge(ln_rstd, b + 1)
                    if not first:
                        dve.wait_ge(pj_ready[1], pj(b - 1, U_XT[1])[1] + 1)
                    for t in range(2 * half, 2 * half + 2):
                        last = nc.vector.tensor_scalar(xn[:, t, :], x[:, t, :], mv[:, t, 0:1], rstd[:, t:t + 1],
                                                       ALU.subtract, ALU.mult)
                    last.then_inc(xn_ready, 1)

                def rotate(b, s, first):
                    bank, before = pj(b, (U_QR, U_KR)[s])
                    dve.wait_ge(pj_ready[bank], before + 1)
                    if not first:
                        dve.wait_ge(rot_parted, N_ROT * b)
                    if not (first and s == 0):
                        dve.wait_ge(rot_ready, 2 * b + s)
                    nc.vector.tensor_tensor(turned[:, 0, :], PJ[bank][0:R, :], rope[0:R, :], ALU.mult)
                    nc.vector.tensor_tensor(turned[:, 1, :], PJ[bank][R:2 * R, :], rope[R:2 * R, :],
                                            ALU.mult).then_inc(pj_free[bank], 1)
                    dve.wait_ge(pj_free[bank], before + 1)
                    nc.vector.tensor_tensor(rot[:, s, :], turned[:, 0, :], turned[:, 1, :], ALU.add).then_inc(rot_ready, 1)

                def second_part(b, u, first):
                    bank, before = pj(b, u)
                    n = (U_Q + U_K).index(u)
                    dve.wait_ge(hi_ready, 4 * b + n + 1)
                    if not first and n in (0, 2):
                        dve.wait_ge(*((hi_written, 16 * N_HI * b), (lo_written, 16 * N_LO * b))[n // 2])
                    if n < 2:
                        hi, lo = q2[:, n, 0, :], q2[:, n, 1, :]
                    else:
                        hi, lo = k_hi[:, n - 2, :], k_lo[:, n - 2, :]
                    nc.vector.tensor_tensor(lo, PJ[bank][:], hi, ALU.subtract).then_inc(pj_free[bank], 1)

                def maximum(b, g, j, first):
                    use = N_MX * b + 12 * g + j
                    bank = MX[j % 2]
                    dve.wait_ge(mx_ready, use + 1)
                    to = nmax[:, g % 2]
                    if j == -1:
                        if not (first and g <= 1):
                            dve.wait_ge(nmax_written, 16 * (NG * b + g - 1))
                        ins = nc.vector.tensor_copy(nmaxT[:], bank[0:GH * TT, 0:P])
                    elif j == 0:
                        ins = nc.vector.tensor_reduce(to[:, :, 0], bank[:].rearrange("p (h k) -> p h k", h=GH),
                                                      AX_X, ALU.max, negate=True)
                    elif j < 3:
                        h = 2 * (j - 1)
                        ins = nc.vector.tensor_reduce(to[:, h:h + 2, 1], bank[:].rearrange("p (h k) -> p h k", h=2),
                                                      AX_X, ALU.max, negate=True)
                    elif j < 7:
                        ins = nc.vector.tensor_reduce(to[:, j - 3, 2:3], bank[:, 0:3 * P], AX_X, ALU.max, negate=True)
                    else:
                        ins = nc.vector.tensor_reduce(to[:, j - 7, 3:4], bank[:], AX_X, ALU.max, negate=True)
                    ins.then_inc(mx_free, 1)

                def untangle(b, g, first=False):
                    count = o_weighed(b, g)
                    if not (first and g == 0):
                        dve.wait_ge(norm_step, 2 * (NG * b + g))
                    dve.wait_ge(o_ready, count + 1)
                    dve.nop(nofuse=True)
                    nc.vector.transpose(o_T[:].rearrange("p j r -> p (j r)"), O[:]).then_inc(o_free, 1)

                def normalise(b, g, first=False):
                    step = 2 * (NG * b + g)
                    half = g % 2
                    dve.wait_ge(o_free, o_weighed(b, g) + 1)
                    nc.vector.reciprocal(inv_sum[:], o_T[:, :, HD]).then_inc(norm_step, 1)
                    dve.wait_ge(norm_step, step + 1)
                    if not half and not (first and g == 0):
                        dve.wait_ge(on_ready, 2 * b + g // 2)
                    nc.vector.tensor_tensor(on_T[:, :, half * HD:(half + 1) * HD], o_T[:, :, 0:HD],
                                            inv_sum[:].unsqueeze(2).broadcast_to([P, T // 32, HD]),
                                            ALU.mult).then_inc(norm_step, 1)

                def turn_back(b, g):
                    dve.wait_ge(norm_step, 2 * (NG * b + g) + 2)
                    dve.nop(nofuse=True)
                    nc.vector.transpose(o_n[:, g // 2, :], on_T[:].rearrange("p j r -> p (j r)")).then_inc(on_ready, 1)

                def output(b, half, last=False):
                    dve.wait_ge(res_loaded, 16 * (b + 1))
                    dve.wait_ge(o_ready, o_output(b, half, last) + 1)
                    nc.vector.tensor_tensor(res[:, 2 * half:2 * half + 2, :],
                                            O[:].rearrange("p (t d) -> p t d", t=2),
                                            res[:, 2 * half:2 * half + 2, :], ALU.add).then_inc(o_free, 1)

                def body(b, first, rest):
                    def others(s):
                        g, hq = s // GH, s % GH
                        todo = []
                        if s - 1 in OUTPUT_STEPS and not first:
                            todo = [lambda: output(b - 1, OUTPUT_STEPS.index(s - 1))]
                        if hq in (1, 2) and not (first and g == 0):
                            at, start = ((b, g - 1), first) if g else ((b - 1, NG - 1), False)
                            if hq == 1:
                                todo += [lambda: untangle(*at, start), lambda: normalise(*at, start)]
                            elif at[1] % 2:
                                todo += [lambda: turn_back(*at)]
                        if rest:
                            for u in STEP_UNITS.get(s - 1, ()):
                                if u in (U_QR, U_KR):
                                    todo.append(lambda u=u: rotate(b + 1, (U_QR, U_KR).index(u), False))
                        if rest >= 2 and s == LN_STEPS[0]:
                            todo += [lambda: ln_statistics(b + 2, 0), lambda: ln_statistics(b + 2, 1), lambda: ln_combine(b + 2)]
                        if rest >= 2 and s == LN_STEPS[1]:
                            todo += [lambda: ln_apply(b + 2, 0, False), lambda: ln_apply(b + 2, 1, False)]
                        return todo

                    for s in range(NH):
                        g, hq = s // GH, s % GH
                        todo = others(s)
                        mb, mg = (b, g + 2) if g < 2 else (b + 1, g - 2)
                        for unit in range(3 * hq - 1, 3 * hq + 2):
                            if g < 2 or rest or s == 2 * GH and unit == -1:
                                maximum(mb, mg, unit, False)
                            if todo:
                                todo.pop(0)()
                        for work in todo:
                            work()
                        if rest:
                            for u in STEP_UNITS.get(s, ()):
                                if u in U_Q + U_K:
                                    second_part(b + 1, u, False)

                nc.vector.memset(ones_row[:], 1.0)
                nc.vector.memset(v[:, :, :, HD:2 * HD], 1.0).then_inc(ones_set, 1)
                for half in range(2):
                    ln_statistics(0, half)
                ln_combine(0)
                for half in range(2):
                    ln_apply(0, half, True)
                dve.wait_ge(w_loaded, 16 * N_W_LOADS)
                for u in range(3, 9):
                    if u in (U_QR, U_KR):
                        rotate(0, (U_QR, U_KR).index(u), True)
                    else:
                        second_part(0, u, True)
                for half in range(2):
                    ln_statistics(1, half)
                ln_combine(1)
                for half in range(2):
                    ln_apply(1, half, False)
                for g in range(2):
                    for j in range(-1, 11):
                        if g or j >= 0:
                            maximum(0, g, j, True)
                body(0, True, 2)
                with dve.Fori(1, NB - 2) as b:
                    body(b, False, 2)
                body(NB - 2, False, 1)
                body(NB - 1, False, 0)
                untangle(NB - 1, NG - 1)
                normalise(NB - 1, NG - 1)
                turn_back(NB - 1, NG - 1)
                for half in range(2):
                    output(NB - 1, half, True)

            @block.scalar
            def _(act):
                act.preload_act_table(ACT.Exp)

                def copy_out(b, u, first):
                    bank, before = pj(b, u)
                    act.wait_ge(pj_ready[bank], before + 1)
                    src, done = PJ[bank], (pj_free[bank], 1)
                    if u in U_XT:
                        if u == U_XT[0] and not first:
                            act.wait_ge(pj_ready[0], pj(b - 1, U_Q[1])[1] + 1)
                            act.wait_ge(pj_ready[1], pj(b - 1, U_QR)[1] + 1)
                        dst = xT[:, u, :]
                    elif u == U_CKV:
                        if not first:
                            act.wait_ge(pj_ready[1], pj(b - 1, U_V[0])[1] + 1)
                        dst = ckvT[:]
                    elif u in U_Q + U_K:
                        if u == U_Q[0] and not first:
                            act.wait_ge(hi_written, 16 * N_HI * b)
                        dst = q2[:, U_Q.index(u), 0, :] if u in U_Q else k_hi[:, U_K.index(u), :]
                        done = (hi_ready, 1)
                    else:
                        if u == U_V[0] and not first:
                            act.wait_ge(o_ready, o_weighed(b - 1, NG - 1) + 1)
                        t = 2 * (u - U_V[0])
                        dst = v[:, t:t + 2, :, 0:HD]
                        src = src.rearrange("p (t h d) -> p t h d", t=2, h=NH)
                    nc.scalar.activation(dst, src if u in U_V else src[:], ACT.Copy).then_inc(*done)

                def first_rotary_parts(b, s, first):
                    if s == 0 and not first:
                        for g in range(NG):
                            act.wait_ge(rope_loaded[g], 16 * N_ROPE * b)
                    act.wait_ge(rot_ready, 2 * b + s + 1)
                    for dst in ((rot_q[0:R, :],), (rot_k_hi[0:R, :], rot_k_hi[R:2 * R, :]))[s]:
                        nc.scalar.activation(dst, rot[:, s, :], ACT.Copy).then_inc(rot_hi_ready, 1)

                def exps(b, g, hq, first):
                    if hq == 0 and not (first and g < 2):
                        act.wait_ge(o_ready, (o_weighed(b, g - 2) if g >= 2 else o_weighed(b - 1, g + 2)) + 1)
                    h = GH * g + hq
                    for j in range(3):
                        act.wait_ge(sc_ready, N_SC * b + 3 * h + j + 1)
                        n = K_N[2] if j == 2 else T
                        at = j * T
                        nc.scalar.activation(probs[:, g % 2, hq, at:at + n], SC[j][:, 0:n], ACT.Exp,
                                             scale=SCALE).then_inc(probs_ready, 1)

                def body(b, first, rest):
                    for s in range(NH):
                        exps(b, s // GH, s % GH, first)
                        if s == 0:
                            for u in U_V:
                                copy_out(b, u, first)
                        if rest:
                            for u in STEP_UNITS.get(s, ()):
                                if u not in (U_QR, U_KR):
                                    copy_out(b + 1, u, False)
                            for u in STEP_UNITS.get(s - 1, ()):
                                if u in (U_QR, U_KR):
                                    first_rotary_parts(b + 1, (U_QR, U_KR).index(u), False)

                for u in range(9):
                    if u in (U_QR, U_KR):
                        first_rotary_parts(0, (U_QR, U_KR).index(u), True)
                    else:
                        copy_out(0, u, True)
                body(0, True, 2)
                with act.Fori(1, NB - 2) as b:
                    body(b, False, 2)
                body(NB - 2, False, 1)
                body(NB - 1, False, 0)

            @block.tensor
            def _(pe):
                pe.wait_ge(w_loaded, 16 * N_W_LOADS)
                pe.wait_ge(zeroed, 2)
                ident, identb = const["ident"], const["identb"]

                def project(b, u, first):
                    bank, before = pj(b, u)
                    if not (first and u < 2):
                        pe.wait_ge(pj_free[bank], before)
                    out = PJ[bank]
                    if u in U_XT:
                        if u == U_XT[0]:
                            pe.wait_ge(xn_ready, 2 * (b + 1))
                        for t in range(TT):
                            last = nc.tensor.transpose(out[:, t * P:(t + 1) * P], xn[:, t, u * P:(u + 1) * P], ident[:])
                    elif u in (U_CKV, U_QR, *U_Q):
                        if u == U_CKV:
                            for before_u in U_XT:
                                wait_out(pe, b, before_u)
                        for c in range(DC):
                            lhsT = {U_CKV: w_down[:, c, :], U_Q[0]: w_q[:, c, 0:P], U_Q[1]: w_q[:, c, P:2 * P],
                                    U_QR: w_qr[:, c, :]}[u]
                            last = nc.tensor.matmul(out[0:lhsT.shape[-1], :], lhsT, xT[:, c, :], start=c == 0, stop=c == DC - 1)
                    elif u in (U_KR, *U_K):
                        if u == U_KR:
                            wait_out(pe, b, U_CKV)
                        lhsT = {U_K[0]: w_ku[:, 0:P], U_K[1]: w_ku[:, P:2 * P], U_KR: w_kr[:]}[u]
                        last = nc.tensor.matmul(out[0:lhsT.shape[-1], :], lhsT, ckvT[:], start=True, stop=True)
                    else:
                        for k in range(2):
                            t = 2 * (u - U_V[0]) + k
                            last = nc.tensor.matmul(out[:, k * D:(k + 1) * D], ckvT[:, t * P:(t + 1) * P], w_vu[:],
                                                    start=True, stop=True)
                    last.then_inc(pj_ready[bank], 1)

                def stacked(b, g):
                    pe.wait_ge(stack_loaded[g], 16 * N_STACK * (b + 1))
                    pe.wait_ge(rope_loaded[g], 16 * N_ROPE * (b + 1))

                def maximum(b, g, j, first):
                    use = N_MX * b + 12 * g + j
                    out = MX[j % 2]
                    if not (first and g == 0 and j < 2):
                        pe.wait_ge(mx_free, use if j == -1 else use - 1)
                    if j == -1:
                        last = nc.tensor.transpose(out[0:GH * TT, 0:P],
                                                   nmax[:, (g - 1) % 2].rearrange("p h i -> p (h i)"), ident[:])
                    else:
                        if j == 0:
                            i, heads = 0, range(GH)
                        elif j < 3:
                            i, heads = 1, range(2 * (j - 1), 2 * j)
                        elif j < 7:
                            i, heads = 2, (j - 3,)
                        else:
                            i, heads = 3, (j - 7,)
                        n = P * (i + 1)
                        for k, hq in enumerate(heads):
                            slot = GH * g + hq
                            nc.tensor.matmul(out[:, k * n:(k + 1) * n], qs[0:KC, slot, i * P:(i + 1) * P],
                                             ks_hi[0:KC, slot, 0:n], start=True, stop=False)
                            last = nc.tensor.matmul(out[:, (k + 1) * n - P:(k + 1) * n], identb[:], maskq[:],
                                                    start=False, stop=True)
                    last.then_inc(mx_ready, 1)

                def score(b, slot, j, first):
                    if not (first and slot == 0):
                        pe.wait_ge(probs_ready, N_SC * b + 3 * slot + j - 2)
                    for kt in ((0,), (1, 3), (2,))[j]:
                        at = K_OFF[kt] - j * T
                        n = K_N[kt]
                        keys = slice(kt * P, (kt + 1) * P)
                        nc.tensor.matmul(SC[j][:, at:at + n], ks_hi[:, slot, keys], qs[:, slot, kt * P:T],
                                         start=True, stop=False)
                        last = nc.tensor.matmul(SC[j][:, at:at + n], ks_lo[:, slot, keys], qs[0:KC, slot, kt * P:T],
                                                start=False, stop=True)
                    last.then_inc(sc_ready, 1)

                def weigh(b, g, first):
                    if not (first and g == 0):
                        pe.wait_ge(o_free, o_weighed(b, g))
                    pe.wait_ge(probs_masked, 2 * (NH * b + GH * (g + 1)))
                    if g == 0:
                        for u in U_V:
                            wait_out(pe, b, u)
                    for kt in range(TT):
                        for hq in range(GH):
                            last = nc.tensor.matmul(O[32 * hq:32 * hq + 32, kt * P:T], v[:, kt, GH * g + hq, :],
                                                    probs[:, g % 2, hq, K_OFF[kt]:K_OFF[kt] + K_N[kt]],
                                                    start=kt == 0, stop=kt == TT - 1)
                    last.then_inc(o_ready, 1)

                def output(b, half, last=False):
                    pe.wait_ge(on_ready, 2 * (b + 1))
                    pe.wait_ge(o_free, o_output(b, half, last))
                    for k in range(2):
                        t = 2 * half + k
                        for c in range(NG // 2):
                            last = nc.tensor.matmul(O[:, k * D:(k + 1) * D], o_n[:, c, t * P:(t + 1) * P], w_o[:, c, :],
                                                    start=c == 0, stop=c == NG // 2 - 1)
                    last.then_inc(o_ready, 1)

                def body(b, first, rest):
                    for s in range(NH):
                        g, hq = s // GH, s % GH
                        if hq == 0:
                            stacked(b, g)
                            pe.wait_ge(score_loaded[g], 16 * N_SCORE * (b + 1))
                        for j in range(3):
                            score(b, s, j, first)
                            unit = 3 * hq + j - 1
                            mb, mg = (b, g + 2) if g < 2 else (b + 1, g - 2)
                            if g < 2 or rest or s == 2 * GH and unit == -1:
                                if unit == 0:
                                    stacked(mb, mg)
                                maximum(mb, mg, unit, False)
                        if hq == 0 and not (first and g == 0):
                            weigh(b, g - 1, first) if g else weigh(b - 1, NG - 1, False)
                        if s == 0:
                            for u in U_V:
                                project(b, u, False)
                        if s in OUTPUT_STEPS and not first:
                            output(b - 1, OUTPUT_STEPS.index(s))
                        if rest:
                            for u in STEP_UNITS.get(s, ()):
                                project(b + 1, u, False)

                for u in range(9):
                    project(0, u, True)
                for g in range(2):
                    stacked(0, g)
                    for j in range(-1, 11):
                        if g or j >= 0:
                            maximum(0, g, j, True)
                pe.wait_ge(row_of_ones, 16)
                pe.wait_ge(ones_set, 1)
                body(0, True, 2)
                with pe.Fori(1, NB - 2) as b:
                    body(b, False, 2)
                body(NB - 2, False, 1)
                body(NB - 1, False, 0)
                weigh(NB - 1, NG - 1, False)
                for half in range(2):
                    output(NB - 1, half, True)


def build(nc, a, rope_table, out):
    N = a["x"].shape[0]
    x1 = nc.dram_tensor("x1", [N, D], F32, kind="Internal").ap()
    x2 = nc.dram_tensor("x2", [N, D], F32, kind="Internal").ap()
    routed = nc.dram_tensor("routed", [E * (N + P) + P, ROW], F32, kind="Internal").ap()
    scratch = {k: nc.dram_tensor(f"scratch_{k}", [N // T, D, 2, T], F16, kind="Internal").ap()
               for k in ("q", "k_hi", "k_lo")}
    scratch["nmax"] = nc.dram_tensor("scratch_nmax", [N // T, NG, GH * T], F16, kind="Internal").ap()
    with ExitStack() as ctx:
        psum = [ctx.enter_context(nc.psum_tensor(f"bank{i}", [P, 512], F32)) for i in range(8)]
        ident = ctx.enter_context(nc.sbuf_tensor("ident", [P, P], F32))
        identb = ctx.enter_context(nc.sbuf_tensor("identb", [P, P], BF16))
        made = ctx.enter_context(nc.semaphore("ident_made"))
        with nc.Block() as block:
            @block.gpsimd
            def _(pool):
                nc.gpsimd.memset(ident[:], 0.0)
                nc.gpsimd.memset(identb[:], 0.0).then_inc(made, 1)
                pool.wait_ge(made, 1)
                for m in (ident, identb):
                    nc.gpsimd.affine_select(out=m[:], in_=m[:], compare_op=ALU.not_equal, fill=1.0,
                                            base=0, pattern=[[-1, P]], channel_multiplier=1)
        const = {"ident": ident, "identb": identb}
        ffn, attention = ffn_weights(nc, ctx), attention_weights(nc, ctx)
        ffn_phase(nc, "f1", psum, const, a["x"], x1, routed, ffn, weights=a,
                  load_next=lambda sp: load_attention_weights(sp, attention, a, rope_table))
        attention_phase(nc, psum, const, x1, x2, attention, scratch)
        ffn_phase(nc, "f2", psum, const, x2, out, routed, ffn)


def rope_constants(np):
    inv = (np.float32(1.0) / np.power(np.float32(10000.0), np.arange(0, R, 2, dtype=np.float32) / np.float32(R))).astype(np.float32)
    angle = np.outer(inv, np.arange(T, dtype=np.float32)).astype(np.float32)
    cos, sin = np.cos(angle), np.sin(angle)
    return np.concatenate([cos, cos, -sin, sin])


def kernel(**inputs):
    import numpy as np
    import concourse.bacc as bacc
    from concourse.bass_utils import run_bass_kernel_spmd

    nc = bacc.Bacc("TRN2", target_bir_lowering=False, num_devices=1)
    x = np.ascontiguousarray(inputs["L0_attn_x"])
    shape = x.shape
    arrays = {"x": x.reshape(-1, shape[-1])}
    for name in inputs:
        if name != "L0_attn_x":
            short = name.replace("L0_attn_W_", "").replace("L0_ffn_", "")
            arrays[short] = np.ascontiguousarray(inputs[name])
    arrays["rope_table"] = rope_constants(np)
    aps = {n: nc.dram_tensor(f"in_{n}", v.shape, mybir.dt.from_np(v.dtype), kind="ExternalInput").ap()
           for n, v in arrays.items()}
    out = nc.dram_tensor("out", arrays["x"].shape, F32, kind="ExternalOutput").ap()
    build(nc, aps, aps["rope_table"], out)
    r = run_bass_kernel_spmd(nc, [{f"in_{n}": v for n, v in arrays.items()}], core_ids=[0])
    return r.results[0]["out"].reshape(shape)
```
